# Optimizing a Trainium2 kernel written in Bass

```python
import numpy as np
import jax
import jax.numpy as jnp

def _softmax(x, axis=-1):
    return jax.nn.softmax(x, axis=axis)

def _gelu(x):
    return jax.nn.gelu(x, approximate=True)

def _silu(x):
    return jax.nn.silu(x)

def _sigmoid(x):
    return jax.nn.sigmoid(x)

def _layernorm(x, axis=-1, eps=1e-05):
    m = jnp.mean(x, axis=axis, keepdims=True)
    v = jnp.var(x, axis=axis, keepdims=True)
    return (x - m) / jnp.sqrt(v + eps)

def _scatter_add(tgt, idx, src, axis=0):
    return tgt.at[idx].add(src)

def _segment_sum(src, seg, n):
    return jax.ops.segment_sum(src, seg, n)
kernel_name = 'mk_decoder_preln_d4_seqx_r8_a8f9dd'

def setup_inputs(seed: int=0):
    np.random.seed(seed)
    _w = jnp.asarray

    def _rec_inputs():
        import jax
        import jax.numpy as jnp
        _rk = jax.random.key(seed)
        x = 7.22e-05 + 1 * jax.random.normal(jax.random.fold_in(_rk, 1), (64, 64, 128), jnp.float32)
        _lenS = 64 - jax.random.randint(jax.random.fold_in(_rk, 7), (64,), 0, max(1, 64 // 4) + 1, jnp.int32)
        _lenS2 = 64 - jax.random.randint(jax.random.fold_in(_rk, 8), (64,), 0, max(1, 64 // 4) + 1, jnp.int32)
        _ctx_1024P = jax.random.normal(jax.random.fold_in(_rk, 11), (64, 16, 128), jnp.float32)
        _ctx_1024c = jax.random.dirichlet(jax.random.fold_in(_rk, 511), 0.3 * jnp.ones((16,), jnp.float32), (64, 64))
        _ctx_1024t = jnp.einsum('bsk,bkd->bsd', _ctx_1024c, _ctx_1024P)
        _ctx_1024t = _ctx_1024t * jax.lax.rsqrt(jnp.mean(jnp.square(_ctx_1024t)) + 1e-12) * 0.953939
        ctx_1024 = 4.13588e-05 + 0.999923 * (_ctx_1024t + 0.3 * jax.random.normal(jax.random.fold_in(_rk, 611), (64, 64, 128), jnp.float32))
        _validS = jnp.arange(64)[None, :] < _lenS[:, None]
        _validS2 = jnp.arange(64)[None, :] < _lenS2[:, None]
        _causal = jnp.tril(jnp.ones((64, 64), dtype=bool))
        mask_BxSxS2_bk0 = jnp.logical_not(jnp.broadcast_to(_validS2[:, None, :], (64, 64, 64)))
        mask_Bx1x1xS2_ff0 = jnp.where(jnp.ones((64, 1, 1, 64), dtype=bool), 0.0, -1000000000.0).astype(jnp.float32)
        return (x, ctx_1024, mask_BxSxS2_bk0, mask_Bx1x1xS2_ff0)
    x, ctx_1024, mask_BxSxS2_bk0, mask_Bx1x1xS2_ff0 = _rec_inputs()

    def _L0_attn_setup():
        import jax, jax.numpy as jnp
        import numpy as np
        B, T, D = (2, 256, 128)
        H = 16
        DH = D // H

        def alibi_bias(n_heads, token_cnt, dtype=jnp.float32):
            slopes = 2.0 ** (-8.0 * jnp.arange(1, n_heads + 1, dtype=dtype) / n_heads)
            pos = jnp.arange(token_cnt, dtype=dtype)
            rel = pos[None, :] - pos[:, None]
            return slopes[:, None, None] * rel[None, :, :]
        key = jax.random.key(seed)
        ks = jax.random.split(key, 5)
        s = 1.0 / np.sqrt(D)
        return {'x': jax.random.normal(ks[0], (B, T, D), dtype=jnp.float32), 'W_query': jax.random.normal(ks[1], (D, D), dtype=jnp.float32) * s, 'W_key': jax.random.normal(ks[2], (D, D), dtype=jnp.float32) * s, 'W_value': jax.random.normal(ks[3], (D, D), dtype=jnp.float32) * s, 'W_proj': jax.random.normal(ks[4], (D, D), dtype=jnp.float32) * s, 'b_proj': jnp.zeros((D,), dtype=jnp.float32)}
    _L0_attn_all = _L0_attn_setup()
    _L0_attn_in = {k: v for k, v in _L0_attn_all.items() if k in ('W_query', 'W_key', 'W_value', 'W_proj', 'b_proj')}
    del _L0_attn_all

    def _L0_xattn_setup():
        import jax, jax.numpy as jnp
        import numpy as np
        B, S, D_IN, D_H = (4, 256, 128, 128)
        key = jax.random.key(seed)
        k1, k2, k3, k4, k5, k6 = jax.random.split(key, 6)
        seq1 = jax.random.normal(k1, (B, S, D_IN), dtype=jnp.float32)
        seq2 = jax.random.normal(k2, (B, S, D_IN), dtype=jnp.float32)
        attn_mask = jax.random.randint(k3, (B, S, S), 0, 2).astype(jnp.bool_)
        scale = 1.0 / np.sqrt(D_IN)
        Wq = jax.random.uniform(k4, (D_H, D_IN), dtype=jnp.float32, minval=-scale, maxval=scale)
        Wk = jax.random.uniform(k5, (D_H, D_IN), dtype=jnp.float32, minval=-scale, maxval=scale)
        Wv = jax.random.uniform(k6, (D_H, D_IN), dtype=jnp.float32, minval=-scale, maxval=scale)
        return {'seq1': seq1, 'seq2': seq2, 'attn_mask': attn_mask, 'Wq': Wq, 'Wk': Wk, 'Wv': Wv}
    _L0_xattn_all = _L0_xattn_setup()
    _L0_xattn_in = {k: v for k, v in _L0_xattn_all.items() if k in ('Wq', 'Wk', 'Wv')}
    del _L0_xattn_all

    def _L0_ffn_setup():
        import jax, jax.numpy as jnp
        import numpy as np
        B, S, D, F, E = (2, 256, 128, 512, 8)
        LN_EPS = 1e-05

        def _xavier(key, shape, fan_in, fan_out):
            a = np.sqrt(6.0 / (fan_in + fan_out))
            return jax.random.uniform(key, shape, jnp.float32, -a, a)
        key = jax.random.key(seed)
        ks = jax.random.split(key, 8)
        tgt = jax.random.normal(ks[0], (B, S, D), jnp.float32)
        router_w = _xavier(ks[1], (E, D), D, E)
        router_b = jnp.zeros((E,), jnp.float32)
        w1 = _xavier(ks[2], (E, D, F), D, F)
        b1 = jnp.zeros((E, F), jnp.float32)
        w2 = _xavier(ks[3], (E, F, D), F, D)
        b2 = jnp.zeros((E, D), jnp.float32)
        gamma = jnp.ones((D,), jnp.float32)
        beta = jnp.zeros((D,), jnp.float32)
        return {'tgt': tgt, 'router_w': router_w, 'router_b': router_b, 'w1': w1, 'b1': b1, 'w2': w2, 'b2': b2, 'gamma': gamma, 'beta': beta}
    _L0_ffn_all = _L0_ffn_setup()
    _L0_ffn_in = {k: v for k, v in _L0_ffn_all.items() if k in ('router_w', 'router_b', 'w1', 'b1', 'w2', 'b2', 'gamma', 'beta')}
    del _L0_ffn_all

    def _L1_attn_setup():
        import jax, jax.numpy as jnp
        import numpy as np
        EMBED_DIM = 128
        NUM_HEADS = 16
        HEAD_DIM = EMBED_DIM // NUM_HEADS
        FEATURE_EPS = 1e-06
        DEN_EPS = 1e-06
        key = jax.random.key(seed)
        k_x, k_qw, k_qb, k_ow, k_ob = jax.random.split(key, 5)
        b, l = (2, 256)
        x = jax.random.normal(k_x, (b, l, EMBED_DIM), dtype=jnp.float32)
        s = 1.0 / np.sqrt(EMBED_DIM)
        qkv_w = jax.random.uniform(k_qw, (3 * EMBED_DIM, EMBED_DIM), minval=-s, maxval=s, dtype=jnp.float32)
        qkv_b = jax.random.uniform(k_qb, (3 * EMBED_DIM,), minval=-s, maxval=s, dtype=jnp.float32)
        out_w = jax.random.uniform(k_ow, (EMBED_DIM, EMBED_DIM), minval=-s, maxval=s, dtype=jnp.float32)
        out_b = jax.random.uniform(k_ob, (EMBED_DIM,), minval=-s, maxval=s, dtype=jnp.float32)
        return {'x': x, 'qkv_w': qkv_w, 'qkv_b': qkv_b, 'out_w': out_w, 'out_b': out_b}
    _L1_attn_all = _L1_attn_setup()
    _L1_attn_in = {k: v for k, v in _L1_attn_all.items() if k in ('qkv_w', 'qkv_b', 'out_w', 'out_b')}
    del _L1_attn_all

    def _L1_xattn_setup():
        import jax, jax.numpy as jnp
        import numpy as np
        B, S, D, H = (2, 256, 128, 16)
        HEAD_DIM = D // H
        MAX_REL = 64

        def _split_heads(x, b):
            return x.reshape(b, -1, H, HEAD_DIM).transpose(0, 2, 1, 3)
        key = jax.random.key(seed)
        ks = jax.random.split(key, 8)
        std = 0.02
        return {'query': jax.random.normal(ks[0], (B, S, D), jnp.float32), 'key': jax.random.normal(ks[1], (B, S, D), jnp.float32), 'value': jax.random.normal(ks[2], (B, S, D), jnp.float32), 'attention_mask': jnp.zeros((B, 1, 1, S), jnp.float32), 'Wq': jax.random.normal(ks[3], (D, D), jnp.float32) * std, 'bq': jnp.zeros((D,), jnp.float32), 'Wk': jax.random.normal(ks[4], (D, D), jnp.float32) * std, 'bk': jnp.zeros((D,), jnp.float32), 'Wv': jax.random.normal(ks[5], (D, D), jnp.float32) * std, 'bv': jnp.zeros((D,), jnp.float32), 'rel_table': jax.random.normal(ks[6], (2 * MAX_REL + 1, HEAD_DIM), jnp.float32) * std}
    _L1_xattn_all = _L1_xattn_setup()
    _L1_xattn_in = {k: v for k, v in _L1_xattn_all.items() if k in ('Wq', 'bq', 'Wk', 'bk', 'Wv', 'bv', 'rel_table')}
    del _L1_xattn_all

    def _L1_ffn_setup():
        import jax, jax.numpy as jnp
        import numpy as np
        D_MODEL = 128
        N_EXPERTS = 8
        TOP_K = 2
        BOTTLENECK = 64
        B, S = (2, 512)
        ADAPTER_SCALE = 0.5

        def _moe_forward(x, w_gate, w_noise, Wd, bd, Wu, bu):
            b, s, d = x.shape
            xf = x.reshape(-1, d)
            T = xf.shape[0]
            clean_logits = xf @ w_gate
            logits = clean_logits
            k1 = min(TOP_K + 1, N_EXPERTS)
            top_logits, top_idx = jax.lax.top_k(logits, k1)
            top_k_logits = top_logits[:, :TOP_K]
            top_k_idx = top_idx[:, :TOP_K]
            top_k_gates = jax.nn.softmax(top_k_logits, axis=-1)
            rows = jnp.arange(T)[:, None]
            gates = jnp.zeros((T, N_EXPERTS), dtype=top_k_gates.dtype)
            gates = gates.at[rows, top_k_idx].set(top_k_gates)
            h = jax.nn.relu(jnp.einsum('td,edb->teb', xf, Wd) + bd[None, :, :])
            y = jnp.einsum('teb,ebd->ted', h, Wu) + bu[None, :, :]
            y = ADAPTER_SCALE * y
            out = jnp.einsum('te,ted->td', gates, y)
            return out.reshape(b, s, d)
        key = jax.random.key(seed)
        ks = jax.random.split(key, 8)
        sd = 0.02
        x = jax.random.normal(ks[0], (B, S, D_MODEL), dtype=jnp.float32)
        w_gate = jax.random.normal(ks[1], (D_MODEL, N_EXPERTS), dtype=jnp.float32) * sd
        w_noise = jax.random.normal(ks[2], (D_MODEL, N_EXPERTS), dtype=jnp.float32) * sd
        Wd = jax.random.normal(ks[3], (N_EXPERTS, D_MODEL, BOTTLENECK), dtype=jnp.float32) * sd
        bd = jnp.zeros((N_EXPERTS, BOTTLENECK), dtype=jnp.float32)
        Wu = jax.random.normal(ks[4], (N_EXPERTS, BOTTLENECK, D_MODEL), dtype=jnp.float32) * sd
        bu = jnp.zeros((N_EXPERTS, D_MODEL), dtype=jnp.float32)
        return {'x': x, 'w_gate': w_gate, 'w_noise': w_noise, 'Wd': Wd, 'bd': bd, 'Wu': Wu, 'bu': bu}
    _L1_ffn_all = _L1_ffn_setup()
    _L1_ffn_in = {k: v for k, v in _L1_ffn_all.items() if k in ('w_gate', 'w_noise', 'Wd', 'bd', 'Wu', 'bu')}
    del _L1_ffn_all

    def _L2_attn_setup():
        import jax, jax.numpy as jnp
        import numpy as np
        import math
        L, B, D = (256, 4, 128)
        ZDIM, HDIM, NDIM = (128, 256, 16)

        def _laplace(x, mu=0.707107, sigma=0.282095):
            return 0.5 * (1.0 + jax.lax.erf((x - mu) / (sigma * math.sqrt(2.0))))

        def _ema(x, delta, alpha, beta, gamma, omega):
            seq_len = x.shape[0]
            scale = math.sqrt(1.0 / delta.shape[1])
            residual = x * omega
            xe = jnp.transpose(x, (1, 2, 0))
            p = jax.nn.sigmoid(delta)
            q = 1.0 - p * jax.nn.sigmoid(alpha)
            vander = jnp.arange(seq_len, dtype=x.dtype)[None, None, :] * jnp.log(q)
            kern = jnp.einsum('dnl,dn->dl', p * beta * jnp.exp(vander), gamma * scale)
            n = 2 * seq_len
            out = jnp.fft.irfft(jnp.fft.rfft(xe, n=n) * jnp.fft.rfft(kern, n=n), n=n)[..., :seq_len]
            out = jnp.transpose(out, (2, 0, 1)).astype(x.dtype)
            return jax.nn.silu(out + residual)

        def _rotary_bias(seq_len, zdim, alpha, beta):
            half = zdim // 2
            freqs = jnp.exp(jnp.arange(half, dtype=jnp.float32) * (-math.log(10000.0) / half))
            ang = jnp.arange(seq_len, dtype=jnp.float32)[:, None] * freqs[None, :]
            sin, cos = (jnp.sin(ang), jnp.cos(ang))

            def rot(v):
                v = jnp.broadcast_to(v, (seq_len, zdim))
                v1, v2 = (v[:, :half], v[:, half:])
                return jnp.concatenate([v1 * cos - v2 * sin, v2 * cos + v1 * sin], axis=1)
            return rot(alpha) @ rot(beta).T
        key = jax.random.key(seed)
        ks = jax.random.split(key, 12)
        std = 0.02
        val = np.ones((NDIM, 1), np.float32)
        val[1::2] = -1.0
        inp = {'x': jax.random.normal(ks[0], (L, B, D), jnp.float32), 'ema_delta': 0.2 * jax.random.normal(ks[1], (D, NDIM, 1), jnp.float32), 'ema_alpha': 0.2 * jax.random.normal(ks[2], (D, NDIM, 1), jnp.float32), 'ema_beta': 0.02 * jax.random.normal(ks[3], (D, NDIM, 1), jnp.float32) + jnp.asarray(val), 'ema_gamma': jax.random.normal(ks[4], (D, NDIM), jnp.float32), 'ema_omega': jax.random.normal(ks[5], (D,), jnp.float32), 'ln_w': jnp.ones((D,), jnp.float32), 'ln_b': jnp.zeros((D,), jnp.float32), 'Wv': std * jax.random.normal(ks[6], (HDIM, D), jnp.float32), 'bv': jnp.zeros((HDIM,), jnp.float32), 'Wmx': std * jax.random.normal(ks[7], (ZDIM + HDIM + 2 * D, D), jnp.float32), 'bmx': jnp.zeros((ZDIM + HDIM + 2 * D,), jnp.float32), 'Wh': std * jax.random.normal(ks[8], (D, HDIM), jnp.float32), 'bh': jnp.zeros((D,), jnp.float32), 'qk_gamma': std * jax.random.normal(ks[9], (2, ZDIM), jnp.float32), 'qk_beta': jnp.zeros((2, ZDIM), jnp.float32), 'rot_alpha': std * jax.random.normal(ks[10], (1, ZDIM), jnp.float32), 'rot_beta': std * jax.random.normal(ks[11], (1, ZDIM), jnp.float32)}
        return inp
    _L2_attn_all = _L2_attn_setup()
    _L2_attn_in = {k: v for k, v in _L2_attn_all.items() if k in ('ema_delta', 'ema_alpha', 'ema_beta', 'ema_gamma', 'ema_omega', 'ln_w', 'ln_b', 'Wv', 'bv', 'Wmx', 'bmx', 'Wh', 'bh', 'qk_gamma', 'qk_beta', 'rot_alpha', 'rot_beta')}
    del _L2_attn_all

    def _L2_xattn_setup():
        import jax, jax.numpy as jnp
        import numpy as np
        D, H = (128, 16)
        DH = D // H

        def _split_heads(z):
            b, t, _ = z.shape
            return z.reshape(b, t, H, DH).transpose(0, 2, 1, 3)
        key = jax.random.key(seed)
        ks = jax.random.split(key, 11)
        b, t, ta = (2, 256, 1500)
        s = 1.0 / np.sqrt(D)
        return {'x': jax.random.normal(ks[0], (b, t, D), dtype=jnp.float32), 'xa': jax.random.normal(ks[1], (b, ta, D), dtype=jnp.float32), 'Wqkv': jax.random.normal(ks[2], (D, 3 * D), dtype=jnp.float32) * s, 'bqkv': jax.random.normal(ks[3], (3 * D,), dtype=jnp.float32) * 0.01, 'Wqkv_aux': jax.random.normal(ks[4], (D, 3 * D), dtype=jnp.float32) * s, 'bqkv_aux': jax.random.normal(ks[5], (3 * D,), dtype=jnp.float32) * 0.01, 'Wo': jax.random.normal(ks[6], (D, D), dtype=jnp.float32) * s, 'bo': jax.random.normal(ks[7], (D,), dtype=jnp.float32) * 0.01, 'g': jnp.zeros((H,), dtype=jnp.float32)}
    _L2_xattn_all = _L2_xattn_setup()
    _L2_xattn_in = {k: v for k, v in _L2_xattn_all.items() if k in ('Wqkv', 'bqkv', 'Wqkv_aux', 'bqkv_aux', 'Wo', 'bo', 'g')}
    del _L2_xattn_all

    def _L2_ffn_setup():
        import jax, jax.numpy as jnp
        import numpy as np
        DIM = 128
        N_EXPERTS = 8
        D_FF = 256
        TOP_K = 2
        key = jax.random.key(seed)
        ks = jax.random.split(key, 5)
        s = 0.02
        return {'x': jax.random.normal(ks[0], (2, 256, DIM), dtype=jnp.float32), 'gate_w': jax.random.normal(ks[1], (N_EXPERTS, DIM), dtype=jnp.float32) * s, 'w1': jax.random.normal(ks[2], (N_EXPERTS, D_FF, DIM), dtype=jnp.float32) * s, 'w2': jax.random.normal(ks[3], (N_EXPERTS, DIM, D_FF), dtype=jnp.float32) * s, 'w3': jax.random.normal(ks[4], (N_EXPERTS, D_FF, DIM), dtype=jnp.float32) * s}
    _L2_ffn_all = _L2_ffn_setup()
    _L2_ffn_in = {k: v for k, v in _L2_ffn_all.items() if k in ('gate_w', 'w1', 'w2', 'w3')}
    del _L2_ffn_all

    def _L3_attn_setup():
        import jax, jax.numpy as jnp
        import numpy as np
        DIM = 128
        HEADS = 16
        HIDDEN = 512
        EPS_ATTN = 1e-06
        EPS_LN = 1e-05

        def layer_norm(x, g, b):
            mu = jnp.mean(x, axis=-1, keepdims=True)
            var = jnp.var(x, axis=-1, keepdims=True)
            return (x - mu) * jax.lax.rsqrt(var + EPS_LN) * g + b
        key = jax.random.key(seed)
        ks = jax.random.split(key, 8)
        s = 0.02
        return {'x': jax.random.normal(ks[0], (4, 512, DIM), jnp.float32), 'norm1_g': jnp.ones((DIM,), jnp.float32), 'norm1_b': jnp.zeros((DIM,), jnp.float32), 'qkv_w': jax.random.normal(ks[1], (3 * DIM, DIM), jnp.float32) * s, 'proj_w': jax.random.normal(ks[2], (DIM, DIM), jnp.float32) * s, 'proj_b': jnp.zeros((DIM,), jnp.float32), 'norm2_g': jnp.ones((DIM,), jnp.float32), 'norm2_b': jnp.zeros((DIM,), jnp.float32), 'fc1_w': jax.random.normal(ks[3], (HIDDEN, DIM), jnp.float32) * s, 'fc1_b': jnp.zeros((HIDDEN,), jnp.float32), 'fc2_w': jax.random.normal(ks[4], (DIM, HIDDEN), jnp.float32) * s, 'fc2_b': jnp.zeros((DIM,), jnp.float32)}
    _L3_attn_all = _L3_attn_setup()
    _L3_attn_in = {k: v for k, v in _L3_attn_all.items() if k in ('norm1_g', 'norm1_b', 'qkv_w', 'proj_w', 'proj_b', 'norm2_g', 'norm2_b', 'fc1_w', 'fc1_b', 'fc2_w', 'fc2_b')}
    del _L3_attn_all

    def _L3_xattn_setup():
        import jax, jax.numpy as jnp
        import numpy as np
        key = jax.random.key(seed)
        k1, k2 = jax.random.split(key)
        B, T, K, D = (8, 512, 64, 128)
        X = jax.random.normal(k1, (B, T, D), dtype=jnp.float32)
        C = jax.random.normal(k2, (B, K, D), dtype=jnp.float32)
        sim_alpha = jnp.ones((1,), dtype=jnp.float32)
        sim_beta = jnp.zeros((1,), dtype=jnp.float32)
        return {'X': X, 'C': C, 'sim_alpha': sim_alpha, 'sim_beta': sim_beta}
    _L3_xattn_all = _L3_xattn_setup()
    _L3_xattn_in = {k: v for k, v in _L3_xattn_all.items() if k in ('sim_alpha', 'sim_beta')}
    del _L3_xattn_all

    def _L3_ffn_setup():
        import jax, jax.numpy as jnp
        import numpy as np
        B, S, D = (1, 256, 128)
        E, F = (16, 128)
        NG, TKG, K = (4, 2, 4)
        NSH = 2
        SCALE = 2.5
        STD = 0.02
        EPG = E // NG

        def _route(x_flat, router_w, bias):
            logits = x_flat.astype(jnp.float32) @ router_w.T
            scores = jax.nn.sigmoid(logits)
            s = scores + bias[None, :]
            sg = s.reshape(-1, NG, EPG)
            group_score = jax.lax.top_k(sg, 2)[0].sum(-1)
            gidx = jax.lax.top_k(group_score, TKG)[1]
            gmask = jnp.sum(jax.nn.one_hot(gidx, NG, dtype=jnp.float32), axis=1) > 0
            emask = jnp.repeat(gmask, EPG, axis=1)
            masked = jnp.where(emask, s, -1.0)
            topk_idx = jax.lax.top_k(masked, K)[1]
            tw = jnp.take_along_axis(scores, topk_idx, axis=1)
            tw = tw / (tw.sum(-1, keepdims=True) + 1e-20)
            tw = tw * SCALE
            return (topk_idx, tw)
        key = jax.random.key(seed)
        ks = jax.random.split(key, 8)
        return {'hidden_states': jax.random.normal(ks[0], (B, S, D), jnp.float32), 'router_w': jax.random.normal(ks[1], (E, D), jnp.float32) * STD, 'bias': jnp.zeros((E,), jnp.float32), 'gate_w': jax.random.normal(ks[2], (E, D, F), jnp.float32) * STD, 'up_w': jax.random.normal(ks[3], (E, D, F), jnp.float32) * STD, 'down_w': jax.random.normal(ks[4], (E, F, D), jnp.float32) * STD, 'sh_gate_w': jax.random.normal(ks[5], (D, NSH * F), jnp.float32) * STD, 'sh_up_w': jax.random.normal(ks[6], (D, NSH * F), jnp.float32) * STD, 'sh_down_w': jax.random.normal(ks[7], (NSH * F, D), jnp.float32) * STD}
    _L3_ffn_all = _L3_ffn_setup()
    _L3_ffn_in = {k: v for k, v in _L3_ffn_all.items() if k in ('router_w', 'bias', 'gate_w', 'up_w', 'down_w', 'sh_gate_w', 'sh_up_w', 'sh_down_w')}
    del _L3_ffn_all
    return {'x': x, 'ctx_1024': ctx_1024, 'mask_BxSxS2_bk0': mask_BxSxS2_bk0, 'mask_Bx1x1xS2_ff0': mask_Bx1x1xS2_ff0, 'L0_attn_W_query': _L0_attn_in['W_query'], 'L0_attn_W_key': _L0_attn_in['W_key'], 'L0_attn_W_value': _L0_attn_in['W_value'], 'L0_attn_W_proj': _L0_attn_in['W_proj'], 'L0_attn_b_proj': _L0_attn_in['b_proj'], 'L0_xattn_Wq': _L0_xattn_in['Wq'], 'L0_xattn_Wk': _L0_xattn_in['Wk'], 'L0_xattn_Wv': _L0_xattn_in['Wv'], 'L0_ffn_router_w': _L0_ffn_in['router_w'], 'L0_ffn_router_b': _L0_ffn_in['router_b'], 'L0_ffn_w1': _L0_ffn_in['w1'], 'L0_ffn_b1': _L0_ffn_in['b1'], 'L0_ffn_w2': _L0_ffn_in['w2'], 'L0_ffn_b2': _L0_ffn_in['b2'], 'L0_ffn_gamma': _L0_ffn_in['gamma'], 'L0_ffn_beta': _L0_ffn_in['beta'], 'L1_attn_qkv_w': _L1_attn_in['qkv_w'], 'L1_attn_qkv_b': _L1_attn_in['qkv_b'], 'L1_attn_out_w': _L1_attn_in['out_w'], 'L1_attn_out_b': _L1_attn_in['out_b'], 'L1_xattn_Wq': _L1_xattn_in['Wq'], 'L1_xattn_bq': _L1_xattn_in['bq'], 'L1_xattn_Wk': _L1_xattn_in['Wk'], 'L1_xattn_bk': _L1_xattn_in['bk'], 'L1_xattn_Wv': _L1_xattn_in['Wv'], 'L1_xattn_bv': _L1_xattn_in['bv'], 'L1_xattn_rel_table': _L1_xattn_in['rel_table'], 'L1_ffn_w_gate': _L1_ffn_in['w_gate'], 'L1_ffn_w_noise': _L1_ffn_in['w_noise'], 'L1_ffn_Wd': _L1_ffn_in['Wd'], 'L1_ffn_bd': _L1_ffn_in['bd'], 'L1_ffn_Wu': _L1_ffn_in['Wu'], 'L1_ffn_bu': _L1_ffn_in['bu'], 'L2_attn_ema_delta': _L2_attn_in['ema_delta'], 'L2_attn_ema_alpha': _L2_attn_in['ema_alpha'], 'L2_attn_ema_beta': _L2_attn_in['ema_beta'], 'L2_attn_ema_gamma': _L2_attn_in['ema_gamma'], 'L2_attn_ema_omega': _L2_attn_in['ema_omega'], 'L2_attn_ln_w': _L2_attn_in['ln_w'], 'L2_attn_ln_b': _L2_attn_in['ln_b'], 'L2_attn_Wv': _L2_attn_in['Wv'], 'L2_attn_bv': _L2_attn_in['bv'], 'L2_attn_Wmx': _L2_attn_in['Wmx'], 'L2_attn_bmx': _L2_attn_in['bmx'], 'L2_attn_Wh': _L2_attn_in['Wh'], 'L2_attn_bh': _L2_attn_in['bh'], 'L2_attn_qk_gamma': _L2_attn_in['qk_gamma'], 'L2_attn_qk_beta': _L2_attn_in['qk_beta'], 'L2_attn_rot_alpha': _L2_attn_in['rot_alpha'], 'L2_attn_rot_beta': _L2_attn_in['rot_beta'], 'L2_xattn_Wqkv': _L2_xattn_in['Wqkv'], 'L2_xattn_bqkv': _L2_xattn_in['bqkv'], 'L2_xattn_Wqkv_aux': _L2_xattn_in['Wqkv_aux'], 'L2_xattn_bqkv_aux': _L2_xattn_in['bqkv_aux'], 'L2_xattn_Wo': _L2_xattn_in['Wo'], 'L2_xattn_bo': _L2_xattn_in['bo'], 'L2_xattn_g': _L2_xattn_in['g'], 'L2_ffn_gate_w': _L2_ffn_in['gate_w'], 'L2_ffn_w1': _L2_ffn_in['w1'], 'L2_ffn_w2': _L2_ffn_in['w2'], 'L2_ffn_w3': _L2_ffn_in['w3'], 'L3_attn_norm1_g': _L3_attn_in['norm1_g'], 'L3_attn_norm1_b': _L3_attn_in['norm1_b'], 'L3_attn_qkv_w': _L3_attn_in['qkv_w'], 'L3_attn_proj_w': _L3_attn_in['proj_w'], 'L3_attn_proj_b': _L3_attn_in['proj_b'], 'L3_attn_norm2_g': _L3_attn_in['norm2_g'], 'L3_attn_norm2_b': _L3_attn_in['norm2_b'], 'L3_attn_fc1_w': _L3_attn_in['fc1_w'], 'L3_attn_fc1_b': _L3_attn_in['fc1_b'], 'L3_attn_fc2_w': _L3_attn_in['fc2_w'], 'L3_attn_fc2_b': _L3_attn_in['fc2_b'], 'L3_xattn_sim_alpha': _L3_xattn_in['sim_alpha'], 'L3_xattn_sim_beta': _L3_xattn_in['sim_beta'], 'L3_ffn_router_w': _L3_ffn_in['router_w'], 'L3_ffn_bias': _L3_ffn_in['bias'], 'L3_ffn_gate_w': _L3_ffn_in['gate_w'], 'L3_ffn_up_w': _L3_ffn_in['up_w'], 'L3_ffn_down_w': _L3_ffn_in['down_w'], 'L3_ffn_sh_gate_w': _L3_ffn_in['sh_gate_w'], 'L3_ffn_sh_up_w': _L3_ffn_in['sh_up_w'], 'L3_ffn_sh_down_w': _L3_ffn_in['sh_down_w']}

def reference(x, ctx_1024, mask_BxSxS2_bk0, mask_Bx1x1xS2_ff0, L0_attn_W_query, L0_attn_W_key, L0_attn_W_value, L0_attn_W_proj, L0_attn_b_proj, L0_xattn_Wq, L0_xattn_Wk, L0_xattn_Wv, L0_ffn_router_w, L0_ffn_router_b, L0_ffn_w1, L0_ffn_b1, L0_ffn_w2, L0_ffn_b2, L0_ffn_gamma, L0_ffn_beta, L1_attn_qkv_w, L1_attn_qkv_b, L1_attn_out_w, L1_attn_out_b, L1_xattn_Wq, L1_xattn_bq, L1_xattn_Wk, L1_xattn_bk, L1_xattn_Wv, L1_xattn_bv, L1_xattn_rel_table, L1_ffn_w_gate, L1_ffn_w_noise, L1_ffn_Wd, L1_ffn_bd, L1_ffn_Wu, L1_ffn_bu, L2_attn_ema_delta, L2_attn_ema_alpha, L2_attn_ema_beta, L2_attn_ema_gamma, L2_attn_ema_omega, L2_attn_ln_w, L2_attn_ln_b, L2_attn_Wv, L2_attn_bv, L2_attn_Wmx, L2_attn_bmx, L2_attn_Wh, L2_attn_bh, L2_attn_qk_gamma, L2_attn_qk_beta, L2_attn_rot_alpha, L2_attn_rot_beta, L2_xattn_Wqkv, L2_xattn_bqkv, L2_xattn_Wqkv_aux, L2_xattn_bqkv_aux, L2_xattn_Wo, L2_xattn_bo, L2_xattn_g, L2_ffn_gate_w, L2_ffn_w1, L2_ffn_w2, L2_ffn_w3, L3_attn_norm1_g, L3_attn_norm1_b, L3_attn_qkv_w, L3_attn_proj_w, L3_attn_proj_b, L3_attn_norm2_g, L3_attn_norm2_b, L3_attn_fc1_w, L3_attn_fc1_b, L3_attn_fc2_w, L3_attn_fc2_b, L3_xattn_sim_alpha, L3_xattn_sim_beta, L3_ffn_router_w, L3_ffn_bias, L3_ffn_gate_w, L3_ffn_up_w, L3_ffn_down_w, L3_ffn_sh_gate_w, L3_ffn_sh_up_w, L3_ffn_sh_down_w):
    import jax
    import jax.numpy as jnp

    def _L0_attn_ref(x, W_query, W_key, W_value, W_proj, b_proj):
        import jax, jax.numpy as jnp
        import numpy as np
        B, T, D = (2, 256, 128)
        H = 16
        DH = D // H

        def alibi_bias(n_heads, token_cnt, dtype=jnp.float32):
            slopes = 2.0 ** (-8.0 * jnp.arange(1, n_heads + 1, dtype=dtype) / n_heads)
            pos = jnp.arange(token_cnt, dtype=dtype)
            rel = pos[None, :] - pos[:, None]
            return slopes[:, None, None] * rel[None, :, :]
        b, t, _ = x.shape

        def heads(y):
            return y.reshape(b, t, H, DH).transpose(0, 2, 1, 3)
        q = heads(x @ W_query)
        k = heads(x @ W_key)
        v = heads(x @ W_value)
        scores = jnp.einsum('bhqd,bhkd->bhqk', q, k)
        causal = jnp.triu(jnp.ones((t, t), dtype=bool), k=1)
        scores = jnp.where(causal[None, None], -jnp.inf, scores)
        scores = scores + alibi_bias(H, t, scores.dtype)[None]
        scores = scores / jnp.sqrt(jnp.asarray(DH, scores.dtype))
        w = jax.nn.softmax(scores, axis=-1)
        ctx = jnp.einsum('bhqk,bhkd->bqhd', w, v).reshape(b, t, H * DH)
        return ctx @ W_proj + b_proj

    def _L0_xattn_ref(seq1, seq2, attn_mask, Wq, Wk, Wv):
        import jax, jax.numpy as jnp
        import numpy as np
        B, S, D_IN, D_H = (4, 256, 128, 128)
        q = jnp.einsum('bsd,hd->bsh', seq1, Wq)
        k = jnp.einsum('bsd,hd->bsh', seq2, Wk)
        v = jnp.einsum('bsd,hd->bsh', seq2, Wv)
        score = jnp.einsum('bqh,bkh->bqk', q, k) / jnp.sqrt(jnp.float32(q.shape[-1]))
        mask_score = jnp.where(attn_mask, jnp.float32(1e-09), score)
        score_matrix = jax.nn.softmax(mask_score, axis=1)
        out = jnp.einsum('bqk,bkh->bqh', score_matrix, v)
        return out

    def _L0_ffn_ref(tgt, router_w, router_b, w1, b1, w2, b2, gamma, beta):
        import jax, jax.numpy as jnp
        import numpy as np
        B, S, D, F, E = (2, 256, 128, 512, 8)
        LN_EPS = 1e-05

        def _xavier(key, shape, fan_in, fan_out):
            a = np.sqrt(6.0 / (fan_in + fan_out))
            return jax.random.uniform(key, shape, jnp.float32, -a, a)
        logits = jnp.einsum('bsd,ed->bse', tgt, router_w) + router_b
        rw = jax.nn.softmax(logits, axis=-1)
        rw = jnp.zeros_like(rw).at[..., 0].set(1.0)
        h = jax.nn.relu(jnp.einsum('bsd,edf->besf', tgt, w1) + b1[None, :, None, :])
        eo = jnp.einsum('besf,efd->besd', h, w2) + b2[None, :, None, :]
        tgt2 = jnp.einsum('besd,bse->bsd', eo, rw)
        x = tgt + tgt2
        mean = jnp.mean(x, axis=-1, keepdims=True)
        var = jnp.mean(jnp.square(x - mean), axis=-1, keepdims=True)
        return (x - mean) * jax.lax.rsqrt(var + LN_EPS) * gamma + beta

    def _L1_attn_ref(x, qkv_w, qkv_b, out_w, out_b):
        import jax, jax.numpy as jnp
        import numpy as np
        EMBED_DIM = 128
        NUM_HEADS = 16
        HEAD_DIM = EMBED_DIM // NUM_HEADS
        FEATURE_EPS = 1e-06
        DEN_EPS = 1e-06
        b, l, e = x.shape
        qkv = (x @ qkv_w.T + qkv_b).reshape(b, l, 3, NUM_HEADS, HEAD_DIM)
        qkv = jnp.transpose(qkv, (2, 0, 3, 1, 4))
        q, k, v = (qkv[0], qkv[1], qkv[2])
        q = jax.nn.relu(q) + FEATURE_EPS
        k = jax.nn.relu(k) + FEATURE_EPS
        kv = jnp.cumsum(jnp.einsum('bhld,bhle->bhlde', k, v), axis=2)
        k_cum = jnp.cumsum(k, axis=2)
        num = jnp.einsum('bhld,bhlde->bhle', q, kv)
        den = jnp.maximum(jnp.einsum('bhld,bhld->bhl', q, k_cum)[..., None], DEN_EPS)
        out = num / den
        out = jnp.transpose(out, (0, 2, 1, 3)).reshape(b, l, e)
        return out @ out_w.T + out_b

    def _L1_xattn_ref(query, key, value, attention_mask, Wq, bq, Wk, bk, Wv, bv, rel_table):
        import jax, jax.numpy as jnp
        import numpy as np
        B, S, D, H = (2, 256, 128, 16)
        HEAD_DIM = D // H
        MAX_REL = 64

        def _split_heads(x, b):
            return x.reshape(b, -1, H, HEAD_DIM).transpose(0, 2, 1, 3)
        b, s, _ = query.shape
        q = _split_heads(query @ Wq + bq, b)
        k = _split_heads(key @ Wk + bk, b)
        v = _split_heads(value @ Wv + bv, b)
        scores = jnp.einsum('bhqd,bhkd->bhqk', q, k)
        idx = jnp.arange(s)
        dist = jnp.clip(idx[None, :] - idx[:, None], -MAX_REL, MAX_REL) + MAX_REL
        rel_k = rel_table[dist]
        scores = scores + jnp.einsum('bhqd,qkd->bhqk', q, rel_k)
        scores = scores / jnp.sqrt(jnp.asarray(HEAD_DIM, scores.dtype))
        scores = scores + attention_mask
        probs = jax.nn.softmax(scores, axis=-1)
        ctx = jnp.einsum('bhqk,bhkd->bhqd', probs, v)
        ctx = ctx.transpose(0, 2, 1, 3).reshape(b, s, H * HEAD_DIM)
        return ctx

    def _L1_ffn_ref(x, w_gate, w_noise, Wd, bd, Wu, bu):
        import jax, jax.numpy as jnp
        import numpy as np
        D_MODEL = 128
        N_EXPERTS = 8
        TOP_K = 2
        BOTTLENECK = 64
        B, S = (2, 512)
        ADAPTER_SCALE = 0.5

        def _moe_forward(x, w_gate, w_noise, Wd, bd, Wu, bu):
            b, s, d = x.shape
            xf = x.reshape(-1, d)
            T = xf.shape[0]
            clean_logits = xf @ w_gate
            logits = clean_logits
            k1 = min(TOP_K + 1, N_EXPERTS)
            top_logits, top_idx = jax.lax.top_k(logits, k1)
            top_k_logits = top_logits[:, :TOP_K]
            top_k_idx = top_idx[:, :TOP_K]
            top_k_gates = jax.nn.softmax(top_k_logits, axis=-1)
            rows = jnp.arange(T)[:, None]
            gates = jnp.zeros((T, N_EXPERTS), dtype=top_k_gates.dtype)
            gates = gates.at[rows, top_k_idx].set(top_k_gates)
            h = jax.nn.relu(jnp.einsum('td,edb->teb', xf, Wd) + bd[None, :, :])
            y = jnp.einsum('teb,ebd->ted', h, Wu) + bu[None, :, :]
            y = ADAPTER_SCALE * y
            out = jnp.einsum('te,ted->td', gates, y)
            return out.reshape(b, s, d)
        return _moe_forward(x, w_gate, w_noise, Wd, bd, Wu, bu)

    def _L2_attn_ref(x, ema_delta, ema_alpha, ema_beta, ema_gamma, ema_omega, ln_w, ln_b, Wv, bv, Wmx, bmx, Wh, bh, qk_gamma, qk_beta, rot_alpha, rot_beta):
        import jax, jax.numpy as jnp
        import numpy as np
        import math
        L, B, D = (256, 4, 128)
        ZDIM, HDIM, NDIM = (128, 256, 16)

        def _laplace(x, mu=0.707107, sigma=0.282095):
            return 0.5 * (1.0 + jax.lax.erf((x - mu) / (sigma * math.sqrt(2.0))))

        def _ema(x, delta, alpha, beta, gamma, omega):
            seq_len = x.shape[0]
            scale = math.sqrt(1.0 / delta.shape[1])
            residual = x * omega
            xe = jnp.transpose(x, (1, 2, 0))
            p = jax.nn.sigmoid(delta)
            q = 1.0 - p * jax.nn.sigmoid(alpha)
            vander = jnp.arange(seq_len, dtype=x.dtype)[None, None, :] * jnp.log(q)
            kern = jnp.einsum('dnl,dn->dl', p * beta * jnp.exp(vander), gamma * scale)
            n = 2 * seq_len
            out = jnp.fft.irfft(jnp.fft.rfft(xe, n=n) * jnp.fft.rfft(kern, n=n), n=n)[..., :seq_len]
            out = jnp.transpose(out, (2, 0, 1)).astype(x.dtype)
            return jax.nn.silu(out + residual)

        def _rotary_bias(seq_len, zdim, alpha, beta):
            half = zdim // 2
            freqs = jnp.exp(jnp.arange(half, dtype=jnp.float32) * (-math.log(10000.0) / half))
            ang = jnp.arange(seq_len, dtype=jnp.float32)[:, None] * freqs[None, :]
            sin, cos = (jnp.sin(ang), jnp.cos(ang))

            def rot(v):
                v = jnp.broadcast_to(v, (seq_len, zdim))
                v1, v2 = (v[:, :half], v[:, half:])
                return jnp.concatenate([v1 * cos - v2 * sin, v2 * cos + v1 * sin], axis=1)
            return rot(alpha) @ rot(beta).T
        seq_len = x.shape[0]
        residual = x
        mean = jnp.mean(x, -1, keepdims=True)
        var = jnp.var(x, -1, keepdims=True)
        xn = (x - mean) * jax.lax.rsqrt(var + 1e-05) * ln_w + ln_b
        v = jax.nn.silu(xn @ Wv.T + bv)
        mx = _ema(xn, ema_delta, ema_alpha, ema_beta, ema_gamma, ema_omega)
        base = mx @ Wmx.T + bmx
        u = jax.nn.sigmoid(base[..., :D])
        zr = jax.nn.silu(base[..., D:D + ZDIM + HDIM])
        hx = base[..., D + ZDIM + HDIM:]
        z, r = (zr[..., :ZDIM], zr[..., ZDIM:])
        z2 = z[..., None, :] * qk_gamma + qk_beta
        q = jnp.transpose(z2[:, :, 0], (1, 0, 2))
        k = jnp.transpose(z2[:, :, 1], (1, 0, 2))
        vb = jnp.transpose(v, (1, 0, 2))
        bias = _rotary_bias(seq_len, ZDIM, rot_alpha, rot_beta)
        qk = jnp.einsum('blz,bmz->blm', q, k) / seq_len + bias
        attn = _laplace(qk)
        h = jnp.einsum('blm,bmh->blh', attn, vb)
        h = jnp.transpose(h, (1, 0, 2))
        h = jax.nn.silu(hx + h * r @ Wh.T + bh)
        return residual + u * (h - residual)

    def _L2_xattn_ref(x, xa, Wqkv, bqkv, Wqkv_aux, bqkv_aux, Wo, bo, g):
        import jax, jax.numpy as jnp
        import numpy as np
        D, H = (128, 16)
        DH = D // H

        def _split_heads(z):
            b, t, _ = z.shape
            return z.reshape(b, t, H, DH).transpose(0, 2, 1, 3)
        qkv = x @ Wqkv + bqkv
        qkv_a = xa @ Wqkv_aux + bqkv_aux
        q, k, v = (_split_heads(c) for c in jnp.split(qkv, 3, axis=-1))
        qa, ka, va = (_split_heads(c) for c in jnp.split(qkv_a, 3, axis=-1))
        scale = 1.0 / jnp.sqrt(jnp.float32(DH))
        dots = jnp.einsum('bhqd,bhkd->bhqk', q, k) * scale
        dots_aux = jnp.einsum('bhqd,bhkd->bhqk', q, ka) * scale
        p = jax.nn.softmax(dots, axis=-1)
        pa = jax.nn.softmax(dots_aux, axis=-1)
        h_main = jnp.einsum('bhqk,bhkd->bhqd', p, v)
        h_aux = jnp.einsum('bhqk,bhkd->bhqd', pa, va)
        gate = jax.nn.sigmoid(g).reshape(1, H, 1, 1)
        out = h_main * (1.0 - gate) + h_aux * gate
        b, _, t, _ = out.shape
        out = out.transpose(0, 2, 1, 3).reshape(b, t, H * DH)
        return out @ Wo + bo

    def _L2_ffn_ref(x, gate_w, w1, w2, w3):
        import jax, jax.numpy as jnp
        import numpy as np
        DIM = 128
        N_EXPERTS = 8
        D_FF = 256
        TOP_K = 2
        orig_shape = x.shape
        xf = x.reshape(-1, orig_shape[-1])
        scores = jnp.einsum('td,ed->te', xf, gate_w)
        probs = jax.nn.softmax(scores.astype(jnp.float32), axis=-1)
        weights, idx = jax.lax.top_k(probs, TOP_K)
        weights = weights / jnp.sum(weights, axis=-1, keepdims=True)
        weights = weights.astype(x.dtype)
        x1 = jax.nn.silu(jnp.einsum('td,efd->tef', xf, w1))
        x3 = jnp.einsum('td,efd->tef', xf, w3)
        out_all = jnp.einsum('tef,edf->ted', x1 * x3, w2)
        expert_outs = jnp.take_along_axis(out_all, idx[:, :, None], axis=1)
        result = jnp.einsum('tkd,tk->td', expert_outs, weights)
        return result.reshape(orig_shape)

    def _L3_attn_ref(x, norm1_g, norm1_b, qkv_w, proj_w, proj_b, norm2_g, norm2_b, fc1_w, fc1_b, fc2_w, fc2_b):
        import jax, jax.numpy as jnp
        import numpy as np
        DIM = 128
        HEADS = 16
        HIDDEN = 512
        EPS_ATTN = 1e-06
        EPS_LN = 1e-05

        def layer_norm(x, g, b):
            mu = jnp.mean(x, axis=-1, keepdims=True)
            var = jnp.var(x, axis=-1, keepdims=True)
            return (x - mu) * jax.lax.rsqrt(var + EPS_LN) * g + b
        B, N, C = x.shape
        H = HEADS
        d = C // H
        h = layer_norm(x, norm1_g, norm1_b)
        qkv = jnp.einsum('bnc,oc->bno', h, qkv_w)
        qkv = qkv.reshape(B, N, 3, H, d)
        q = jnp.transpose(qkv[:, :, 0], (0, 2, 1, 3))
        k = jnp.transpose(qkv[:, :, 1], (0, 2, 1, 3))
        v = jnp.transpose(qkv[:, :, 2], (0, 2, 1, 3))
        q = jax.nn.elu(q) + 1.0
        k = jax.nn.elu(k) + 1.0
        kv = jnp.einsum('bhnd,bhne->bhde', k, v)
        ksum = jnp.sum(k, axis=2)
        z = 1.0 / (jnp.einsum('bhnd,bhd->bhn', q, ksum) + EPS_ATTN)
        attn_out = jnp.einsum('bhnd,bhde->bhne', q, kv) * z[..., None]
        attn_out = jnp.transpose(attn_out, (0, 2, 1, 3)).reshape(B, N, C)
        attn_out = jnp.einsum('bnc,oc->bno', attn_out, proj_w) + proj_b
        x = x + attn_out
        h = layer_norm(x, norm2_g, norm2_b)
        h = jax.nn.gelu(jnp.einsum('bnc,hc->bnh', h, fc1_w) + fc1_b, approximate=False)
        h = jnp.einsum('bnh,ch->bnc', h, fc2_w) + fc2_b
        return x + h

    def _L3_xattn_ref(X, C, sim_alpha, sim_beta):
        import jax, jax.numpy as jnp
        import numpy as np
        K = C.shape[1]
        sim = jax.nn.sigmoid(sim_beta + sim_alpha * jnp.einsum('bkd,btd->bkt', C, X))
        max_idx = jnp.argmax(sim, axis=1)
        mask = jax.nn.one_hot(max_idx, K, axis=1, dtype=sim.dtype)
        sim_out = sim * mask
        agg = jnp.einsum('bkt,btd->bkd', sim_out, X) + C
        denom = jnp.sum(mask, axis=-1, keepdims=True) + 1.0
        out_k = agg / denom
        out = jnp.einsum('bkt,bkd->btd', sim, out_k)
        return X + out

    def _L3_ffn_ref(hidden_states, router_w, bias, gate_w, up_w, down_w, sh_gate_w, sh_up_w, sh_down_w):
        import jax, jax.numpy as jnp
        import numpy as np
        B, S, D = (1, 256, 128)
        E, F = (16, 128)
        NG, TKG, K = (4, 2, 4)
        NSH = 2
        SCALE = 2.5
        STD = 0.02
        EPG = E // NG

        def _route(x_flat, router_w, bias):
            logits = x_flat.astype(jnp.float32) @ router_w.T
            scores = jax.nn.sigmoid(logits)
            s = scores + bias[None, :]
            sg = s.reshape(-1, NG, EPG)
            group_score = jax.lax.top_k(sg, 2)[0].sum(-1)
            gidx = jax.lax.top_k(group_score, TKG)[1]
            gmask = jnp.sum(jax.nn.one_hot(gidx, NG, dtype=jnp.float32), axis=1) > 0
            emask = jnp.repeat(gmask, EPG, axis=1)
            masked = jnp.where(emask, s, -1.0)
            topk_idx = jax.lax.top_k(masked, K)[1]
            tw = jnp.take_along_axis(scores, topk_idx, axis=1)
            tw = tw / (tw.sum(-1, keepdims=True) + 1e-20)
            tw = tw * SCALE
            return (topk_idx, tw)
        x = hidden_states.reshape(-1, D)
        topk_idx, tw = _route(x, router_w, bias)
        combine = (jax.nn.one_hot(topk_idx, E, dtype=tw.dtype) * tw[..., None]).sum(1)
        h = jnp.einsum('td,edf->etf', x, gate_w)
        u = jnp.einsum('td,edf->etf', x, up_w)
        y = jnp.einsum('etf,efd->etd', jax.nn.silu(h) * u, down_w)
        routed = jnp.einsum('etd,te->td', y, combine)
        sh = jax.nn.silu(x @ sh_gate_w) * (x @ sh_up_w) @ sh_down_w
        return (routed + sh).reshape(hidden_states.shape)
    x = x + _L0_attn_ref(_layernorm(x, axis=-1), L0_attn_W_query, L0_attn_W_key, L0_attn_W_value, L0_attn_W_proj, L0_attn_b_proj)
    x = x + _L0_xattn_ref(_layernorm(x, axis=-1), ctx_1024, mask_BxSxS2_bk0, L0_xattn_Wq, L0_xattn_Wk, L0_xattn_Wv)
    x = x + _L0_ffn_ref(_layernorm(x, axis=-1), L0_ffn_router_w, L0_ffn_router_b, L0_ffn_w1, L0_ffn_b1, L0_ffn_w2, L0_ffn_b2, L0_ffn_gamma, L0_ffn_beta)
    x = x + _L1_attn_ref(_layernorm(x, axis=-1), L1_attn_qkv_w, L1_attn_qkv_b, L1_attn_out_w, L1_attn_out_b)
    x = x + _L1_xattn_ref(_layernorm(x, axis=-1), ctx_1024, ctx_1024, mask_Bx1x1xS2_ff0, L1_xattn_Wq, L1_xattn_bq, L1_xattn_Wk, L1_xattn_bk, L1_xattn_Wv, L1_xattn_bv, L1_xattn_rel_table)
    x = x + _L1_ffn_ref(_layernorm(x, axis=-1), L1_ffn_w_gate, L1_ffn_w_noise, L1_ffn_Wd, L1_ffn_bd, L1_ffn_Wu, L1_ffn_bu)
    x = x + _L2_attn_ref(_layernorm(x, axis=-1), L2_attn_ema_delta, L2_attn_ema_alpha, L2_attn_ema_beta, L2_attn_ema_gamma, L2_attn_ema_omega, L2_attn_ln_w, L2_attn_ln_b, L2_attn_Wv, L2_attn_bv, L2_attn_Wmx, L2_attn_bmx, L2_attn_Wh, L2_attn_bh, L2_attn_qk_gamma, L2_attn_qk_beta, L2_attn_rot_alpha, L2_attn_rot_beta)
    x = x + _L2_xattn_ref(_layernorm(x, axis=-1), ctx_1024, L2_xattn_Wqkv, L2_xattn_bqkv, L2_xattn_Wqkv_aux, L2_xattn_bqkv_aux, L2_xattn_Wo, L2_xattn_bo, L2_xattn_g)
    x = x + _L2_ffn_ref(_layernorm(x, axis=-1), L2_ffn_gate_w, L2_ffn_w1, L2_ffn_w2, L2_ffn_w3)
    x = x + _L3_attn_ref(_layernorm(x, axis=-1), L3_attn_norm1_g, L3_attn_norm1_b, L3_attn_qkv_w, L3_attn_proj_w, L3_attn_proj_b, L3_attn_norm2_g, L3_attn_norm2_b, L3_attn_fc1_w, L3_attn_fc1_b, L3_attn_fc2_w, L3_attn_fc2_b)
    x = x + _L3_xattn_ref(_layernorm(x, axis=-1), ctx_1024, L3_xattn_sim_alpha, L3_xattn_sim_beta)
    x = x + _L3_ffn_ref(_layernorm(x, axis=-1), L3_ffn_router_w, L3_ffn_bias, L3_ffn_gate_w, L3_ffn_up_w, L3_ffn_down_w, L3_ffn_sh_gate_w, L3_ffn_sh_up_w, L3_ffn_sh_down_w)
    return x

_drawn_inputs = setup_inputs


def setup_inputs(seed=0):
    import zlib

    import numpy as np

    out = dict(_drawn_inputs(seed))
    spreads = {'L0_attn_b_proj': (0.0, 0.1),
     'L0_ffn_router_b': (0.0, 0.1),
     'L0_ffn_b1': (0.0, 0.1),
     'L0_ffn_b2': (0.0, 0.1),
     'L0_ffn_gamma': (1.0, 0.2),
     'L0_ffn_beta': (0.0, 0.1),
     'L1_xattn_bq': (0.0, 0.8),
     'L1_xattn_bk': (0.0, 0.8),
     'L1_xattn_bv': (0.0, 0.1),
     'L1_ffn_bd': (0.0, 0.588),
     'L1_ffn_bu': (0.0, 0.1),
     'L2_attn_ln_w': (1.0, 0.6),
     'L2_attn_ln_b': (0.0, 0.454),
     'L2_attn_bv': (0.0, 0.8),
     'L2_attn_bmx': (0.0, 0.279),
     'L2_attn_bh': (0.0, 0.315),
     'L2_attn_qk_beta': (0.0, 0.8),
     'L2_xattn_g': (0.0, 0.34),
     'L3_attn_norm1_g': (1.0, 0.6),
     'L3_attn_norm1_b': (0.0, 0.739),
     'L3_attn_proj_b': (0.0, 0.1),
     'L3_attn_norm2_g': (1.0, 0.6),
     'L3_attn_norm2_b': (0.0, 0.8),
     'L3_attn_fc1_b': (0.0, 0.391),
     'L3_attn_fc2_b': (0.0, 0.1),
     'L3_ffn_bias': (0.0, 0.8)}
    factors = {'L1_xattn_Wq': 8.0,
     'L1_xattn_Wk': 8.0,
     'L1_xattn_rel_table': 8.0,
     'L1_ffn_Wd': 5.391,
     'L1_ffn_Wu': 4.029,
     'L2_attn_ema_delta': 6.072,
     'L2_attn_ema_alpha': 6.583,
     'L2_attn_Wv': 8.0,
     'L2_attn_Wh': 8.0,
     'L2_attn_qk_gamma': 8.0,
     'L2_attn_rot_alpha': 8.0,
     'L2_attn_rot_beta': 8.0,
     'L2_xattn_bqkv': 6.699,
     'L2_xattn_bqkv_aux': 5.385,
     'L2_xattn_bo': 4.132,
     'L2_ffn_gate_w': 6.177,
     'L2_ffn_w1': 5.045,
     'L2_ffn_w2': 5.353,
     'L2_ffn_w3': 5.806,
     'L3_attn_qkv_w': 3.654,
     'L3_attn_proj_w': 3.639,
     'L3_ffn_router_w': 8.0,
     'L3_ffn_gate_w': 8.0,
     'L3_ffn_up_w': 8.0,
     'L3_ffn_down_w': 8.0,
     'L3_ffn_sh_gate_w': 8.0,
     'L3_ffn_sh_up_w': 8.0,
     'L3_ffn_sh_down_w': 8.0}
    for name, (base, spread) in spreads.items():
        noise = np.random.default_rng([zlib.crc32(name.encode()), seed]).standard_normal(out[name].shape)
        drawn = base * np.exp(spread * noise) if base else spread * noise
        out[name] = jnp.asarray(drawn.astype(out[name].dtype))
    for name, factor in factors.items():
        out[name] = (out[name] * factor).astype(out[name].dtype)
    return out
```

```python
from contextlib import ExitStack

import numpy as np
import concourse.bass as bass
from concourse import mybir

F32 = mybir.dt.float32
BF16 = mybir.dt.bfloat16
U8 = mybir.dt.uint8
ALU = mybir.AluOpType
ACT = mybir.ActivationFunctionType
AX = mybir.AxisListType

D = 128
B, S = 64, 64
T = B * S
GW = 512
G = T // GW
TPG = GW // 128
H, DH = 16, 8
NQ = 4
LN_EPS = 1e-5
NEG = -1.0e30
LOWEST = -3.0e38


class Stage:

    def __init__(self, nc):
        self.nc, self.stack, self.sems = nc, ExitStack(), []

    def __enter__(self):
        self.stack.__enter__()
        return self

    def sem(self, *names):
        new = [self.nc.alloc_semaphore(n) for n in names]
        self.sems += new
        return new if len(new) > 1 else new[0]

    def block(self):
        engines = (self.nc.vector, self.nc.scalar, self.nc.tensor, self.nc.sync)
        for i, s in enumerate(self.sems):
            engines[i % len(engines)].sem_inc(s, 1)
        self.nc.all_engine_barrier()
        return self.nc.Block(no_gpsimd_drain=True)

    def sb(self, name, shape, dt=F32):
        return self.stack.enter_context(self.nc.sbuf_tensor(name, shape, dt))

    def __exit__(self, *a):
        self.nc.clear_and_free_semaphores(self.sems)
        self.nc.all_engine_barrier()
        return self.stack.__exit__(*a)


def count(n):
    return n + 1


class Chain:

    def __init__(self, eng, sem, per=0):
        self.eng, self.sem, self.per, self.k, self.base = eng, sem, per, 0, 0

    def turn(self, base):
        assert self.k in (0, self.per), (self.k, self.per)
        self.k, self.base = 0, base * self.per

    def link(self, ins):
        self.k += 1
        ins.then_inc(self.sem, 1)
        self.eng.wait_ge(self.sem, count(self.base + self.k))


class Core:

    def __init__(self, nc, cols, stack, dram):
        self.nc, self.cols, self.dram = nc, cols, dram
        sb = lambda n, s, dt=F32: stack.enter_context(nc.sbuf_tensor(n, s, dt))
        self.x = sb("x_residual", [D, T])
        self.ctx = sb("ctx_features", [D, T])
        self.h = sb("h_normed", [D, T])
        experts = sb("weights_experts", [128, max(cols["l2f"][""], cols["l3f"][""])])
        self.packed = {"first": sb("weights_first", [128, cols["first"][""]]),
                       "shared": sb("weights_shared", [128, cols["shared"][""]]), "l2f": experts, "l3f": experts}
        self.areas = {name: area for area, pieces in cols.items() for name in pieces if name}
        self.ps = stack.enter_context(nc.psum_tensor("banks", [128, 8 * 512], F32))

    def w(self, name):
        area = self.areas[name]
        o, w, rows = self.cols[area][name]
        return self.packed[area][0:rows, o:o + w]

    def bank(self, i, n=512):
        return self.ps[:, i * 512:i * 512 + n]


def layer_norm(k, src, dst, tag, gain=None, bias=None, add_to=None, add=None):
    nc = k.nc
    mean_w, eps = k.w("c_mean"), k.w("c_eps")
    with Stage(nc) as st:
        mean_ready, centred, squared, var_ready, logged, rstd_ready, scaled, normed = st.sem(
            *[f"{tag}_{n}" for n in "mean_ready centred squared var_ready logged rstd_ready scaled normed".split()])
        sq = st.sb(f"{tag}_squares", [D, T])

        with st.block() as block:
            @block.tensor
            def _(pe):
                def mean(g):
                    c = bass.ds(g * GW, GW)
                    nc.tensor.matmul(k.ps[:, c], mean_w, src[:, c]).then_inc(mean_ready, 1)

                def variance(g):
                    c = bass.ds(g * GW, GW)
                    pe.wait_ge(squared, count(g + 1))
                    nc.tensor.matmul(k.ps[:, c], mean_w, sq[:, c]).then_inc(var_ready, 1)

                mean(0)
                mean(1)
                mean(2)
                with pe.Fori(0, G - 3) as g:
                    variance(g)
                    mean(g + 3)
                for g in range(G - 3, G):
                    variance(g)

            @block.scalar
            def _(act):
                nc.scalar.preload_act_table_set("natural_log_exp_and_others")

                def square(g):
                    act.wait_ge(centred, count(g + 1))
                    act.wait_ge(mean_ready, count(1))
                    nc.scalar.activation(sq[:, bass.ds(g * GW, GW)], dst[:, bass.ds(g * GW, GW)],
                                         ACT.Square).then_inc(squared, 1)

                def rstd(g):
                    v = k.ps[:, bass.ts(g, GW)]
                    act.wait_ge(var_ready, count(g + 1))
                    act.wait_ge(mean_ready, count(1))
                    nc.scalar.activation(v, v, ACT.Ln, bias=eps).then_inc(logged, 1)
                    act.wait_ge(mean_ready, count(1))
                    act.wait_ge(logged, count(g + 1))
                    nc.scalar.activation(v, v, ACT.Exp, scale=-0.5).then_inc(rstd_ready, 1)

                square(0)
                square(1)
                with act.Fori(0, G - 2) as g:
                    rstd(g)
                    square(g + 2)
                rstd(G - 2)
                rstd(G - 1)

            @block.vector
            def _(dve):
                def centre(g):
                    c = bass.ds(g * GW, GW)
                    dve.wait_ge(mean_ready, count(g + 1))
                    nc.vector.tensor_tensor(dst[:, c], src[:, c], k.ps[:, c], ALU.subtract).then_inc(centred, 1)

                def scale(g):
                    c = bass.ts(g, GW)
                    dve.wait_ge(rstd_ready, count(g + 1))
                    if gain is None:
                        nc.vector.tensor_tensor(dst[:, c], dst[:, c], k.ps[:, c], ALU.mult).then_inc(scaled, 1)
                    else:
                        nc.vector.scalar_tensor_tensor(dst[:, c], dst[:, c], gain, k.ps[:, c],
                                                       ALU.mult, ALU.mult).then_inc(scaled, 1)
                        dve.wait_ge(scaled, count(g + 1))
                        nc.vector.tensor_scalar(dst[:, c], dst[:, c], bias, None, ALU.add).then_inc(normed, 1)

                centre(0)
                centre(1)
                with dve.Fori(0, G - 2) as g:
                    centre(g + 2)
                    scale(g)
                scale(G - 2)
                scale(G - 1)

            if add_to is not None:
                @block.gpsimd
                def _(pool):
                    with pool.Fori(0, G) as g:
                        c = bass.ts(g, GW)
                        pool.wait_ge(scaled if gain is None else normed, count(g + 1))
                        nc.gpsimd.tensor_tensor(add_to[:, c], add_to[:, c], (dst if add is None else add)[:, c], ALU.add)


class Load:

    def __init__(self, k, parts):
        self.k, nc = k, k.nc
        self.loaded = [nc.alloc_semaphore(name + "_loaded") for name, _, _ in parts]
        with nc.Block(no_gpsimd_drain=True) as block:
            @block.sync
            def _(sp):
                for (_, to, source), loaded in zip(parts, self.loaded):
                    nc.sync.dma_start(to, source).then_inc(loaded, 16)

    def finish(self):
        nc = self.k.nc
        with nc.Block(no_gpsimd_drain=True) as block:
            @block.sync
            def _(sp):
                for loaded in self.loaded:
                    sp.wait_ge(loaded, 16)
        nc.clear_and_free_semaphores(self.loaded)
        nc.all_engine_barrier()


def store_stage(k, out):
    nc = k.nc
    with Stage(nc) as st:
        stored = st.sem("x_stored")
        with st.block() as block:
            @block.sync
            def _(sp):
                nc.sync.dma_start(out, k.x[:, :]).then_inc(stored, 16)
                sp.wait_ge(stored, count(16))


def softmax_attention(k, tag, q, sources, out_w=None, out_b=None, score_bias=None, rel=None, normed=False):
    nc, ns = k.nc, len(sources)
    NB = 2 * ns
    NU = NB * TPG
    TURNS = G // 2
    gated, biased_scores = sources[0][5] is not None, score_bias is not None or rel is not None
    if not normed:
        layer_norm(k, k.x, k.h, tag + "_ln")
    with Stage(nc) as st:
        (zeroed, q_mm, q_sb, k_mm, k_sb, staged, v_mm, v_sb, s_mm, biased, max_ready, s_read, e_ready, sum_ready,
         r_ready, p_ready, t_mm, pt_sb, pv_mm, c_read, c_ready, o_mm, x_done, offset) = st.sem(*[f"{tag}_{n}" for n in (
             "zeroed q_mm q_sb k_mm k_sb staged v_mm v_sb s_mm biased max_ready s_read e_ready sum_ready "
             "r_ready p_ready t_mm pt_sb pv_mm c_read c_ready o_mm x_done offset").split()])
        if rel is not None:
            rel_loaded = st.sem(tag + "_rel_loaded0", tag + "_rel_loaded1")
            relb = st.sb(tag + "_rel", [128, 2, 2, H // 2 * S])
        ke = st.sb(tag + "_keys_spread", [D, 2, GW // S, 2, S])
        qe = st.sb(tag + "_queries_spread", [D, 2, GW // S, 2, S])
        twice = st.sb(tag + "_source_twice", [D, GW // S, 2, S])
        ve = st.sb(tag + "_values_spread", [128, GW // S, 2, D])
        prob = st.sb(tag + "_probs", [128, 4, H, S])
        pt = st.sb(tag + "_probs_turned", [128, 2, 8, 128])
        cf = st.sb(tag + "_context", [D, 2, GW])
        spread_bias = st.sb(tag + "_spread_bias", [D, 1 + ns, 2])
        small = st.sb(tag + "_small", [128, 3, 4, H])
        if gated:
            gates = st.sb(tag + "_gates", [D, 3])
            gate_exp, gate_step, mixed = st.sem(tag + "_gate_exp", tag + "_gate_step", tag + "_mixed")
        scores = k.ps[:, 2 * 512:6 * 512].rearrange("p (r c) -> p r c", r=NQ)[:, :, 0:NQ * S]
        by_head = lambda a: a.rearrange("p r (h s) -> p r h s", s=S)
        by_seq = lambda a: a.rearrange("p r (b c) -> p r b c", b=2)
        scale = float(DH) ** -0.5

        def turns(eng, step):
            def body(it, last):
                for m in range(NU):
                    step(it, m, m // TPG, m % TPG, last)
            with eng.Fori(0, TURNS - 1) as it:
                body(it, False)
            body(TURNS - 1, True)

        unit = lambda it, m: it * NU + m
        phase = lambda it, j: it * NB + j
        group = lambda it, j: it * 2 + j // ns
        more = lambda m, last: not (last and m >= NU)
        more_phases = lambda j, last: not (last and j >= NB)

        with st.block() as block:
            if rel is not None:
                @block.sync
                def _(sp):
                    def load(u, p):
                        for h in range(2):
                            nc.sync.dma_start(relb[64 * h:64 * h + 64, p], rel[bass.ds(u * 128, 128), h * 512:h * 512 + 512]
                                              .rearrange("(b s) n -> s b n", b=2)).then_inc(rel_loaded[p], 16)

                    load(0, 0)
                    load(1, 1)
                    with sp.Fori(0, T // 256 - 1) as i:
                        for p in range(2):
                            sp.wait_ge(biased, count(i * 2 + (p + 1)))
                            load(i * 2 + (p + 2), p)

            @block.gpsimd
            def _(pool):
                def stage(it, j, half):
                    c = bass.ds(group(it, j) * GW + half * (GW // 2), GW // 2)
                    nc.gpsimd.tensor_copy(twice[:, 4 * half:4 * half + 4], sources[j % ns][0][:, c]
                                          .rearrange("p (b s) -> p b s", s=S).unsqueeze(2)
                                          .broadcast_to([D, 4, 2, S])).then_inc(staged, 1)

                def normalise(it, m):
                    pool.wait_ge(r_ready, count(unit(it, m) + 1))
                    p = prob[:, m % 4]
                    nc.gpsimd.tensor_tensor(p, p, small[:, 2, m % 4].unsqueeze(2).broadcast_to([128, H, S]),
                                            ALU.mult).then_inc(p_ready, 1)

                nc.gpsimd.memset(ve[:, :, :, :], 0.0).then_inc(zeroed, 1)
                stage(0, 0, 0)
                stage(0, 0, 1)
                normalise(0, 0)

                def step(it, m, j, u, last):
                    if more(m + 1, last):
                        normalise(it, m + 1)
                    if u < 2 and more_phases(j + 1, last):
                        pool.wait_ge(v_mm, count(phase(it, j) * 2 + (u + 1)))
                        stage(it, j + 1, u)

                turns(pool, step)

            @block.tensor
            def _(pe):
                def scores_mm(it, m):
                    j, t = m // TPG % NB, m % TPG
                    if t == 0:
                        pe.wait_ge(k_sb, count(phase(it, m // TPG) + 1))
                    pe.wait_ge(s_read, count(unit(it, m)))
                    for b in range(2):
                        for r in range(NQ):
                            f = slice(32 * r, 32 * r + 32)
                            x = nc.tensor.matmul(scores[:, r, b * 2 * S:(b + 1) * 2 * S],
                                                 qe[f, j // ns, t * 2 + b].rearrange("p h s -> p (h s)"),
                                                 ke[f, j % 2, t * 2 + b].rearrange("p h s -> p (h s)"),
                                                 tile_position=(32 * r, 0))
                    x.then_inc(s_mm, 1)

                def turn(it, m):
                    pe.wait_ge(pt_sb, count(unit(it, m)))
                    pe.wait_ge(p_ready, count(unit(it, m) + 1))
                    for i in range(8):
                        x = nc.tensor.transpose(k.bank(6 + i // 4)[:, (i % 4) * 128:(i % 4) * 128 + 128],
                                                prob[:, m % 4, 2 * i:2 * i + 2].rearrange("p h s -> p (h s)"),
                                                k.w("c_ident"))
                    x.then_inc(t_mm, 1)

                def values(it, m):
                    j, t = m // TPG, m % TPG
                    if t == 0:
                        pe.wait_ge(v_sb, count(phase(it, j) * 2 + 1))
                        if out_w is None or gated:
                            pe.wait_ge(c_read, count(phase(it, j)))
                        if out_w is not None and j % ns == 0:
                            pe.wait_ge(x_done, count(group(it, j)))
                    if t == 2:
                        pe.wait_ge(v_sb, count(phase(it, j) * 2 + 2))
                    pe.wait_ge(pt_sb, count(unit(it, m) + 1))
                    for b in range(2):
                        for r in range(NQ):
                            f = slice(32 * r, 32 * r + 32)
                            for h in range(2):
                                x = nc.tensor.matmul(
                                    k.bank(1)[f, t * 128 + b * 64:t * 128 + b * 64 + 64],
                                    ve[:, t * 2 + b, h, f], pt[:, m % 2, 2 * r + b, h * 64:h * 64 + 64],
                                    start=(h == 0), stop=(h == 1), tile_position=(0, 32 * r))
                    x.then_inc(pv_mm, 1)

                def query(it, j):
                    nc.tensor.matmul(k.bank(0), k.w(q[0]), k.h[:, bass.ts(group(it, j), GW)]).then_inc(q_mm, 1)

                def key(it, j):
                    s = sources[j % ns]
                    pe.wait_ge(q_sb, count(group(it, j) + 1))
                    nc.tensor.matmul(k.bank(0), k.w(s[1]), s[0][:, bass.ts(group(it, j), GW)]).then_inc(k_mm, 1)

                def value(it, j, half):
                    if half == 0:
                        pe.wait_ge(k_sb, count(phase(it, j) + 1))
                    else:
                        pe.wait_ge(v_sb, count(phase(it, j) * 2 + 1))
                    pe.wait_ge(staged, count(phase(it, j) * 2 + (half + 1)))
                    for b in range(4):
                        x = nc.tensor.matmul(k.bank(0)[:, b * D:b * D + D],
                                             twice[:, 4 * half + b].rearrange("p c s -> p (c s)"),
                                             k.w(sources[j % ns][3]))
                    x.then_inc(v_mm, 1)

                query(0, 0)
                key(0, 0)
                value(0, 0, 0)
                value(0, 0, 1)
                scores_mm(0, 0)
                scores_mm(0, 1)

                def step(it, m, j, u, last):
                    following = more_phases(j + 1, last)
                    turn(it, m)
                    if more(m + 2, last):
                        scores_mm(it, m + 2)
                    if u == 1 and following:
                        pe.wait_ge(v_sb, count(phase(it, j) * 2 + 2))
                        if (j + 1) % ns == 0:
                            query(it, j + 1)
                    values(it, m)
                    if following:
                        if u == 1:
                            key(it, j + 1)
                        if u >= 2:
                            value(it, j + 1, u - 2)
                    if u == TPG - 1 and j % ns == ns - 1 and out_w is not None:
                        pe.wait_ge(c_ready, count(group(it, j) + 1))
                        nc.tensor.matmul(k.bank(1), k.w(out_w), cf[:, 0]).then_inc(o_mm, 1)

                turns(pe, step)

            @block.scalar
            def _(act):
                lower, upper = k.w("c_by_h"), k.w("c_by_p")

                def spread(out, mask, bias, row):
                    for i in range(2):
                        x = nc.scalar.activation(out[:, :, i], k.bank(0).rearrange("p (b s) -> p b s", s=S),
                                                 ACT.Identity, scale=mask[:, i:i + 1],
                                                 bias=spread_bias[:, row, i:i + 1] if bias else 0.0)
                    return x

                def query(it, j):
                    act.wait_ge(q_mm, count(group(it, j) + 1))
                    spread(qe[:, j // ns % 2], lower, q[1], 0).then_inc(q_sb, 1)

                def key(it, j):
                    act.wait_ge(k_mm, count(phase(it, j) + 1))
                    spread(ke[:, j % 2], upper, sources[j % ns][2], 1 + j % ns).then_inc(k_sb, 1)

                def value(it, j, half):
                    act.wait_ge(v_mm, count(phase(it, j) * 2 + (half + 1)))
                    for p in range(2):
                        rows = slice(64 * p, 64 * p + 64)
                        for h in range(2):
                            f = lambda a: a.rearrange("p b (r n e) -> p b r n e", r=NQ, n=NQ)[:, :, :, 2 * p + h]
                            x = nc.scalar.copy(f(ve[rows, 4 * half:4 * half + 4, h]),
                                               f(k.bank(0)[rows].rearrange("p (b d) -> p b d", d=D)))
                    x.then_inc(v_sb, 1)

                def exp(it, m):
                    act.wait_ge(s_read, count(unit(it, m) + 1))
                    nc.scalar.activation(prob[:, m % 4], prob[:, m % 4], ACT.Exp, scale=scale).then_inc(e_ready, 1)

                nc.scalar.preload_act_table(ACT.Exp)
                if gated:
                    nc.scalar.activation(gates[:, 0:1], k.w(sources[0][5]), ACT.Exp, scale=-1.0).then_inc(gate_exp, 1)
                if q[1] is not None:
                    nc.scalar.activation(spread_bias[:, 0], lower, ACT.Identity, scale=k.w(q[1]))
                    for i in range(ns):
                        x = nc.scalar.activation(spread_bias[:, 1 + i], upper, ACT.Identity, scale=k.w(sources[i][2]))
                    x.then_inc(offset, 1)
                    act.wait_ge(offset, count(1))
                query(0, 0)
                key(0, 0)
                act.wait_ge(zeroed, count(1))
                value(0, 0, 0)
                value(0, 0, 1)
                exp(0, 0)
                exp(0, 1)

                def step(it, m, j, u, last):
                    following = more_phases(j + 1, last)
                    act.wait_ge(t_mm, count(unit(it, m) + 1))
                    nc.scalar.copy(pt[:, m % 2].rearrange("p j q -> p (j q)"), k.ps[:, 6 * 512:8 * 512]).then_inc(pt_sb, 1)
                    if u == 1 and following and (j + 1) % ns == 0:
                        query(it, j + 1)
                    if more(m + 2, last):
                        exp(it, m + 2)
                    if following:
                        if u == 1:
                            key(it, j + 1)
                        if u >= 2:
                            value(it, j + 1, u - 2)

                turns(act, step)

            @block.vector
            def _(dve):
                if gated:
                    e, a, b = gates[:, 0:1], gates[:, 1:2], gates[:, 2:3]
                    dve.wait_ge(gate_exp, count(1))
                    nc.vector.tensor_scalar(a, e, 1.0, None, ALU.add).then_inc(gate_step, 1)
                    dve.wait_ge(gate_step, count(1))
                    nc.vector.reciprocal(b, a).then_inc(gate_step, 1)
                    dve.wait_ge(gate_step, count(2))
                    nc.vector.tensor_scalar(a, b, -1.0, 1.0, ALU.mult, ALU.add).then_inc(gate_step, 1)
                    dve.wait_ge(gate_step, count(3))

                def centre(it, m):
                    n = unit(it, m)
                    mx = small[:, 0, m % 4].rearrange("p (r h) -> p r h", r=NQ)
                    dve.wait_ge(s_mm, count(n + 1))
                    if rel is not None:
                        dve.wait_ge(rel_loaded[m % 2], count(it * (16 * NU) + 32 * (m // 2 + 1)))
                        extra = relb[:, m % 2].rearrange("p b (r c) -> p r b c", r=NQ)
                    if score_bias is not None:
                        extra = k.w(score_bias).rearrange("p (r c) -> p r c", r=NQ).unsqueeze(2)\
                            .broadcast_to([128, NQ, 2, 2 * S])
                    if biased_scores:
                        nc.vector.tensor_tensor(by_seq(scores), by_seq(scores), extra, ALU.add).then_inc(biased, 1)
                        dve.wait_ge(biased, count(n + 1))
                    nc.vector.tensor_reduce(mx, by_head(scores), AX.X, ALU.max).then_inc(max_ready, 1)
                    dve.wait_ge(max_ready, count(n + 1))
                    nc.vector.tensor_tensor(prob[:, m % 4].rearrange("p (r h) s -> p r h s", r=NQ), by_head(scores),
                                            mx.unsqueeze(3).broadcast_to([128, NQ, NQ, S]), ALU.subtract).then_inc(s_read, 1)

                def total(it, m):
                    n = unit(it, m)
                    dve.wait_ge(e_ready, count(n + 1))
                    nc.vector.tensor_reduce(small[:, 1, m % 4], prob[:, m % 4], AX.X, ALU.add).then_inc(sum_ready, 1)
                    dve.wait_ge(sum_ready, count(n + 1))
                    nc.vector.reciprocal(small[:, 2, m % 4], small[:, 1, m % 4]).then_inc(r_ready, 1)

                def finish(it, j):
                    i, x = j % ns, k.x[:, bass.ts(group(it, j), GW)]
                    if out_w is None:
                        nc.vector.scalar_tensor_tensor(x, k.bank(1), k.w(sources[0][4]), x, ALU.add, ALU.add)\
                            .then_inc(c_read, 1)
                        return
                    if gated:
                        nc.vector.tensor_scalar(cf[:, i], k.bank(1), k.w(sources[i][4]), gates[:, 1 + i:2 + i],
                                                ALU.add, ALU.mult).then_inc(c_read, 1)
                        if i == 0:
                            return
                        dve.wait_ge(c_read, count(phase(it, j) + 1))
                        nc.vector.tensor_tensor(cf[:, 0], cf[:, 0], cf[:, 1], ALU.add).then_inc(c_ready, 1)
                    else:
                        nc.vector.tensor_copy(cf[:, 0], k.bank(1)).then_inc(c_ready, 1)
                    dve.wait_ge(o_mm, count(group(it, j) + 1))
                    nc.vector.scalar_tensor_tensor(x, k.bank(1), k.w(out_b), x, ALU.add, ALU.add).then_inc(x_done, 1)

                centre(0, 0)
                total(0, 0)
                centre(0, 1)

                def step(it, m, j, u, last):
                    if more(m + 1, last):
                        total(it, m + 1)
                    if more(m + 2, last):
                        centre(it, m + 2)
                    if u == TPG - 1:
                        dve.wait_ge(pv_mm, count(unit(it, m) + 1))
                        finish(it, j)

                turns(dve, step)


def l0_attn(k):
    softmax_attention(k, "l0a", ("l0a_wq", None), [(k.h, "l0a_wk", None, "l0a_wv", None, None)],
                      out_w="l0a_wo", out_b="l0a_bo", score_bias="c_alibi")


def l2_xattn(k):
    softmax_attention(k, "l2x", ("l2x_wq", "l2x_bq"),
                      [(k.h, "l2x_wk", "l2x_bk", "l2x_wv", "l2x_bv", "l2x_gate"),
                       (k.ctx, "l2x_wka", "l2x_bka", "l2x_wva", "l2x_bva", "l2x_gate")],
                      out_w="l2x_wo", out_b="l2x_bo")



def seq(ap, g, t, b2):
    return ap[:, bass.ds(g * GW + (t * 128 + b2 * 64), 64)]


def l0_xattn(k):
    nc = k.nc
    layer_norm(k, k.x, k.h, "l0x_ln")
    with Stage(nc) as st:
        (q_mm, k_mm, v_mm, q_sb, k_sb, v_sb, s_mm, s_ready, e_ready, p_ready, c_mm, x_done, step, mask_loaded, cg_ready) = st.sem(
            "q_mm", "k_mm", "v_mm", "q_sb", "k_sb", "v_sb", "s_mm", "s_ready", "e_ready", "p_ready", "c_mm",
            "x_done", "step", "mask_loaded", "cg_ready")
        q = st.sb("l0x_q", [D, GW])
        kk = st.sb("l0x_k", [D, GW])
        v = st.sb("l0x_v", [128, TPG, D])
        mask = st.sb("l0x_mask", [128, T // 128, S], k.dram["cross_mask"].dtype)
        cg = st.sb("l0x_ctx_group", [D, GW])
        mf = st.sb("l0x_maskf", [128, TPG, S])
        keep = st.sb("l0x_keep", [128, TPG, S])
        sc = st.sb("l0x_scores", [128, TPG, S])
        small = st.sb("l0x_small", [128, 3, TPG])
        scores = k.bank(3, TPG * S).rearrange("p (t q) -> p t q", t=TPG)
        with st.block() as block:
            @block.sync
            def _(sp):
                nc.sync.dma_start(mask[:, :, :], k.dram["cross_mask"]).then_inc(mask_loaded, 16)

            @block.gpsimd
            def _(pool):
                with pool.Fori(0, G) as g:
                    pool.wait_ge(v_mm, count(g))
                    nc.gpsimd.tensor_copy(cg[:, :], k.ctx[:, bass.ts(g, GW)]).then_inc(cg_ready, 1)

            @block.tensor
            def _(pe):
                with pe.Fori(0, G) as g:
                    nc.tensor.matmul(k.bank(0), k.w("l0x_wq"), k.h[:, bass.ts(g, GW)]).then_inc(q_mm, 1)
                    nc.tensor.matmul(k.bank(1), k.w("l0x_wk"), k.ctx[:, bass.ts(g, GW)]).then_inc(k_mm, 1)
                    pe.wait_ge(cg_ready, count(g + 1))
                    for t in range(TPG):
                        m = nc.tensor.matmul(k.bank(2)[:, t * D:(t + 1) * D],
                                             cg[:, t * 128:t * 128 + 128], k.w("l0x_wv"))
                    m.then_inc(v_mm, 1)
                    pe.wait_ge(q_sb, count(g + 1))
                    pe.wait_ge(k_sb, count(g + 1))
                    for t in range(TPG):
                        for b in range(2):
                            c = slice(t * 128 + b * 64, t * 128 + b * 64 + 64)
                            m = nc.tensor.matmul(scores[b * 64:b * 64 + 64, t, :], kk[:, c], q[:, c])
                    m.then_inc(s_mm, 1)
                    pe.wait_ge(v_sb, count(g + 1))
                    pe.wait_ge(p_ready, count(g + 1))
                    pe.wait_ge(x_done, count(g))
                    for t in range(TPG):
                        for b in range(2):
                            r = slice(b * 64, b * 64 + 64)
                            m = nc.tensor.matmul(k.bank(4 + b)[:, t * 64:t * 64 + 64], v[r, t, :], sc[r, t, :])
                    m.then_inc(c_mm, 1)

            @block.scalar
            def _(act):
                with act.Fori(0, G) as g:
                    act.wait_ge(s_mm, count(g))
                    act.wait_ge(q_mm, count(g + 1))
                    nc.scalar.copy(q[:, :], k.bank(0)).then_inc(q_sb, 1)
                    act.wait_ge(k_mm, count(g + 1))
                    nc.scalar.copy(kk[:, :], k.bank(1)).then_inc(k_sb, 1)
                    act.wait_ge(c_mm, count(g))
                    act.wait_ge(v_mm, count(g + 1))
                    nc.scalar.copy(v[:, :, :].rearrange("p t d -> p (t d)"), k.bank(2)).then_inc(v_sb, 1)
                    act.wait_ge(s_ready, count(g + 1))
                    nc.scalar.activation(sc[:, :, :], sc[:, :, :], ACT.Exp).then_inc(e_ready, 1)

            @block.vector
            def _(dve):
                dve.wait_ge(mask_loaded, count(16))
                ch = Chain(dve, step, 7)
                mx, sm, rc = small[:, 0, :], small[:, 1, :], small[:, 2, :]
                wide = lambda a: a.unsqueeze(2).broadcast_to([128, TPG, S])
                with dve.Fori(0, G) as g:
                    ch.turn(g)
                    dve.wait_ge(p_ready, count(g))
                    ch.link(nc.vector.tensor_copy(mf[:, :, :], mask[:, bass.ts(g, TPG), :]))
                    ch.link(nc.vector.tensor_scalar(keep[:, :, :], mf[:, :, :], -1.0, 1.0, ALU.mult, ALU.add))
                    dve.wait_ge(s_mm, count(g + 1))
                    dve.wait_ge(c_mm, count(g))
                    ch.link(nc.vector.scalar_tensor_tensor(sc[:, :, :], scores, float(D) ** -0.5, keep[:, :, :],
                                                           ALU.mult, ALU.mult))
                    ch.link(nc.vector.scalar_tensor_tensor(sc[:, :, :], mf[:, :, :], 1e-9, sc[:, :, :],
                                                           ALU.mult, ALU.add))
                    ch.link(nc.vector.tensor_reduce(mx, sc[:, :, :], AX.X, ALU.max))
                    nc.vector.tensor_tensor(sc[:, :, :], sc[:, :, :], wide(mx), ALU.subtract).then_inc(s_ready, 1)
                    dve.wait_ge(e_ready, count(g + 1))
                    ch.link(nc.vector.tensor_reduce(sm, sc[:, :, :], AX.X, ALU.add))
                    ch.link(nc.vector.reciprocal(rc, sm))
                    nc.vector.tensor_tensor(sc[:, :, :], sc[:, :, :], wide(rc), ALU.mult).then_inc(p_ready, 1)
                    dve.wait_ge(c_mm, count(g + 1))
                    xg = k.x[:, bass.ts(g, GW)].rearrange("p (t b s) -> p b t s", b=2, s=64)
                    for b in range(2):
                        m = nc.vector.tensor_tensor(xg[:, b], xg[:, b],
                                                    k.bank(4 + b, 256).rearrange("p (t s) -> p t s", s=64), ALU.add)
                    m.then_inc(x_done, 1)


def feed_forward(k, tag, func, chunks, target, out_bias=None, gates=None, tail=None, src=None):
    nc, n = k.nc, len(chunks)
    src = k.h if src is None else src
    twice = any(c[2] is not None for c in chunks)
    gated = gates is not None
    with Stage(nc) as st:
        h_mm, rest_mm, acted, multiplied, hidden, out_mm, out_done = st.sem(*[f"{tag}_{s}" for s in (
            "h_mm rest_mm acted multiplied hidden out_mm out_done").split()])
        a = st.sb(tag + "_activated", [D, 2, GW])
        m1 = st.sb(tag + "_multiplied", [D, 2, GW])
        m2 = st.sb(tag + "_hidden", [D, 2, GW])
        def final(c):
            return a if c[2] is None and c[4] is None else (m2 if c[4] is not None else m1)

        with st.block() as block:
            @block.tensor
            def _(pe):
                def first(g, i):
                    w1, b1, w3, w2, sel = chunks[i]
                    hg = src[:, bass.ds(g * GW, GW)]
                    m = nc.tensor.matmul(k.bank(i % 2), w1, hg)
                    m.then_inc(h_mm, 1)
                    if w3 is not None:
                        m = nc.tensor.matmul(k.bank(2 + i % 2), w3, hg)
                    if sel is not None and (i == 0 or chunks[i - 1][4] != sel):
                        m = nc.tensor.matmul(k.bank(4 + sel % 2), gates.sel[:, sel * 128:sel * 128 + 128],
                                             gates.pieces[:, bass.ds(g * GW, GW)])
                    if w3 is not None or sel is not None:
                        m.then_inc(rest_mm, 1)

                def second(g, i):
                    pe.wait_ge(hidden, count(g * n + i + 1))
                    if i == 0:
                        pe.wait_ge(out_done, count(g))
                    m = nc.tensor.matmul(k.bank(6), chunks[i][3], final(chunks[i])[:, i % 2], start=(i == 0),
                                         stop=(i == n - 1 and tail is None))
                    if i == n - 1:
                        if tail is not None:
                            m = nc.tensor.matmul(k.bank(6), tail, gates.plain[:, bass.ts(g, GW)], start=False, stop=True)
                        m.then_inc(out_mm, 1)

                def group(g, last):
                    for i in range(n):
                        if i + 1 < n:
                            first(g, i + 1)
                        elif not last:
                            first(g + 1, 0)
                        second(g, i)

                first(0, 0)
                with pe.Fori(0, G - 1) as g:
                    group(g, False)
                group(G - 1, True)

            @block.scalar
            def _(act):
                nc.scalar.preload_act_table(func)
                with act.Fori(0, G) as g:
                    for i, (w1, b1, w3, w2, sel) in enumerate(chunks):
                        act.wait_ge(h_mm, count(g * n + i + 1))
                        if b1 is None:
                            ins = nc.scalar.activation(a[:, i % 2], k.bank(i % 2), func)
                        else:
                            ins = nc.scalar.activation(a[:, i % 2], k.bank(i % 2), func, bias=b1)
                        ins.then_inc(hidden if final(chunks[i]) is a else acted, 1)

            with_rest = [c[2] is not None or c[4] is not None for c in chunks]
            both = [c[2] is not None and c[4] is not None for c in chunks]

            @block.vector
            def _(dve):
                with dve.Fori(0, G) as g:
                    for i, (w1, b1, w3, w2, sel) in enumerate(chunks):
                        if not with_rest[i]:
                            continue
                        dve.wait_ge(acted, count(g * sum(with_rest) + sum(with_rest[:i]) + 1))
                        dve.wait_ge(rest_mm, count(g * sum(with_rest) + sum(with_rest[:i]) + 1))
                        if w3 is not None:
                            nc.vector.tensor_tensor(m1[:, i % 2], a[:, i % 2], k.bank(2 + i % 2), ALU.mult)\
                                .then_inc(multiplied if both[i] else hidden, 1)
                        if both[i]:
                            dve.wait_ge(multiplied, count(g * sum(both) + sum(both[:i]) + 1))
                        if sel is not None:
                            nc.vector.tensor_tensor(m2[:, i % 2], (m1 if w3 is not None else a)[:, i % 2],
                                                    k.bank(4 + sel % 2), ALU.mult).then_inc(hidden, 1)
                    c = bass.ts(g, GW)
                    dve.wait_ge(out_mm, count(g + 1))
                    if out_bias is not None:
                        nc.vector.scalar_tensor_tensor(target[:, c], k.bank(6), out_bias, target[:, c],
                                                       ALU.add, ALU.add).then_inc(out_done, 1)
                    else:
                        nc.vector.tensor_tensor(target[:, c], target[:, c], k.bank(6), ALU.add).then_inc(out_done, 1)


class Gates:

    def __init__(self, k, tag, E, selectors, stack, plain=False):
        buf = lambda name, shape, dt: stack.enter_context(k.nc.sbuf_tensor(tag + name, shape, dt))
        self.E, self.source = E, k.dram[selectors]
        self.pieces = buf("_gate_pieces", [3 * E, T], BF16)
        self.sel = buf("_selectors", list(self.source.shape), BF16)
        self.plain = buf("_gates", [E, T], F32) if plain else None


def route(k, tag, E, topk, router_w, mode, gates, bias=None):
    nc, NT = k.nc, T // 128
    with Stage(nc) as st:
        logits_mm, exp_in, exp_out, turned, plain_turned, sel_loaded, ident_ready, ready, step = st.sem(
            *[f"{tag}_{s}" for s in ("logits_mm exp_in exp_out turned plain_turned sel_loaded ident_ready ready step").split()])
        lg = k.bank(0, NT * E).rearrange("p (t e) -> p t e", e=E)
        val = st.sb(tag + "_values", [128, NT, E])
        wgt = st.sb(tag + "_weights", [128, NT, E])
        chosen = st.sb(tag + "_chosen", [128, NT, E])
        one = st.sb(tag + "_one", [128, 2, NT])
        marks = st.sb(tag + "_marks", [128, 2, NT, E])
        rest = st.sb(tag + "_rest", [128, 2, NT, E])
        pieces = st.sb(tag + "_pieces", [128, NT, 3, E], BF16)
        ident = st.sb(tag + "_identity", [128, 128], BF16)
        sel = st.sb(tag + "_selectors", list(gates.source.shape))
        if mode == "groups":
            NG, EG = 4, 4
            pair = st.sb(tag + "_pair", [128, NT, NG, 6])
            gs = st.sb(tag + "_group_score", [128, NT, NG])
            gsel = st.sb(tag + "_group_chosen", [128, NT, NG])

        with st.block() as block:
            @block.tensor
            def _(pe):
                for t in range(NT):
                    m = nc.tensor.matmul(lg[:, t, :], k.h[:, t * 128:t * 128 + 128], router_w)
                m.then_inc(logits_mm, 1)
                pe.wait_ge(ident_ready, count(1))
                pe.wait_ge(ready, count(1))
                for t in range(NT):
                    m = nc.tensor.matmul(k.ps[0:3 * E, t * 128:t * 128 + 128],
                                         pieces[:, t].rearrange("p n e -> p (n e)"), ident[:, :])
                    if t % TPG == TPG - 1:
                        m.then_inc(turned, 1)
                if gates.plain is not None:
                    for t in range(NT):
                        if t % TPG == 0:
                            pe.wait_ge(plain_turned, count(t // TPG + 1))
                        m = nc.tensor.transpose(k.ps[0:E, t * 128:t * 128 + 128], wgt[:, t, :], k.w("c_ident"))
                        if t % TPG == TPG - 1:
                            m.then_inc(turned, 1)

            @block.sync
            def _(sp):
                nc.sync.dma_start(sel[:, :], gates.source).then_inc(sel_loaded, 16)

            @block.gpsimd
            def _(pool):
                nc.gpsimd.tensor_copy(ident[:, :], k.w("c_ident")).then_inc(ident_ready, 1)
                pool.wait_ge(sel_loaded, count(16))
                nc.gpsimd.tensor_copy(gates.sel[:, :], sel[:, :])

            @block.scalar
            def _(act):
                act.wait_ge(exp_in, count(1))
                nc.scalar.activation(wgt[:, :, :], wgt[:, :, :], ACT.Exp,
                                     scale=-1.0 if mode == "groups" else 1.0).then_inc(exp_out, 1)
                for g in range(G):
                    act.wait_ge(turned, count(g + 1))
                    nc.scalar.copy(gates.pieces[:, g * GW:g * GW + GW], k.bank(g)[0:3 * E, :]).then_inc(plain_turned, 1)
                if gates.plain is not None:
                    for g in range(G):
                        act.wait_ge(turned, count(G + g + 1))
                        nc.scalar.copy(gates.plain[:, g * GW:g * GW + GW], k.bank(g)[0:E, :])

            @block.vector
            def _(dve):
                ch = Chain(dve, step)
                over = lambda a: a.unsqueeze(2).broadcast_to([128, NT, E])
                mx, rc = one[:, 0], one[:, 1]

                def choose(v, n, topk, out):
                    m0, m1 = marks[:, 0, :, 0:n], marks[:, 1, :, 0:n]
                    wide = lambda a: a.unsqueeze(2).broadcast_to([128, NT, n])
                    for i in range(topk):
                        ch.link(nc.vector.tensor_reduce(mx, v, AX.X, ALU.max))
                        ch.link(nc.vector.tensor_tensor(m0, v, wide(mx), ALU.is_equal))
                        ch.link(nc.vector.tensor_tensor(m0, m0, k.w("c_falling")[:, S - n:S].unsqueeze(1)
                                                        .broadcast_to([128, NT, n]), ALU.mult))
                        ch.link(nc.vector.tensor_reduce(mx, m0, AX.X, ALU.max))
                        pick = out if i == 0 else m1
                        ch.link(nc.vector.tensor_tensor(pick, m0, wide(mx), ALU.is_equal))
                        if i < topk - 1:
                            ch.link(nc.vector.scalar_tensor_tensor(v, pick, LOWEST, v, ALU.mult, ALU.add))
                        if i:
                            ch.link(nc.vector.tensor_tensor(out, out, m1, ALU.add))

                dve.wait_ge(logits_mm, count(1))
                if mode == "groups":
                    nc.vector.tensor_copy(wgt[:, :, :], lg).then_inc(exp_in, 1)
                    dve.wait_ge(exp_out, count(1))
                    ch.link(nc.vector.tensor_scalar(wgt[:, :, :], wgt[:, :, :], 1.0, None, ALU.add))
                    ch.link(nc.vector.reciprocal(wgt[:, :, :], wgt[:, :, :]))
                    ch.link(nc.vector.tensor_tensor(val[:, :, :], wgt[:, :, :], bias.unsqueeze(1)
                                                    .broadcast_to([128, NT, E]), ALU.add))
                    v4 = val[:, :, :].rearrange("p t (g e) -> p t g e", g=NG)
                    pairs = [(a, b) for a in range(EG) for b in range(a + 1, EG)]
                    for i, (a, b) in enumerate(pairs):
                        ins = nc.vector.tensor_tensor(pair[:, :, :, i], v4[:, :, :, a], v4[:, :, :, b], ALU.add)
                    ch.link(ins)
                    ch.link(nc.vector.tensor_reduce(gs[:, :, :], pair[:, :, :, :], AX.X, ALU.max))
                    choose(gs[:, :, :], NG, 2, gsel[:, :, :])
                    ch.link(nc.vector.tensor_scalar(gs[:, :, :], gsel[:, :, :], -1.0, None, ALU.add))
                    gb = gsel[:, :, :].unsqueeze(3).broadcast_to([128, NT, NG, EG])
                    ch.link(nc.vector.tensor_tensor(v4, v4, gb, ALU.mult))
                    ch.link(nc.vector.tensor_tensor(v4, v4, gs[:, :, :].unsqueeze(3).broadcast_to(
                        [128, NT, NG, EG]), ALU.add))
                else:
                    ch.link(nc.vector.tensor_reduce(mx, lg, AX.X, ALU.max))
                    nc.vector.tensor_tensor(wgt[:, :, :], lg, over(mx), ALU.subtract).then_inc(exp_in, 1)
                    if mode == "logits":
                        ch.link(nc.vector.tensor_copy(val[:, :, :], lg))
                    dve.wait_ge(exp_out, count(1))
                    if mode == "probs":
                        ch.link(nc.vector.tensor_reduce(mx, wgt[:, :, :], AX.X, ALU.add))
                        ch.link(nc.vector.reciprocal(rc, mx))
                        ch.link(nc.vector.tensor_tensor(wgt[:, :, :], wgt[:, :, :], over(rc), ALU.mult))
                        ch.link(nc.vector.tensor_copy(val[:, :, :], wgt[:, :, :]))
                choose(val[:, :, :], E, topk, chosen[:, :, :])
                ch.link(nc.vector.tensor_tensor(wgt[:, :, :], wgt[:, :, :], chosen[:, :, :], ALU.mult))
                ch.link(nc.vector.tensor_reduce(mx, wgt[:, :, :], AX.X, ALU.add))
                if mode == "groups":
                    ch.link(nc.vector.tensor_scalar(mx, mx, 1e-20, None, ALU.add))
                ch.link(nc.vector.reciprocal(rc, mx))
                if mode != "probs":
                    ch.link(nc.vector.tensor_scalar(rc, rc, 2.5 if mode == "groups" else 0.5, None, ALU.mult))
                ch.link(nc.vector.tensor_tensor(wgt[:, :, :], wgt[:, :, :], over(rc), ALU.mult))
                ch.link(nc.vector.tensor_copy(pieces[:, :, 0], wgt[:, :, :]))
                ch.link(nc.vector.tensor_tensor(rest[:, 0], wgt[:, :, :], pieces[:, :, 0], ALU.subtract))
                ch.link(nc.vector.tensor_copy(pieces[:, :, 1], rest[:, 0]))
                ch.link(nc.vector.tensor_tensor(rest[:, 1], rest[:, 0], pieces[:, :, 1], ALU.subtract))
                nc.vector.tensor_copy(pieces[:, :, 2], rest[:, 1]).then_inc(ready, 1)


def l0_ffn(k):
    layer_norm(k, k.x, k.h, "l0f_ln")
    feed_forward(k, "l0f", ACT.Relu, [(k.w(f"l0f_w1_{i}"), k.w(f"l0f_b1_{i}"), None, k.w(f"l0f_w2_{i}"), None)
                                      for i in range(4)], k.h, out_bias=k.w("l0f_b2"))
    layer_norm(k, k.h, k.h, "l0f_ln2", gain=k.w("l0f_gamma"), bias=k.w("l0f_beta"), add_to=k.x)


def l1_ffn(k):
    layer_norm(k, k.x, k.h, "l1f_ln")
    with ExitStack() as stack:
        gates = Gates(k, "l1f", 8, "sel_l1", stack, plain=True)
        route(k, "l1f_route", 8, 2, k.w("l1f_gate"), "logits", gates)
        feed_forward(k, "l1f", ACT.Relu, [(k.w(f"l1f_wd_{i}"), k.w(f"l1f_bd_{i}"), None, k.w(f"l1f_wu_{i}"), i)
                                          for i in range(4)], k.x, gates=gates, tail=k.w("l1f_bu"))


def l2_ffn(k):
    layer_norm(k, k.x, k.h, "l2f_ln")
    with ExitStack() as stack:
        gates = Gates(k, "l2f", 8, "sel_l2", stack)
        route(k, "l2f_route", 8, 2, k.w("l2f_gate"), "probs", gates)
        feed_forward(k, "l2f", ACT.Silu, [(k.w(f"l2f_w1_{i}"), None, k.w(f"l2f_w3_{i}"), k.w(f"l2f_w2_{i}"), i // 2)
                                          for i in range(16)], k.x, gates=gates)


def l3_ffn(k):
    layer_norm(k, k.x, k.h, "l3f_ln")
    with ExitStack() as stack:
        gates = Gates(k, "l3f", 16, "sel_l3", stack)
        route(k, "l3f_route", 16, 4, k.w("l3f_router"), "groups", gates, bias=k.w("l3f_bias"))
        chunks = [(k.w(f"l3f_g_{i}"), None, k.w(f"l3f_u_{i}"), k.w(f"l3f_d_{i}"), i) for i in range(16)]
        chunks += [(k.w(f"l3f_sg_{i}"), None, k.w(f"l3f_su_{i}"), k.w(f"l3f_sd_{i}"), None) for i in range(2)]
        feed_forward(k, "l3f", ACT.Silu, chunks, k.x, gates=gates)


def l1_attn(k):
    nc, tag = k.nc, "l1a"
    TURNS = G // 2
    layer_norm(k, k.x, k.h, "l1a_ln")
    with Stage(nc) as st:
        (zeroed, q_mm, k_mm, q_relu, k_relu, q_plus, k_plus, q_spread, k_spread, scanned, dk_ready, den_mm, maxed,
         rd_ready, bias_ready, s_mm, a_ready, staged, v_mm, v_sb, n_mm, c_raw, c_ready, o_mm, x_done) = st.sem(*["l1a_" + n for n in (
             "zeroed q_mm k_mm q_relu k_relu q_plus k_plus q_spread k_spread scanned dk_ready den_mm maxed "
             "rd_ready bias_ready s_mm a_ready staged v_mm v_sb n_mm c_raw c_ready o_mm x_done").split()])
        qr = st.sb("l1a_q_relu", [D, GW])
        kr = st.sb("l1a_k_relu", [D, GW])
        qf = st.sb("l1a_q", [D, GW])
        kf = st.sb("l1a_k", [D, GW])
        kc = st.sb("l1a_k_running_sum", [D, GW])
        dk = st.sb("l1a_q_times_sum", [D, GW])
        rd = st.sb("l1a_one_over_sum", [D, GW])
        cf = st.sb("l1a_context", [D, GW])
        bias = st.sb("l1a_value_bias", [D, GW])
        qe = st.sb("l1a_q_spread", [D, 2, GW // S, 2, S])
        ke = st.sb("l1a_k_spread", [D, 2, GW // S, 2, S])
        twice = st.sb("l1a_source_twice", [D, GW // S, 2, S])
        ve = st.sb("l1a_values_spread", [128, GW // S, 2, D])
        am = st.sb("l1a_weights", [128, 2, H, S])
        scores = k.ps[:, 2 * 512:6 * 512].rearrange("p (r c) -> p r c", r=NQ)[:, :, 0:NQ * S]

        def turns(eng, step):
            with eng.Fori(0, TURNS - 1) as it:
                for m in range(2 * TPG):
                    step(it * 2 + m // TPG, m // TPG, m % TPG, False)
            for m in range(2 * TPG):
                step((TURNS - 1) * 2 + m // TPG, m // TPG, m % TPG, m >= TPG)

        with st.block() as block:
            @block.gpsimd
            def _(pool):
                def stage(g, half):
                    c = bass.ds(g * GW + half * (GW // 2), GW // 2)
                    nc.gpsimd.tensor_copy(twice[:, 4 * half:4 * half + 4], k.h[:, c].rearrange("p (b s) -> p b s", s=S)
                                          .unsqueeze(2).broadcast_to([D, 4, 2, S])).then_inc(staged, 1)

                nc.gpsimd.memset(ve[:, :, :, :], 0.0).then_inc(zeroed, 1)
                stage(0, 0)
                stage(0, 1)

                def step(g, j, u, last):
                    if last:
                        return
                    if u == 1:
                        pool.wait_ge(v_mm, count(g * 2 + 1))
                        stage(g + 1, 0)
                    if u == 2:
                        pool.wait_ge(v_mm, count(g * 2 + 2))
                        stage(g + 1, 1)

                turns(pool, step)

            @block.tensor
            def _(pe):
                def weights(n, g, j, t):
                    if t == 0:
                        pe.wait_ge(k_spread, count(g + 1))
                    pe.wait_ge(a_ready, count(n))
                    for b in range(2):
                        for r in range(NQ):
                            f = slice(32 * r, 32 * r + 32)
                            x = nc.tensor.matmul(scores[:, r, b * 2 * S:(b + 1) * 2 * S],
                                                 ke[f, j, t * 2 + b].rearrange("p h s -> p (h s)"),
                                                 qe[f, j, t * 2 + b].rearrange("p h s -> p (h s)"),
                                                 tile_position=(32 * r, 0))
                    x.then_inc(s_mm, 1)

                def values(n, g, t):
                    if t == 0:
                        pe.wait_ge(v_sb, count(g * 2 + 1))
                        pe.wait_ge(c_ready, count(g))
                    if t == 2:
                        pe.wait_ge(v_sb, count(g * 2 + 2))
                    pe.wait_ge(a_ready, count(n + 1))
                    for b in range(2):
                        for r in range(NQ):
                            f = slice(32 * r, 32 * r + 32)
                            for h in range(2):
                                x = nc.tensor.matmul(
                                    k.bank(1)[f, t * 128 + b * 64:t * 128 + b * 64 + 64],
                                    ve[:, t * 2 + b, h, f], am[:, t % 2, 4 * r + 2 * b + h],
                                    start=(h == 0), stop=(h == 1), tile_position=(0, 32 * r))
                    x.then_inc(n_mm, 1)

                def query(g):
                    nc.tensor.matmul(k.bank(0), k.w("l1a_wq"), k.h[:, bass.ds(g * GW, GW)]).then_inc(q_mm, 1)

                def key(g):
                    nc.tensor.matmul(k.bank(7), k.w("l1a_wk"), k.h[:, bass.ds(g * GW, GW)]).then_inc(k_mm, 1)

                def value(g, half):
                    pe.wait_ge(k_relu if half else q_relu, count(g + 1))
                    pe.wait_ge(staged, count(g * 2 + (half + 1)))
                    for b in range(4):
                        x = nc.tensor.matmul(k.bank(7 if half else 0)[:, b * D:b * D + D],
                                             twice[:, 4 * half + b].rearrange("p c s -> p (c s)"), k.w("l1a_wv"))
                    x.then_inc(v_mm, 1)

                query(0)
                key(0)
                value(0, 0)
                value(0, 1)
                weights(0, 0, 0, 0)

                def step(g, j, u, last):
                    n = g * TPG + u
                    if not (last and u == TPG - 1):
                        weights(n + 1, g + (u + 1) // TPG, (j + (u + 1) // TPG) % 2, (u + 1) % TPG)
                    if u == 0:
                        pe.wait_ge(x_done, count(g))
                        pe.wait_ge(dk_ready, count(g + 1))
                        nc.tensor.matmul(k.bank(6), k.w("c_heads"), dk[:, :]).then_inc(den_mm, 1)
                    values(n, g, u)
                    if not last:
                        if u == 0:
                            query(g + 1)
                        if u == 1:
                            pe.wait_ge(v_sb, count(g * 2 + 2))
                            key(g + 1)
                        if u >= 2:
                            value(g + 1, u - 2)
                    if u == TPG - 1:
                        pe.wait_ge(c_ready, count(g + 1))
                        nc.tensor.matmul(k.bank(6), k.w("l1a_wo"), cf[:, :]).then_inc(o_mm, 1)

                turns(pe, step)

            @block.scalar
            def _(act):
                def query(g, j):
                    act.wait_ge(q_mm, count(g + 1))
                    nc.scalar.activation(qr[:, :], k.bank(0), ACT.Relu, bias=k.w("l1a_bq")).then_inc(q_relu, 1)
                    act.wait_ge(q_plus, count(g + 1))
                    spread(qe[:, j], qf, k.w("c_by_h")).then_inc(q_spread, 1)

                def key(g, j):
                    act.wait_ge(k_mm, count(g + 1))
                    nc.scalar.activation(kr[:, :], k.bank(7), ACT.Relu, bias=k.w("l1a_bk")).then_inc(k_relu, 1)
                    act.wait_ge(k_plus, count(g + 1))
                    spread(ke[:, j], kf, k.w("c_by_p")).then_inc(k_spread, 1)

                def spread(out, f, mask):
                    for i in range(2):
                        x = nc.scalar.mul(out[:, :, i], f[:, :].rearrange("p (b s) -> p b s", s=S), mask[:, i:i + 1])
                    return x

                def value(g, half):
                    act.wait_ge(v_mm, count(g * 2 + (half + 1)))
                    for p in range(2):
                        rows = slice(64 * p, 64 * p + 64)
                        for h in range(2):
                            f = lambda a: a.rearrange("p b (r n e) -> p b r n e", r=NQ, n=NQ)[:, :, :, 2 * p + h]
                            x = nc.scalar.copy(f(ve[rows, 4 * half:4 * half + 4, h]),
                                               f(k.bank(7 if half else 0)[rows].rearrange("p (b d) -> p b d", d=D)))
                    x.then_inc(v_sb, 1)

                query(0, 0)
                key(0, 0)
                act.wait_ge(zeroed, count(1))
                value(0, 0)
                value(0, 1)

                def step(g, j, u, last):
                    if not last:
                        if u == 0:
                            query(g + 1, (j + 1) % 2)
                        if u == 1:
                            key(g + 1, (j + 1) % 2)
                        if u >= 2:
                            value(g + 1, u - 2)

                turns(act, step)

            @block.vector
            def _(dve):
                causal = k.w("c_causal").unsqueeze(1).unsqueeze(1).broadcast_to([128, NQ, NQ, S])

                def mask(n, t):
                    dve.wait_ge(s_mm, count(n + 1))
                    nc.vector.tensor_tensor(am[:, t % 2].rearrange("p (r h) s -> p r h s", r=NQ),
                                            scores.rearrange("p r (h s) -> p r h s", s=S), causal,
                                            ALU.mult).then_inc(a_ready, 1)

                def query_plus(g):
                    dve.wait_ge(q_relu, count(g + 1))
                    nc.vector.tensor_scalar(qf[:, :], qr[:, :], 1e-6, None, ALU.add).then_inc(q_plus, 1)

                def key_plus(g):
                    dve.wait_ge(k_relu, count(g + 1))
                    nc.vector.tensor_scalar(kf[:, :], kr[:, :], 1e-6, None, ALU.add).then_inc(k_plus, 1)

                def running_sum(g):
                    dve.wait_ge(k_plus, count(g + 1))
                    nc.vector.tensor_tensor_scan(kc[:, :], k.w("c_restart"), kf[:, :], 0.0, ALU.mult, ALU.add)\
                        .then_inc(scanned, 1)
                    dve.wait_ge(scanned, count(g + 1))
                    nc.vector.tensor_tensor(dk[:, :], qf[:, :], kc[:, :], ALU.mult).then_inc(dk_ready, 1)

                query_plus(0)
                key_plus(0)
                running_sum(0)
                mask(0, 0)

                def step(g, j, u, last):
                    n = g * TPG + u
                    if u == 1 and not last:
                        dve.wait_ge(k_spread, count(g + 1))
                        query_plus(g + 1)
                    if u == 2 and not last:
                        key_plus(g + 1)
                    if not (last and u == TPG - 1):
                        mask(n + 1, (u + 1) % TPG)
                    if u == 0:
                        dve.wait_ge(den_mm, count(g + 1))
                        nc.vector.tensor_scalar(rd[:, :], k.bank(6), 1e-6, None, ALU.max).then_inc(maxed, 1)
                        dve.wait_ge(maxed, count(g + 1))
                        nc.vector.reciprocal(rd[:, :], rd[:, :]).then_inc(rd_ready, 1)
                        dve.wait_ge(rd_ready, count(g + 1))
                        nc.vector.scalar_tensor_tensor(bias[:, :], k.bank(6), k.w("l1a_bv"), rd[:, :],
                                                       ALU.mult, ALU.mult).then_inc(bias_ready, 1)
                    if u == 2 and not last:
                        running_sum(g + 1)
                    if u == TPG - 1:
                        dve.wait_ge(bias_ready, count(g + 1))
                        dve.wait_ge(n_mm, count(n + 1))
                        nc.vector.tensor_tensor(cf[:, :], k.bank(1), rd[:, :], ALU.mult).then_inc(c_raw, 1)
                        dve.wait_ge(c_raw, count(g + 1))
                        nc.vector.tensor_tensor(cf[:, :], cf[:, :], bias[:, :], ALU.add).then_inc(c_ready, 1)
                        dve.wait_ge(o_mm, count(g + 1))
                        xc = k.x[:, bass.ds(g * GW, GW)]
                        nc.vector.scalar_tensor_tensor(xc, k.bank(6), k.w("l1a_bo"), xc, ALU.add, ALU.add)\
                            .then_inc(x_done, 1)

                turns(dve, step)


def l1_xattn(k):
    nc = k.nc
    rel = nc.dram_tensor("relative_scores", (T, H * S), F32, kind="Internal").ap()
    rel_rows = rel.rearrange("(b s) n -> s b n", s=S)
    layer_norm(k, k.x, k.h, "l1x_ln")
    R = 2 * S - 1
    PAIRS = S // 2
    with Stage(nc) as st:
        q_mm, q_ready, table_loaded, mask_loaded, mask_scaled = st.sem(
            "l1r_q_mm", "l1r_q_ready", "l1r_table_loaded", "l1r_mask_loaded", "l1r_mask_scaled")
        staged = st.sem("l1r_staged0", "l1r_staged1")
        r_mm = st.sem("l1r_mm0", "l1r_mm1")
        rows_ready = st.sem("l1r_rows0", "l1r_rows1")
        stored = st.sem("l1r_stored0", "l1r_stored1")
        qf = st.sb("l1r_q", [D, T])
        table = st.sb("l1r_table", [D, H, R])
        qs = st.sb("l1r_q_positions", [D, 2, 2, B])
        rs = st.sb("l1r_rows", [2 * B, 2, H * S])
        mask = st.sb("l1r_mask", [2 * B, S])
        with st.block() as block:
            @block.sync
            def _(sp):
                nc.sync.dma_start(table[:, :, :].rearrange("p h r -> p (h r)"), k.dram["rel_in"]).then_inc(table_loaded, 16)
                for i in range(2):
                    nc.sync.dma_start(mask[i * B:(i + 1) * B, :], k.dram["mask_in"]).then_inc(mask_loaded, 16)
                with sp.Fori(0, PAIRS // 2) as i:
                    for p in range(2):
                        for pos in range(2):
                            sp.wait_ge(rows_ready[p], count(i + 1))
                            nc.sync.dma_start(rel_rows[bass.ds(i * 4 + (2 * p + pos), 1)].rearrange("s b n -> (s b) n"),
                                              rs[pos * B:(pos + 1) * B, p]).then_inc(stored[p], 16)
                for p in range(2):
                    sp.wait_ge(stored[p], count(16 * PAIRS))

            @block.gpsimd
            def _(pool):
                pool.wait_ge(q_ready, count(G))
                q3 = qf[:, :].rearrange("p (b s) -> p s b", s=S)
                with pool.Fori(0, PAIRS // 2) as i:
                    for p in range(2):
                        pool.wait_ge(r_mm[p], count(i))
                        nc.gpsimd.tensor_copy(qs[:, p], q3[:, bass.ds(i * 4 + 2 * p, 2), :]).then_inc(staged[p], 1)

            @block.tensor
            def _(pe):
                for g in range(G):
                    nc.tensor.matmul(k.bank(g), k.w("l1x_wq"), k.h[:, g * GW:g * GW + GW]).then_inc(q_mm, 1)
                pe.wait_ge(q_ready, count(G))
                pe.wait_ge(table_loaded, count(16))
                for i in range(PAIRS // 2):
                    for p in range(2):
                        pe.wait_ge(staged[p], count(i + 1))
                        pe.wait_ge(rows_ready[p], count(i))
                        for half in range(2):
                            for pos in range(2):
                                first = S - 1 - (4 * i + 2 * p + pos)
                                m = nc.tensor.matmul(k.bank(2 * p + half)[pos * B:(pos + 1) * B, :], qs[:, p, pos],
                                                     table[:, 8 * half:8 * half + 8, first:first + S],
                                                     tile_position=(0, 64 * pos))
                        m.then_inc(r_mm[p], 1)

            @block.vector
            def _(dve):
                for g in range(G):
                    dve.wait_ge(q_mm, count(g + 1))
                    nc.vector.tensor_scalar(qf[:, g * GW:g * GW + GW], k.bank(g), k.w("l1x_bq"), None, ALU.add)\
                        .then_inc(q_ready, 1)
                dve.wait_ge(mask_loaded, count(32))
                nc.vector.tensor_scalar(mask[:, :], mask[:, :], float(DH) ** 0.5, None, ALU.mult).then_inc(mask_scaled, 1)
                dve.wait_ge(mask_scaled, count(1))
                with dve.Fori(0, PAIRS // 2) as i:
                    for p in range(2):
                        dve.wait_ge(stored[p], count(i * 32))
                        dve.wait_ge(r_mm[p], count(i + 1))
                        nc.vector.tensor_tensor(rs[:, p].rearrange("b (h s) -> b h s", s=S),
                                                k.ps[:, 2 * p * 512:(2 * p + 2) * 512].rearrange("b (h s) -> b h s", s=S),
                                                mask[:, :].unsqueeze(1).broadcast_to([2 * B, H, S]), ALU.add)\
                            .then_inc(rows_ready[p], 1)
    softmax_attention(k, "l1x", ("l1x_wq", "l1x_bq"), [(k.ctx, "l1x_wk", "l1x_bk", "l1x_wv", "l1x_bv", None)],
                      rel=rel, normed=True)


def l2_attn(k):
    nc = k.nc
    SIGMA, MU = 0.282095, 0.707107
    layer_norm(k, k.x, k.h, "l2a_ln")
    with ExitStack() as outer:
        xn = outer.enter_context(nc.sbuf_tensor("l2a_xn", [D, T], F32))
        mx = outer.enter_context(nc.sbuf_tensor("l2a_averaged", [D, T], F32))
        bias = outer.enter_context(nc.sbuf_tensor("l2a_bias", [128, S], F32))
        hb = outer.enter_context(nc.sbuf_tensor("l2a_hx_bias", [D, 2], F32))
        layer_norm(k, k.h, xn, "l2a_ln2", gain=k.w("l2a_ln_w"), bias=k.w("l2a_ln_b"))
        with Stage(nc) as st:
            step, act_step, bias_in, bias_mm, kern_in, kern_ready, tap, dve_averaged, pe_averaged, diag_ready, diag_used \
                = st.sem(*["l2e_" + n for n in ("step act_step bias_in bias_mm kern_in kern_ready tap dve_averaged "
                                                "pe_averaged diag_ready diag_used").split()])
            N = 16
            sm = st.sb("l2e_small", [D, 4, N])
            pw = st.sb("l2e_powers", [D, N, S])
            kern = st.sb("l2e_kernel", [D, S])
            rot = st.sb("l2e_rotary", [D, 3, 128])
            p_, a_, lq, cf = (sm[:, i] for i in range(4))
            DIAGS = 4
            diag = st.sb("l2e_diagonals", [D, DIAGS, D])
            PE_BANKS = (7, 6)
            DVE_PARTS = ((0, 6 * GW),)
            with st.block() as block:
                @block.scalar
                def _(act):
                    act.wait_ge(kern_in, count(1))
                    nc.scalar.preload_act_table_set("natural_log_exp_and_others")
                    nc.scalar.activation(sm[:, 0:2], k.w("l2a_delta_alpha").rearrange("p (a n) -> p a n", a=2),
                                         ACT.Exp, scale=-1.0).then_inc(act_step, 1)
                    act.wait_ge(kern_in, count(2))
                    nc.scalar.activation(lq, lq, ACT.Ln).then_inc(act_step, 1)
                    act.wait_ge(kern_in, count(3))
                    nc.scalar.activation(pw[:, :, :], pw[:, :, :], ACT.Exp).then_inc(act_step, 1)
                    act.wait_ge(kern_ready, count(1))
                    for j in range(S):
                        if j >= DIAGS:
                            act.wait_ge(diag_used, count(j - DIAGS + 1))
                        nc.scalar.mul(diag[:, j % DIAGS], k.w("c_ident"), kern[:, j:j + 1]).then_inc(diag_ready, 1)
                    act.wait_ge(dve_averaged, count(len(DVE_PARTS)))
                    act.wait_ge(pe_averaged, count(1))
                    for g in range(G):
                        nc.scalar.activation(mx[:, g * GW:g * GW + GW], k.bank(g), ACT.Silu)

                @block.tensor
                def _(pe):
                    pe.wait_ge(bias_in, count(1))
                    nc.tensor.matmul(k.bank(7, S), rot[:, 2], rot[:, 0, 0:S]).then_inc(bias_mm, 1)
                    for j in range(S):
                        pe.wait_ge(diag_ready, count(j + 1))
                        for g in PE_BANKS:
                            first = max(g * GW, j * S)
                            if first < (g + 1) * GW:
                                m = nc.tensor.matmul(k.ps[:, first:(g + 1) * GW], diag[:, j % DIAGS],
                                                     xn[:, first - j * S:(g + 1) * GW - j * S],
                                                     start=(j == 0), stop=(j * S >= g * GW + GW - S))
                        m.then_inc(diag_used if j < S - 1 else pe_averaged, 1)

                @block.vector
                def _(dve):
                    ch = Chain(dve, step)
                    nc.vector.tensor_scalar(hb[:, 1:2], k.w("l2a_bmx0"), 0.5, None, ALU.mult)
                    nc.vector.tensor_tensor(hb[:, 0:1], k.w("l2a_bmx4"), k.w("l2a_bh"), ALU.add).then_inc(kern_in, 1)
                    for i, (a, s) in enumerate((("l2a_ra", "l2a_ras"), ("l2a_rb", "l2a_rbs"))):
                        ch.link(nc.vector.tensor_scalar(rot[:, 1, :], k.w("c_sin"), k.w(s), None, ALU.mult))
                        m = nc.vector.scalar_tensor_tensor(rot[:, 2 * i, :], k.w("c_cos"), k.w(a), rot[:, 1, :],
                                                           ALU.mult, ALU.add)
                        if i == 0:
                            ch.link(m)
                    m.then_inc(bias_in, 1)
                    dve.wait_ge(act_step, count(1))
                    ch.link(nc.vector.tensor_scalar(sm[:, 0:2], sm[:, 0:2], 1.0, None, ALU.add))
                    ch.link(nc.vector.reciprocal(sm[:, 0:2], sm[:, 0:2]))
                    ch.link(nc.vector.tensor_tensor(lq, p_, a_, ALU.mult))
                    nc.vector.tensor_scalar(lq, lq, -1.0, 1.0, ALU.mult, ALU.add).then_inc(kern_in, 1)
                    dve.wait_ge(bias_mm, count(1))
                    ch.link(nc.vector.tensor_scalar(bias[:, :], k.bank(7, S), -MU, 1.0 / SIGMA, ALU.add, ALU.mult))
                    ch.link(nc.vector.tensor_tensor(cf, p_, k.w("l2a_beta"), ALU.mult))
                    ch.link(nc.vector.scalar_tensor_tensor(cf, k.w("l2a_gamma"), float(N) ** -0.5, cf, ALU.mult, ALU.mult))
                    dve.wait_ge(act_step, count(2))
                    nc.vector.tensor_tensor(pw[:, :, :], lq.unsqueeze(2).broadcast_to([D, N, S]),
                                            k.w("c_pos").unsqueeze(1).broadcast_to([D, N, S]), ALU.mult)\
                        .then_inc(kern_in, 1)
                    dve.wait_ge(act_step, count(3))
                    ch.link(nc.vector.tensor_tensor(pw[:, :, :], pw[:, :, :], cf.unsqueeze(2).broadcast_to([D, N, S]),
                                                    ALU.mult))
                    ch.link(nc.vector.tensor_reduce(kern[:, :], pw[:, :, :].rearrange("p n s -> p s n"), AX.X, ALU.add))
                    nc.vector.tensor_tensor(kern[:, 0:1], kern[:, 0:1], k.w("l2a_omega"), ALU.add).then_inc(kern_ready, 1)
                    dve.wait_ge(kern_ready, count(1))
                    for i, (start, end) in enumerate(DVE_PARTS):
                        for j in range(end // S):
                            c = max(start, j * S)
                            o, src = k.ps[:, c:end], xn[:, c - j * S:end - j * S]
                            if j == 0:
                                ch.link(nc.vector.tensor_scalar(o, src, kern[:, 0:1], None, ALU.mult))
                            else:
                                m = nc.vector.scalar_tensor_tensor(o, src, kern[:, j:j + 1], o, ALU.mult, ALU.add)
                                if j < end // S - 1:
                                    ch.link(m)
                        m.then_inc(dve_averaged, 1)
        with Stage(nc) as st:
            (staged, v_mm, v_sb, uz_mm, r_mm, uz_sb, r_sb, qk_ready, s_mm, shifted, at_zero, t_ready, inverted, g_ready,
             a_ready, gate_ready, h_mm, r_ready, o_mm, o_sb, less, gated, summed, x_done) = st.sem(*["l2a_" + n for n in (
                 "staged v_mm v_sb uz_mm r_mm uz_sb r_sb qk_ready s_mm shifted at_zero t_ready inverted g_ready "
                 "a_ready gate_ready h_mm r_ready o_mm o_sb less gated summed x_done").split()])
            xg = st.sb("l2a_xn_group", [D, GW // S, S])
            vs = st.sb("l2a_values", [128, TPG, 2 * D])
            uz = st.sb("l2a_u_z", [D, 2, GW])
            rg = st.sb("l2a_r", [D, 2, GW])
            ug = st.sb("l2a_update_gate", [D, GW])
            qk = st.sb("l2a_qk", [D, 2, GW])
            tt = st.sb("l2a_t", [128, 4, TPG, S])
            hr = st.sb("l2a_hr", [D, 2, GW])
            hh = st.sb("l2a_h_new", [D, GW])
            mg = lambda g: mx[:, :].rearrange("p (l s) -> p s l", s=S)[:, bass.ds(g * (GW // S), GW // S), :]
            of_group = lambda a, g: a[:, :].rearrange("p (l s) -> p s l", s=S)[:, bass.ds(g * (GW // S), GW // S), :]

            def turns(eng, step):
                with eng.Fori(0, G - 1) as g:
                    step(g, False)
                step(G - 1, True)

            with st.block() as block:
                @block.gpsimd
                def _(pool):
                    nc.gpsimd.tensor_copy(xg[:, :, :], of_group(xn, 0)).then_inc(staged, 1)
                    with pool.Fori(1, G) as g:
                        pool.wait_ge(v_mm, count(g))
                        nc.gpsimd.tensor_copy(xg[:, :, :], of_group(xn, g)).then_inc(staged, 1)

                @block.tensor
                def _(pe):
                    def values(g):
                        pe.wait_ge(staged, count(g + 1))
                        pe.wait_ge(v_sb, count(g))
                        for t in range(TPG):
                            o = k.bank(t // 2)[:, t % 2 * 256:t % 2 * 256 + 256]
                            nc.tensor.matmul(o, xg[:, 2 * t:2 * t + 2].rearrange("p a b -> p (a b)"), k.w("l2a_wv"),
                                             start=True, stop=False)
                            m = nc.tensor.matmul(o, k.w("c_ones_row"), k.w("l2a_bv"), start=False, stop=True)
                        m.then_inc(v_mm, 1)

                    def update_and_z(g):
                        pe.wait_ge(uz_sb, count(2 * g))
                        for i in range(2):
                            nc.tensor.matmul(k.bank(4 + i), k.w(f"l2a_wmx{i}"), mg(g)).then_inc(uz_mm, 1)

                    def reset(g):
                        for i in range(2):
                            nc.tensor.matmul(k.bank(2 + i), k.w(f"l2a_wmx{2 + i}"), mg(g)).then_inc(r_mm, 1)

                    values(0)
                    update_and_z(0)
                    reset(0)

                    def step(g, last):
                        pe.wait_ge(qk_ready, count(g + 1))
                        for t in range(TPG):
                            for b in range(2):
                                c = slice(t * 128 + b * 64, t * 128 + b * 64 + 64)
                                m = nc.tensor.matmul(k.bank(6)[b * 64:b * 64 + 64, t * S:t * S + S], qk[:, 1, c], qk[:, 0, c])
                        m.then_inc(s_mm, 1)
                        if not last:
                            values(g + 1)
                        pe.wait_ge(o_sb, count(g))
                        nc.tensor.matmul(k.bank(7), k.w("l2a_wmx4"), mg(g), start=True, stop=False)
                        pe.wait_ge(v_sb, count(g + 1))
                        pe.wait_ge(r_sb, count(2 * g + 2))
                        pe.wait_ge(a_ready, count(g + 1))
                        for t in range(TPG):
                            for b in range(2):
                                rows = slice(b * 64, b * 64 + 64)
                                for c in range(2):
                                    m = nc.tensor.matmul(k.bank(2 + b)[:, c * 256 + t * S:c * 256 + t * S + S],
                                                         vs[rows, t, c * D:c * D + D], tt[rows, 3, t])
                        m.then_inc(h_mm, 1)
                        if not last:
                            update_and_z(g + 1)
                        pe.wait_ge(r_ready, count(g + 1))
                        nc.tensor.matmul(k.bank(7), k.w("l2a_wh0"), hr[:, 0], start=False, stop=False)
                        nc.tensor.matmul(k.bank(7), k.w("l2a_wh1"), hr[:, 1], start=False, stop=True).then_inc(o_mm, 1)
                        if not last:
                            reset(g + 1)

                    turns(pe, step)

                @block.scalar
                def _(act):
                    def values(g):
                        act.wait_ge(v_mm, count(g + 1))
                        nc.scalar.activation(vs[:, :, :].rearrange("p t d -> p (t d)"), k.ps[:, 0:1024], ACT.Silu)\
                            .then_inc(v_sb, 1)

                    def update_and_z(g):
                        act.wait_ge(uz_mm, count(2 * g + 1))
                        nc.scalar.activation(uz[:, 0], k.bank(4), ACT.Tanh, bias=hb[:, 1:2], scale=0.5).then_inc(uz_sb, 1)
                        act.wait_ge(uz_mm, count(2 * g + 2))
                        nc.scalar.activation(uz[:, 1], k.bank(5), ACT.Silu, bias=k.w("l2a_bmx1")).then_inc(uz_sb, 1)

                    def reset(g):
                        for i in range(2):
                            act.wait_ge(r_mm, count(2 * g + (i + 1)))
                            nc.scalar.activation(rg[:, i], k.bank(2 + i), ACT.Silu, bias=k.w(f"l2a_bmx{2 + i}"))\
                                .then_inc(r_sb, 1)

                    nc.scalar.preload_act_table(ACT.Silu)
                    values(0)
                    update_and_z(0)
                    reset(0)

                    def step(g, last):
                        act.wait_ge(t_ready, count(g + 1))
                        nc.scalar.activation(tt[:, 2], tt[:, 0], ACT.Gelu).then_inc(g_ready, 1)
                        act.wait_ge(h_mm, count(g + 1))
                        if not last:
                            values(g + 1)
                            act.wait_ge(gate_ready, count(g + 1))
                            update_and_z(g + 1)
                        act.wait_ge(summed, count(g))
                        act.wait_ge(o_mm, count(g + 1))
                        nc.scalar.activation(hh[:, :], k.bank(7), ACT.Silu, bias=hb[:, 0:1]).then_inc(o_sb, 1)
                        if not last:
                            reset(g + 1)

                    turns(act, step)

                @block.vector
                def _(dve):
                    def queries_keys(g):
                        dve.wait_ge(uz_sb, count(2 * g + 2))
                        for i in range(2):
                            m = nc.vector.tensor_scalar(qk[:, i], uz[:, 1], k.w("l2a_qg")[:, i:i + 1],
                                                        k.w("l2a_qb")[:, i:i + 1], ALU.mult, ALU.add)
                        m.then_inc(qk_ready, 1)

                    queries_keys(0)
                    t0, eq, ge, at = (tt[:, i] for i in range(4))

                    def step(g, last):
                        dve.wait_ge(s_mm, count(g + 1))
                        nc.vector.scalar_tensor_tensor(
                            t0, k.bank(6, TPG * S).rearrange("p (t s) -> p t s", s=S), 1.0 / (S * SIGMA),
                            bias[:, :].unsqueeze(1).broadcast_to([128, TPG, S]), ALU.mult, ALU.add).then_inc(shifted, 1)
                        dve.wait_ge(shifted, count(g + 1))
                        nc.vector.tensor_scalar(eq, t0, 0.0, 1e-20, ALU.is_equal, ALU.mult).then_inc(at_zero, 1)
                        dve.wait_ge(at_zero, count(g + 1))
                        nc.vector.tensor_tensor(t0, t0, eq, ALU.add).then_inc(t_ready, 1)
                        dve.wait_ge(t_ready, count(g + 1))
                        nc.vector.reciprocal(eq, t0).then_inc(inverted, 1)
                        dve.wait_ge(inverted, count(g + 1))
                        dve.wait_ge(g_ready, count(g + 1))
                        nc.vector.tensor_tensor(at, ge, eq, ALU.mult).then_inc(a_ready, 1)
                        nc.vector.tensor_scalar(ug[:, :], uz[:, 0], 0.5, 0.5, ALU.mult, ALU.add).then_inc(gate_ready, 1)
                        dve.wait_ge(h_mm, count(g + 1))
                        for b in range(2):
                            for c in range(2):
                                v = lambda a: a.rearrange("p (t b s) -> p b t s", b=2, s=S)[:, b]
                                m = nc.vector.tensor_tensor(v(hr[:, c]), k.bank(2 + b)[:, c * 256:c * 256 + 256].rearrange(
                                    "p (t s) -> p t s", s=S), v(rg[:, c]), ALU.mult)
                        m.then_inc(r_ready, 1)
                        if not last:
                            queries_keys(g + 1)
                        w = lambda a: a.rearrange("p (s l) -> p s l", l=S)
                        dve.wait_ge(gate_ready, count(g + 1))
                        dve.wait_ge(o_sb, count(g + 1))
                        nc.vector.tensor_tensor(w(hh[:, :]), w(hh[:, :]), of_group(k.h, g), ALU.subtract).then_inc(less, 1)
                        dve.wait_ge(less, count(g + 1))
                        nc.vector.tensor_tensor(hh[:, :], hh[:, :], ug[:, :], ALU.mult).then_inc(gated, 1)
                        dve.wait_ge(gated, count(g + 1))
                        nc.vector.tensor_tensor(w(hh[:, :]), w(hh[:, :]), of_group(k.h, g), ALU.add).then_inc(summed, 1)
                        dve.wait_ge(summed, count(g + 1))
                        nc.vector.tensor_tensor(of_group(k.x, g), of_group(k.x, g), w(hh[:, :]), ALU.add).then_inc(x_done, 1)

                    turns(dve, step)


def l3_attn(k):
    nc = k.nc
    layer_norm(k, k.x, k.h, "l3a_ln")
    with nc.sbuf_tensor("l3a_normed", [D, T], F32) as n:
        layer_norm(k, k.h, n, "l3a_ln1", gain=k.w("l3a_g1"), bias=k.w("l3a_b1"))
        with Stage(nc) as st:
            (staged, q_mm, kv_mm, low, exped, qf_ready, kf_ready, v_sb, ksum_mm, masked, num_mm, c_ready, o_mm, h_done,
             step, ones_set) = st.sem(*["l3a_" + s for s in (
                 "staged q_mm kv_mm low exped qf_ready kf_ready v_sb ksum_mm masked num_mm c_ready o_mm h_done step "
                 "ones_set").split()])
            ng = st.sb("l3a_n_group", [D, GW])
            lo = st.sb("l3a_low", [128, 2, GW])
            qf = st.sb("l3a_q", [D, GW])
            kf = st.sb("l3a_k", [128, TPG, D])
            vv = st.sb("l3a_v_ones", [128, TPG, 2, D])
            kvm = st.sb("l3a_kv_masked", [D, 2, TPG, 2, D])
            rd = st.sb("l3a_den", [D, GW])
            cf = st.sb("l3a_context", [D, GW])
            kvb = k.ps[:, 512:1536].rearrange("p (t a d) -> p t a d", t=TPG, a=2)
            with st.block() as block:
                @block.gpsimd
                def _(pool):
                    nc.gpsimd.memset(vv[:, :, 1], 1.0).then_inc(ones_set, 1)
                    with pool.Fori(0, G) as g:
                        pool.wait_ge(kv_mm, count(g))
                        nc.gpsimd.tensor_copy(ng[:, :], n[:, bass.ts(g, GW)]).then_inc(staged, 1)

                @block.tensor
                def _(pe):
                    pe.wait_ge(ones_set, count(1))
                    with pe.Fori(0, G) as g:
                        nc.tensor.matmul(k.bank(0), k.w("l3a_wq"), n[:, bass.ts(g, GW)]).then_inc(q_mm, 1)
                        pe.wait_ge(staged, count(g + 1))
                        pe.wait_ge(h_done, count(g))
                        for t in range(TPG):
                            m = nc.tensor.matmul(k.bank(1 + t // 2)[:, t % 2 * 256:t % 2 * 256 + 256],
                                                 ng[:, t * 128:t * 128 + 128], k.w("l3a_wkv"))
                        m.then_inc(kv_mm, 1)
                        pe.wait_ge(kf_ready, count(g + 1))
                        pe.wait_ge(v_sb, count(g + 1))
                        for t in range(TPG):
                            for b in range(2):
                                rows = slice(b * 64, b * 64 + 64)
                                m = nc.tensor.matmul(k.bank(3 + 2 * b + t // 2)[:, t % 2 * 256:t % 2 * 256 + 256],
                                                     kf[rows, t], vv[rows, t].rearrange("p a d -> p (a d)"))
                        m.then_inc(ksum_mm, 1)
                        pe.wait_ge(masked, count(g + 1))
                        pe.wait_ge(qf_ready, count(g + 1))
                        for a, bank in ((1, 0), (0, 7)):
                            for t in range(TPG):
                                for b in range(2):
                                    c = slice(t * 128 + b * 64, t * 128 + b * 64 + 64)
                                    m = nc.tensor.matmul(k.bank(bank)[:, c], kvm[:, b, t, a], qf[:, c])
                            m.then_inc(num_mm, 1)
                        pe.wait_ge(c_ready, count(g + 1))
                        nc.tensor.matmul(k.bank(1), k.w("l3a_wo"), cf[:, :]).then_inc(o_mm, 1)

                @block.scalar
                def _(act):
                    nc.scalar.preload_act_table(ACT.Exp)
                    with act.Fori(0, G) as g:
                        act.wait_ge(low, count(2 * g + 1))
                        nc.scalar.activation(lo[:, 0], lo[:, 0], ACT.Exp).then_inc(exped, 1)
                        act.wait_ge(low, count(2 * g + 2))
                        nc.scalar.activation(lo[:, 1], lo[:, 1], ACT.Exp).then_inc(exped, 1)
                        act.wait_ge(kf_ready, count(g + 1))
                        nc.scalar.copy(vv[:, :, 0], kvb[:, :, 1]).then_inc(v_sb, 1)

                @block.vector
                def _(dve):
                    ch = Chain(dve, step, 2)
                    with dve.Fori(0, G) as g:
                        ch.turn(g)
                        l3 = lo[:, 1].rearrange("p (t d) -> p t d", d=D)
                        dve.wait_ge(q_mm, count(g + 1))
                        nc.vector.tensor_scalar(lo[:, 0], k.bank(0), 0.0, None, ALU.min).then_inc(low, 1)
                        dve.wait_ge(kv_mm, count(g + 1))
                        nc.vector.tensor_scalar(l3, kvb[:, :, 0], 0.0, None, ALU.min).then_inc(low, 1)
                        dve.wait_ge(exped, count(2 * g + 1))
                        nc.vector.scalar_tensor_tensor(qf[:, :], k.bank(0), 0.0, lo[:, 0], ALU.max, ALU.add)\
                            .then_inc(qf_ready, 1)
                        dve.wait_ge(exped, count(2 * g + 2))
                        nc.vector.scalar_tensor_tensor(kf[:, :, :], kvb[:, :, 0], 0.0, l3, ALU.max, ALU.add)\
                            .then_inc(kf_ready, 1)
                        dve.wait_ge(ksum_mm, count(g + 1))
                        heads = k.w("c_heads").unsqueeze(1).broadcast_to([D, 2 * 2 * TPG, D])
                        nc.vector.tensor_tensor(kvm[:, :, :, :, :].rearrange("p b t a d -> p (b t a) d"),
                                                k.ps[:, 3 * 512:7 * 512].rearrange("p (n d) -> p n d", d=D), heads,
                                                ALU.mult).then_inc(masked, 1)
                        dve.wait_ge(num_mm, count(2 * g + 1))
                        ch.link(nc.vector.tensor_scalar(rd[:, :], k.bank(0), 1e-6, None, ALU.add))
                        ch.link(nc.vector.reciprocal(rd[:, :], rd[:, :]))
                        dve.wait_ge(num_mm, count(2 * g + 2))
                        nc.vector.tensor_tensor(cf[:, :], k.bank(7), rd[:, :], ALU.mult).then_inc(c_ready, 1)
                        dve.wait_ge(o_mm, count(g + 1))
                        hc = k.h[:, bass.ts(g, GW)]
                        nc.vector.scalar_tensor_tensor(hc, k.bank(1), k.w("l3a_bo"), hc, ALU.add, ALU.add)\
                            .then_inc(h_done, 1)
        layer_norm(k, k.h, n, "l3a_ln2", gain=k.w("l3a_g2"), bias=k.w("l3a_b2"), add_to=k.x, add=k.h)
        feed_forward(k, "l3a_ff", ACT.Gelu, [(k.w(f"l3a_w1_{i}"), k.w(f"l3a_fb_{i}"), None, k.w(f"l3a_w2_{i}"), None)
                                             for i in range(4)], k.x, out_bias=k.w("l3a_fb2"), src=n)


def l3_xattn(k):
    nc = k.nc
    layer_norm(k, k.x, k.h, "l3x_ln", add_to=k.x)
    with Stage(nc) as st:
        (staged, turn_mm, turned, s_mm, e_ready, simk, chosen, agg_mm, ok_ready, out_mm, x_done, step, ones_set, ab) = st.sem(
            *["l3x_" + s for s in ("staged turn_mm turned s_mm e_ready simk chosen agg_mm ok_ready out_mm x_done step "
                                   "ones_set ab").split()])
        hg = st.sb("l3x_h_group", [D, 2, GW])
        tm = st.sb("l3x_token_major", [128, 2, TPG, D])
        sim = st.sb("l3x_sim", [128, 2, TPG, S])
        pick = st.sb("l3x_pick", [128, 3, TPG, S])
        mxs = st.sb("l3x_max", [128, 3, TPG])
        okk = st.sb("l3x_rows", [128, TPG, D])
        ones = st.sb("l3x_ones", [128, 1])
        neg = st.sb("l3x_negated", [128, 2])
        both = lambda: sim[:, :, :, :].rearrange("p a t s -> p (a t s)")
        with st.block() as block:
            @block.gpsimd
            def _(pool):
                nc.gpsimd.memset(ones[:, :], 1.0).then_inc(ones_set, 1)
                with pool.Fori(0, G) as g:
                    pool.wait_ge(s_mm, count(g))
                    nc.gpsimd.tensor_copy(hg[:, 0], k.h[:, bass.ts(g, GW)])
                    nc.gpsimd.tensor_copy(hg[:, 1], k.ctx[:, bass.ts(g, GW)]).then_inc(staged, 1)

            @block.tensor
            def _(pe):
                pe.wait_ge(ones_set, count(1))
                with pe.Fori(0, G) as g:
                    pe.wait_ge(staged, count(g + 1))
                    pe.wait_ge(x_done, count(g))
                    for a in range(2):
                        for t in range(TPG):
                            m = nc.tensor.transpose(k.bank(a)[:, t * D:t * D + D], hg[:, a, t * 128:t * 128 + 128],
                                                    k.w("c_ident"))
                    m.then_inc(turn_mm, 1)
                    for a in range(2):
                        for t in range(TPG):
                            for b in range(2):
                                c = slice(t * 128 + b * 64, t * 128 + b * 64 + 64)
                                m = nc.tensor.matmul(k.bank(2)[b * 64:b * 64 + 64, a * 256 + t * S:a * 256 + t * S + S],
                                                     hg[:, a, c], hg[:, 1 - a, c])
                    m.then_inc(s_mm, 1)
                    pe.wait_ge(turned, count(1))
                    pe.wait_ge(turned, count(g + 1))
                    pe.wait_ge(chosen, count(g + 1))
                    for t in range(TPG):
                        for b in range(2):
                            rows = slice(b * 64, b * 64 + 64)
                            nc.tensor.matmul(k.bank(4 + b)[rows, t * D:t * D + D], pick[rows, 2, t], tm[rows, 0, t])
                            m = nc.tensor.matmul(k.bank(6 + b)[rows, t:t + 1], pick[rows, 1, t], ones[rows, :])
                    m.then_inc(agg_mm, 1)
                    pe.wait_ge(ok_ready, count(g + 1))
                    for t in range(TPG):
                        for b in range(2):
                            rows = slice(b * 64, b * 64 + 64)
                            m = nc.tensor.matmul(k.bank(b)[:, t * S:t * S + S], okk[rows, t], sim[rows, 1, t])
                    m.then_inc(out_mm, 1)

            @block.scalar
            def _(act):
                nc.scalar.preload_act_table(ACT.Exp)
                act.wait_ge(ab, count(1))
                with act.Fori(0, G) as g:
                    act.wait_ge(out_mm, count(g))
                    act.wait_ge(s_mm, count(g + 1))
                    nc.scalar.activation(both(), k.bank(2), ACT.Exp, scale=neg[:, 0:1], bias=neg[:, 1:2]).then_inc(e_ready, 1)
                    act.wait_ge(turn_mm, count(g + 1))
                    nc.scalar.copy(tm[:, :, :, :].rearrange("p a t d -> p (a t d)"), k.ps[:, 0:1024]).then_inc(turned, 1)

            @block.vector
            def _(dve):
                ch = Chain(dve, step, 9)
                nc.vector.tensor_scalar(neg[:, :], k.w("l3x_ab"), -1.0, None, ALU.mult).then_inc(ab, 1)
                mx, den, rc = (mxs[:, i] for i in range(3))
                wide = lambda a: a.unsqueeze(2).broadcast_to([128, TPG, S])
                with dve.Fori(0, G) as g:
                    ch.turn(g)
                    dve.wait_ge(e_ready, count(g + 1))
                    ch.link(nc.vector.tensor_scalar(both(), both(), 1.0, None, ALU.add))
                    ch.link(nc.vector.reciprocal(both(), both()))
                    ch.link(nc.vector.tensor_reduce(mx, sim[:, 0], AX.X, ALU.max))
                    ch.link(nc.vector.tensor_tensor(pick[:, 0], sim[:, 0], wide(mx), ALU.is_equal))
                    ch.link(nc.vector.tensor_tensor(pick[:, 0], pick[:, 0], k.w("c_falling").unsqueeze(1)
                                                    .broadcast_to([128, TPG, S]), ALU.mult))
                    ch.link(nc.vector.tensor_reduce(mx, pick[:, 0], AX.X, ALU.max))
                    ch.link(nc.vector.tensor_tensor(pick[:, 1], pick[:, 0], wide(mx), ALU.is_equal))
                    nc.vector.tensor_tensor(pick[:, 2], pick[:, 1], sim[:, 0], ALU.mult).then_inc(chosen, 1)
                    dve.wait_ge(agg_mm, count(g + 1))
                    dve.wait_ge(turned, count(g + 1))
                    for b in range(2):
                        rows = slice(b * 64, b * 64 + 64)
                        nc.vector.tensor_tensor(okk[rows].rearrange("p t d -> p (t d)"), k.bank(4 + b)[rows],
                                                tm[rows, 1].rearrange("p t d -> p (t d)"), ALU.add)
                        m = nc.vector.tensor_scalar(den[rows], k.bank(6 + b, TPG)[rows], 1.0, None, ALU.add)
                    ch.link(m)
                    ch.link(nc.vector.reciprocal(rc, den))
                    nc.vector.tensor_tensor(okk[:, :, :], okk[:, :, :], rc.unsqueeze(2).broadcast_to([128, TPG, D]),
                                            ALU.mult).then_inc(ok_ready, 1)
                    dve.wait_ge(out_mm, count(g + 1))
                    xg = k.x[:, bass.ts(g, GW)].rearrange("p (t b s) -> p b t s", b=2, s=64)
                    for b in range(2):
                        m = nc.vector.tensor_tensor(xg[:, b], xg[:, b],
                                                    k.bank(b, 256).rearrange("p (t s) -> p t s", s=64), ALU.add)
                    m.then_inc(x_done, 1)


def build(nc, cols, dram, out):
    with ExitStack() as stack:
        k = Core(nc, cols, stack, dram)
        experts = lambda area: (area + "_experts", k.packed[area][:, 0:cols[area][""]], dram["packed_" + area])
        needed_first = Load(k, [("x", k.x[:, :], dram["x_in"]), ("first", k.packed["first"][:, :], dram["packed_first"])])
        rest = Load(k, [("ctx", k.ctx[:, :], dram["ctx_in"]),
                        ("shared", k.packed["shared"][:, :], dram["packed_shared"]), experts("l2f")])
        needed_first.finish()
        l0_attn(k)
        rest.finish()
        l0_xattn(k)
        l0_ffn(k)
        l1_attn(k)
        l1_xattn(k)
        l1_ffn(k)
        l2_attn(k)
        l2_xattn(k)
        l2_ffn(k)
        last_experts = Load(k, [experts("l3f")])
        l3_attn(k)
        l3_xattn(k)
        last_experts.finish()
        l3_ffn(k)
        store_stage(k, out)


def layout(inp):
    n = lambda name: np.asarray(inp[name])
    col = lambda a: a.reshape(-1, 1)
    one = np.float32
    c = {}
    c["c_mean"] = np.full((D, D), 1.0 / D, one)
    c["c_eps"] = np.full((D, 1), LN_EPS, one)
    c["c_ident"] = np.eye(128, dtype=one)
    c["c_by_h"] = (np.arange(D)[:, None] // DH % 2 == np.arange(2)).astype(one)
    c["c_by_p"] = (np.arange(D)[:, None] // DH % NQ // 2 == np.arange(2)).astype(one)
    slope = (2.0 ** (-8.0 * np.arange(1, H + 1, dtype=one) / H)).astype(one)
    pos = np.arange(S, dtype=one)
    h, qpos = np.arange(128)[:, None, None, None] // S, np.tile(pos, 2)[:, None, None, None]
    r, p = np.arange(NQ)[None, :, None, None], np.arange(2)[None, None, :, None]
    c["c_alibi"] = np.where(pos > qpos, one(NEG), slope[4 * r + 2 * p + h] * (pos - qpos)).astype(one).reshape(128, -1)
    c["l0a_wq"], c["l0a_wk"], c["l0a_wv"] = n("L0_attn_W_query"), n("L0_attn_W_key"), n("L0_attn_W_value")
    c["l0a_wo"], c["l0a_bo"] = n("L0_attn_W_proj"), col(n("L0_attn_b_proj"))
    w, b = n("L2_xattn_Wqkv"), n("L2_xattn_bqkv")
    c["l2x_wq"], c["l2x_wk"], c["l2x_wv"] = w[:, 0:D], w[:, D:2 * D], w[:, 2 * D:]
    c["l2x_bq"], c["l2x_bk"], c["l2x_bv"] = col(b[0:D]), col(b[D:2 * D]), col(b[2 * D:])
    w, b = n("L2_xattn_Wqkv_aux"), n("L2_xattn_bqkv_aux")
    c["l2x_wka"], c["l2x_wva"], c["l2x_bka"], c["l2x_bva"] = w[:, D:2 * D], w[:, 2 * D:], col(b[D:2 * D]), col(b[2 * D:])
    c["l2x_wo"], c["l2x_bo"] = n("L2_xattn_Wo"), col(n("L2_xattn_bo"))
    c["l2x_gate"] = col(np.repeat(n("L2_xattn_g"), DH))
    w1, w2, b1 = n("L0_ffn_w1")[0], n("L0_ffn_w2")[0], n("L0_ffn_b1")[0]
    for i in range(4):
        r = slice(i * 128, i * 128 + 128)
        c[f"l0f_w1_{i}"], c[f"l0f_b1_{i}"], c[f"l0f_w2_{i}"] = w1[:, r], col(b1[r]), w2[r]
    c["l0f_b2"], c["l0f_gamma"], c["l0f_beta"] = col(n("L0_ffn_b2")[0]), col(n("L0_ffn_gamma")), col(n("L0_ffn_beta"))
    wd, bd, wu = n("L1_ffn_Wd"), n("L1_ffn_bd"), n("L1_ffn_Wu")
    c["l1f_gate"], c["l1f_bu"] = n("L1_ffn_w_gate"), n("L1_ffn_bu")
    for i in range(4):
        e = slice(2 * i, 2 * i + 2)
        c[f"l1f_wd_{i}"] = wd[e].transpose(1, 0, 2).reshape(128, 128)
        c[f"l1f_bd_{i}"], c[f"l1f_wu_{i}"] = col(bd[e]), wu[e].reshape(128, 128)
    w1, w2, w3 = n("L2_ffn_w1"), n("L2_ffn_w2"), n("L2_ffn_w3")
    c["l2f_gate"] = n("L2_ffn_gate_w").T
    for i in range(16):
        e, r = i // 2, slice(i % 2 * 128, i % 2 * 128 + 128)
        c[f"l2f_w1_{i}"], c[f"l2f_w3_{i}"], c[f"l2f_w2_{i}"] = w1[e, r].T, w3[e, r].T, w2[e][:, r].T
    c["l3f_router"] = n("L3_ffn_router_w").T
    c["l3f_bias"] = np.broadcast_to(n("L3_ffn_bias")[None], (128, 16))
    for i in range(16):
        c[f"l3f_g_{i}"], c[f"l3f_u_{i}"], c[f"l3f_d_{i}"] = n("L3_ffn_gate_w")[i], n("L3_ffn_up_w")[i], n("L3_ffn_down_w")[i]
    for i in range(2):
        r = slice(i * 128, i * 128 + 128)
        c[f"l3f_sg_{i}"], c[f"l3f_su_{i}"] = n("L3_ffn_sh_gate_w")[:, r], n("L3_ffn_sh_up_w")[:, r]
        c[f"l3f_sd_{i}"] = n("L3_ffn_sh_down_w")[r]
    c["c_ones_row"] = np.ones((1, 128), one)
    c["c_heads"] = (np.arange(D)[:, None] // DH == np.arange(D) // DH).astype(one)
    c["c_restart"] = np.broadcast_to((np.arange(GW) % S != 0).astype(one)[None], (128, GW))
    c["c_causal"] = (np.arange(128)[:, None] % S <= np.arange(S)).astype(one)
    c["c_pos"] = np.broadcast_to(pos[None], (128, S))
    c["c_falling"] = np.broadcast_to((S - pos)[None], (128, S))
    freqs = np.exp(np.arange(D // 2, dtype=one) * one(-np.log(10000.0) / (D // 2)))
    ang = np.tile(freqs[:, None] * pos[None, :], (2, 2))
    c["c_cos"] = np.cos(ang).astype(one)
    c["c_sin"] = (np.sin(ang) * np.where(np.arange(D) < D // 2, -1.0, 1.0)[:, None]).astype(one)
    w, b = n("L1_attn_qkv_w"), n("L1_attn_qkv_b")
    c["l1a_wq"], c["l1a_wk"], c["l1a_wv"] = w[0:D].T, w[D:2 * D].T, w[2 * D:].T
    c["l1a_bq"], c["l1a_bk"], c["l1a_bv"] = col(b[0:D]), col(b[D:2 * D]), col(b[2 * D:])
    c["l1a_wo"], c["l1a_bo"] = n("L1_attn_out_w").T, col(n("L1_attn_out_b"))
    for x in "qkv":
        c[f"l1x_w{x}"], c[f"l1x_b{x}"] = n(f"L1_xattn_W{x}"), col(n(f"L1_xattn_b{x}"))
    for x in ("ln_w", "ln_b", "bh"):
        c[f"l2a_{x}"] = col(n(f"L2_attn_{x}"))
    c["l2a_delta_alpha"] = np.concatenate([n("L2_attn_ema_delta")[:, :, 0], n("L2_attn_ema_alpha")[:, :, 0]], axis=1)
    c["l2a_beta"], c["l2a_gamma"], c["l2a_omega"] = (n("L2_attn_ema_beta")[:, :, 0], n("L2_attn_ema_gamma"),
                                                     col(n("L2_attn_ema_omega")))
    c["l2a_wv"], c["l2a_bv"] = n("L2_attn_Wv").T, n("L2_attn_bv")[None]
    for i in range(5):
        r = slice(i * D, i * D + D)
        c[f"l2a_wmx{i}"], c[f"l2a_bmx{i}"] = n("L2_attn_Wmx")[r].T, col(n("L2_attn_bmx")[r])
    for i in range(2):
        c[f"l2a_wh{i}"] = n("L2_attn_Wh")[:, i * D:i * D + D].T
    c["l2a_qg"], c["l2a_qb"] = n("L2_attn_qk_gamma").T, n("L2_attn_qk_beta").T
    for x, name in (("ra", "alpha"), ("rb", "beta")):
        v = n(f"L2_attn_rot_{name}")[0]
        c[f"l2a_{x}"], c[f"l2a_{x}s"] = col(v), col(np.roll(v, D // 2))
    w = n("L3_attn_qkv_w")
    c["l3a_wq"], c["l3a_wkv"], c["l3a_wo"] = w[0:D].T, w[D:].T, n("L3_attn_proj_w").T
    c["l3a_bo"] = col(n("L3_attn_proj_b"))
    for i in (1, 2):
        c[f"l3a_g{i}"], c[f"l3a_b{i}"] = col(n(f"L3_attn_norm{i}_g")), col(n(f"L3_attn_norm{i}_b"))
    for i in range(4):
        r = slice(i * 128, i * 128 + 128)
        c[f"l3a_w1_{i}"], c[f"l3a_w2_{i}"] = n("L3_attn_fc1_w")[r].T, n("L3_attn_fc2_w")[:, r].T
        c[f"l3a_fb_{i}"] = col(n("L3_attn_fc1_b")[r])
    c["l3a_fb2"] = col(n("L3_attn_fc2_b"))
    c["l3x_ab"] = np.broadcast_to(np.stack([n("L3_xattn_sim_alpha")[0], n("L3_xattn_sim_beta")[0]])[None], (128, 2))
    c["l0x_wq"] = n("L0_xattn_Wq").T
    c["l0x_wk"] = n("L0_xattn_Wk").T
    c["l0x_wv"] = n("L0_xattn_Wv").T
    return c


def kernel(**inputs):
    import concourse.bacc as bacc
    from concourse.bass_utils import run_bass_kernel_spmd

    nc = bacc.Bacc("TRN2", target_bir_lowering=False, num_devices=1)
    pieces = layout(inputs)
    cols, packed = {}, {}
    early = {"c_mean", "c_eps", "c_ident", "c_by_h", "c_by_p", "c_alibi"}
    area_of = lambda name: ("first" if name in early or name[:3] == "l0a" else
                            name[:3] if name[:3] in ("l2f", "l3f") else "shared")
    for area in ("first", "shared", "l2f", "l3f"):
        own = {name: a for name, a in pieces.items() if area_of(name) == area}
        at, where = 0, {}
        for name, a in own.items():
            where[name] = (at, a.shape[1], a.shape[0])
            at += a.shape[1]
        where[""] = at
        cols[area], packed[area] = where, np.zeros((128, at), np.float32)
        for name, a in own.items():
            o, w, r = where[name]
            packed[area][0:r, o:o + w] = a
    n = lambda name: np.asarray(inputs[name])
    tiles = lambda a: np.ascontiguousarray(a.reshape(B // 2, 128, S).transpose(1, 0, 2))
    table = np.zeros((D, 2, NQ, 2, 2 * S - 1), np.float32)
    for head in range(H):
        table[head * DH:head * DH + DH, head % 2, head // NQ, head % NQ // 2] = n("L1_xattn_rel_table")[1:2 * S].T
    arrays = {
        "rel_in": table.reshape(D, -1),
        "mask_in": n("mask_Bx1x1xS2_ff0").reshape(B, S),
        **{name: np.tile(np.repeat(np.eye(e, dtype=np.float32), width, axis=1), (3, 1))
           for name, e, width in (("sel_l1", 8, 64), ("sel_l2", 8, 128), ("sel_l3", 16, 128))},
        "x_in": np.ascontiguousarray(n("x").reshape(T, D).T),
        "ctx_in": np.ascontiguousarray(n("ctx_1024").reshape(T, D).T),
        **{"packed_" + area: a for area, a in packed.items()},
        "cross_mask": tiles(n("mask_BxSxS2_bk0").transpose(0, 2, 1)),
    }
    aps = {name: nc.dram_tensor(name, a.shape, mybir.dt.from_np(a.dtype), kind="ExternalInput").ap()
           for name, a in arrays.items()}
    out = nc.dram_tensor("y_out", (D, T), F32, kind="ExternalOutput").ap()
    build(nc, cols, aps, out)
    r = run_bass_kernel_spmd(nc, [arrays], core_ids=[0])
    return np.ascontiguousarray(r.results[0]["y_out"].T).reshape(B, S, D)
```

```python
from contextlib import ExitStack

import numpy as np
import concourse.bass as bass
from concourse import mybir

F32 = mybir.dt.float32
BF16 = mybir.dt.bfloat16
U8 = mybir.dt.uint8
ALU = mybir.AluOpType
ACT = mybir.ActivationFunctionType
AX = mybir.AxisListType

D = 128
B, S = 64, 64
T = B * S
GW = 512
G = T // GW
TPG = GW // 128
H, DH = 16, 8
NQ = 4
LN_EPS = 1e-5
NEG = -1.0e30
LOWEST = -3.0e38


class Stage:

    def __init__(self, nc):
        self.nc, self.stack, self.sems = nc, ExitStack(), []

    def __enter__(self):
        self.stack.__enter__()
        return self

    def sem(self, *names):
        new = [self.nc.alloc_semaphore(n) for n in names]
        self.sems += new
        return new if len(new) > 1 else new[0]

    def block(self):
        engines = (self.nc.vector, self.nc.scalar, self.nc.tensor, self.nc.sync)
        for i, s in enumerate(self.sems):
            engines[i % len(engines)].sem_inc(s, 1)
        self.nc.all_engine_barrier()
        return self.nc.Block(no_gpsimd_drain=True)

    def sb(self, name, shape, dt=F32):
        return self.stack.enter_context(self.nc.sbuf_tensor(name, shape, dt))

    def __exit__(self, *a):
        self.nc.clear_and_free_semaphores(self.sems)
        self.nc.all_engine_barrier()
        return self.stack.__exit__(*a)


def count(n):
    return n + 1


class Chain:

    def __init__(self, eng, sem, per=0):
        self.eng, self.sem, self.per, self.k, self.base = eng, sem, per, 0, 0

    def turn(self, base):
        assert self.k in (0, self.per), (self.k, self.per)
        self.k, self.base = 0, base * self.per

    def link(self, ins):
        self.k += 1
        ins.then_inc(self.sem, 1)
        self.eng.wait_ge(self.sem, count(self.base + self.k))


class Core:

    def __init__(self, nc, cols, stack, dram):
        self.nc, self.cols, self.dram = nc, cols, dram
        sb = lambda n, s, dt=F32: stack.enter_context(nc.sbuf_tensor(n, s, dt))
        self.x = sb("x_residual", [D, T])
        self.ctx = sb("ctx_features", [D, T])
        self.h = sb("h_normed", [D, T])
        experts = sb("weights_experts", [128, max(cols["l2f"][""], cols["l3f"][""])])
        self.packed = {"first": sb("weights_first", [128, cols["first"][""]]),
                       "shared": sb("weights_shared", [128, cols["shared"][""]]), "l2f": experts, "l3f": experts}
        self.areas = {name: area for area, pieces in cols.items() for name in pieces if name}
        self.ps = stack.enter_context(nc.psum_tensor("banks", [128, 8 * 512], F32))

    def w(self, name):
        area = self.areas[name]
        o, w, rows = self.cols[area][name]
        return self.packed[area][0:rows, o:o + w]

    def bank(self, i, n=512):
        return self.ps[:, i * 512:i * 512 + n]


def layer_norm(k, src, dst, tag, gain=None, bias=None, add_to=None, add=None):
    nc = k.nc
    mean_w, eps = k.w("c_mean"), k.w("c_eps")
    with Stage(nc) as st:
        mean_ready, centred, squared, var_ready, logged, rstd_ready, scaled, normed = st.sem(
            *[f"{tag}_{n}" for n in "mean_ready centred squared var_ready logged rstd_ready scaled normed".split()])
        sq = st.sb(f"{tag}_squares", [D, T])

        with st.block() as block:
            @block.tensor
            def _(pe):
                def mean(g):
                    c = bass.ds(g * GW, GW)
                    nc.tensor.matmul(k.ps[:, c], mean_w, src[:, c]).then_inc(mean_ready, 1)

                def variance(g):
                    c = bass.ds(g * GW, GW)
                    pe.wait_ge(squared, count(g + 1))
                    nc.tensor.matmul(k.ps[:, c], mean_w, sq[:, c]).then_inc(var_ready, 1)

                mean(0)
                mean(1)
                mean(2)
                with pe.Fori(0, G - 3) as g:
                    variance(g)
                    mean(g + 3)
                for g in range(G - 3, G):
                    variance(g)

            @block.scalar
            def _(act):
                nc.scalar.preload_act_table_set("natural_log_exp_and_others")

                def square(g):
                    act.wait_ge(centred, count(g + 1))
                    act.wait_ge(mean_ready, count(1))
                    nc.scalar.activation(sq[:, bass.ds(g * GW, GW)], dst[:, bass.ds(g * GW, GW)],
                                         ACT.Square).then_inc(squared, 1)

                def rstd(g):
                    v = k.ps[:, bass.ts(g, GW)]
                    act.wait_ge(var_ready, count(g + 1))
                    act.wait_ge(mean_ready, count(1))
                    nc.scalar.activation(v, v, ACT.Ln, bias=eps).then_inc(logged, 1)
                    act.wait_ge(mean_ready, count(1))
                    act.wait_ge(logged, count(g + 1))
                    nc.scalar.activation(v, v, ACT.Exp, scale=-0.5).then_inc(rstd_ready, 1)

                square(0)
                square(1)
                with act.Fori(0, G - 2) as g:
                    rstd(g)
                    square(g + 2)
                rstd(G - 2)
                rstd(G - 1)

            @block.vector
            def _(dve):
                def centre(g):
                    c = bass.ds(g * GW, GW)
                    dve.wait_ge(mean_ready, count(g + 1))
                    nc.vector.tensor_tensor(dst[:, c], src[:, c], k.ps[:, c], ALU.subtract).then_inc(centred, 1)

                def scale(g):
                    c = bass.ts(g, GW)
                    dve.wait_ge(rstd_ready, count(g + 1))
                    if gain is None:
                        nc.vector.tensor_tensor(dst[:, c], dst[:, c], k.ps[:, c], ALU.mult).then_inc(scaled, 1)
                    else:
                        nc.vector.scalar_tensor_tensor(dst[:, c], dst[:, c], gain, k.ps[:, c],
                                                       ALU.mult, ALU.mult).then_inc(scaled, 1)
                        dve.wait_ge(scaled, count(g + 1))
                        nc.vector.tensor_scalar(dst[:, c], dst[:, c], bias, None, ALU.add).then_inc(normed, 1)

                centre(0)
                centre(1)
                with dve.Fori(0, G - 2) as g:
                    centre(g + 2)
                    scale(g)
                scale(G - 2)
                scale(G - 1)

            if add_to is not None:
                @block.gpsimd
                def _(pool):
                    with pool.Fori(0, G) as g:
                        c = bass.ts(g, GW)
                        pool.wait_ge(scaled if gain is None else normed, count(g + 1))
                        nc.gpsimd.tensor_tensor(add_to[:, c], add_to[:, c], (dst if add is None else add)[:, c], ALU.add)


class Load:

    def __init__(self, k, parts):
        self.k, nc = k, k.nc
        self.loaded = [nc.alloc_semaphore(name + "_loaded") for name, _, _ in parts]
        with nc.Block(no_gpsimd_drain=True) as block:
            @block.sync
            def _(sp):
                for (_, to, source), loaded in zip(parts, self.loaded):
                    nc.sync.dma_start(to, source).then_inc(loaded, 16)

    def finish(self):
        nc = self.k.nc
        with nc.Block(no_gpsimd_drain=True) as block:
            @block.sync
            def _(sp):
                for loaded in self.loaded:
                    sp.wait_ge(loaded, 16)
        nc.clear_and_free_semaphores(self.loaded)
        nc.all_engine_barrier()


def softmax_attention(k, tag, q, sources, out_w=None, out_b=None, score_bias=None, rel=None, normed=False):
    nc, ns = k.nc, len(sources)
    NB = 2 * ns
    NU = NB * TPG
    TURNS = G // 2
    gated, biased_scores = sources[0][5] is not None, score_bias is not None or rel is not None
    if not normed:
        layer_norm(k, k.x, k.h, tag + "_ln")
    with Stage(nc) as st:
        (zeroed, q_mm, q_sb, k_mm, k_sb, staged, v_mm, v_sb, s_mm, biased, max_ready, s_read, e_ready, sum_ready,
         r_ready, p_ready, t_mm, pt_sb, pv_mm, c_read, c_ready, o_mm, x_done, offset) = st.sem(*[f"{tag}_{n}" for n in (
             "zeroed q_mm q_sb k_mm k_sb staged v_mm v_sb s_mm biased max_ready s_read e_ready sum_ready "
             "r_ready p_ready t_mm pt_sb pv_mm c_read c_ready o_mm x_done offset").split()])
        if rel is not None:
            rel_loaded = st.sem(tag + "_rel_loaded0", tag + "_rel_loaded1")
            relb = st.sb(tag + "_rel", [128, 2, 2, H // 2 * S])
        ke = st.sb(tag + "_keys_spread", [D, 2, GW // S, 2, S])
        qe = st.sb(tag + "_queries_spread", [D, 2, GW // S, 2, S])
        twice = st.sb(tag + "_source_twice", [D, GW // S, 2, S])
        ve = st.sb(tag + "_values_spread", [128, GW // S, 2, D])
        prob = st.sb(tag + "_probs", [128, 4, H, S])
        pt = st.sb(tag + "_probs_turned", [128, 2, 8, 128])
        cf = st.sb(tag + "_context", [D, 2, GW])
        spread_bias = st.sb(tag + "_spread_bias", [D, 1 + ns, 2])
        small = st.sb(tag + "_small", [128, 3, 4, H])
        if gated:
            gates = st.sb(tag + "_gates", [D, 3])
            gate_exp, gate_step = st.sem(tag + "_gate_exp", tag + "_gate_step")
        scores = k.ps[:, 2 * 512:6 * 512].rearrange("p (r c) -> p r c", r=NQ)[:, :, 0:NQ * S]
        by_head = lambda a: a.rearrange("p r (h s) -> p r h s", s=S)
        by_seq = lambda a: a.rearrange("p r (b c) -> p r b c", b=2)
        scale = float(DH) ** -0.5

        def turns(eng, step):
            def body(it, last):
                for m in range(NU):
                    step(it, m, m // TPG, m % TPG, last)
            with eng.Fori(0, TURNS - 1) as it:
                body(it, False)
            body(TURNS - 1, True)

        unit = lambda it, m: it * NU + m
        phase = lambda it, j: it * NB + j
        group = lambda it, j: it * 2 + j // ns
        more = lambda m, last: not (last and m >= NU)
        more_phases = lambda j, last: not (last and j >= NB)

        with st.block() as block:
            if rel is not None:
                @block.sync
                def _(sp):
                    def load(u, p):
                        for h in range(2):
                            nc.sync.dma_start(relb[64 * h:64 * h + 64, p], rel[bass.ds(u * 128, 128), h * 512:h * 512 + 512]
                                              .rearrange("(b s) n -> s b n", b=2)).then_inc(rel_loaded[p], 16)

                    load(0, 0)
                    load(1, 1)
                    with sp.Fori(0, T // 256 - 1) as i:
                        for p in range(2):
                            sp.wait_ge(biased, count(i * 2 + (p + 1)))
                            load(i * 2 + (p + 2), p)

            @block.gpsimd
            def _(pool):
                def stage(it, j, half):
                    c = bass.ds(group(it, j) * GW + half * (GW // 2), GW // 2)
                    nc.gpsimd.tensor_copy(twice[:, 4 * half:4 * half + 4], sources[j % ns][0][:, c]
                                          .rearrange("p (b s) -> p b s", s=S).unsqueeze(2)
                                          .broadcast_to([D, 4, 2, S])).then_inc(staged, 1)

                def normalise(it, m):
                    pool.wait_ge(r_ready, count(unit(it, m) + 1))
                    p = prob[:, m % 4]
                    nc.gpsimd.tensor_tensor(p, p, small[:, 2, m % 4].unsqueeze(2).broadcast_to([128, H, S]),
                                            ALU.mult).then_inc(p_ready, 1)

                nc.gpsimd.memset(ve[:, :, :, :], 0.0).then_inc(zeroed, 1)
                stage(0, 0, 0)
                stage(0, 0, 1)
                normalise(0, 0)
                normalise(0, 1)

                def step(it, m, j, u, last):
                    if more(m + 2, last):
                        normalise(it, m + 2)
                    if u < 2 and more_phases(j + 1, last):
                        pool.wait_ge(v_mm, count(phase(it, j) * 2 + (u + 1)))
                        stage(it, j + 1, u)

                turns(pool, step)

            @block.tensor
            def _(pe):
                def scores_mm(it, m):
                    j, t = m // TPG % NB, m % TPG
                    if t == 0:
                        pe.wait_ge(k_sb, count(phase(it, m // TPG) + 1))
                    pe.wait_ge(s_read, count(unit(it, m)))
                    for b in range(2):
                        for r in range(NQ):
                            f = slice(32 * r, 32 * r + 32)
                            x = nc.tensor.matmul(scores[:, r, b * 2 * S:(b + 1) * 2 * S],
                                                 qe[f, j // ns, t * 2 + b].rearrange("p h s -> p (h s)"),
                                                 ke[f, j % 2, t * 2 + b].rearrange("p h s -> p (h s)"),
                                                 tile_position=(32 * r, 0))
                    x.then_inc(s_mm, 1)

                def turn(it, m):
                    pe.wait_ge(pt_sb, count(unit(it, m)))
                    pe.wait_ge(p_ready, count(unit(it, m) + 1))
                    for i in range(8):
                        x = nc.tensor.transpose(k.bank(6 + i // 4)[:, (i % 4) * 128:(i % 4) * 128 + 128],
                                                prob[:, m % 4, 2 * i:2 * i + 2].rearrange("p h s -> p (h s)"),
                                                k.w("c_ident"))
                    x.then_inc(t_mm, 1)

                def values(it, m):
                    j, t = m // TPG, m % TPG
                    if t == 0:
                        pe.wait_ge(v_sb, count(phase(it, j) * 2 + 1))
                        if out_w is None or gated:
                            pe.wait_ge(c_read, count(phase(it, j)))
                        if out_w is not None and j % ns == 0:
                            pe.wait_ge(x_done, count(group(it, j)))
                    if t == 2:
                        pe.wait_ge(v_sb, count(phase(it, j) * 2 + 2))
                    pe.wait_ge(pt_sb, count(unit(it, m) + 1))
                    for b in range(2):
                        for r in range(NQ):
                            f = slice(32 * r, 32 * r + 32)
                            for h in range(2):
                                x = nc.tensor.matmul(
                                    k.bank(1)[f, t * 128 + b * 64:t * 128 + b * 64 + 64],
                                    ve[:, t * 2 + b, h, f], pt[:, m % 2, 2 * r + b, h * 64:h * 64 + 64],
                                    start=(h == 0), stop=(h == 1), tile_position=(0, 32 * r))
                    x.then_inc(pv_mm, 1)

                def query(it, j):
                    nc.tensor.matmul(k.bank(0), k.w(q[0]), k.h[:, bass.ts(group(it, j), GW)]).then_inc(q_mm, 1)

                def key(it, j):
                    s = sources[j % ns]
                    pe.wait_ge(q_sb, count(group(it, j) + 1))
                    nc.tensor.matmul(k.bank(0), k.w(s[1]), s[0][:, bass.ts(group(it, j), GW)]).then_inc(k_mm, 1)

                def value(it, j, half):
                    if half == 0:
                        pe.wait_ge(k_sb, count(phase(it, j) + 1))
                    else:
                        pe.wait_ge(v_sb, count(phase(it, j) * 2 + 1))
                    pe.wait_ge(staged, count(phase(it, j) * 2 + (half + 1)))
                    for b in range(4):
                        x = nc.tensor.matmul(k.bank(0)[:, b * D:b * D + D],
                                             twice[:, 4 * half + b].rearrange("p c s -> p (c s)"),
                                             k.w(sources[j % ns][3]))
                    x.then_inc(v_mm, 1)

                query(0, 0)
                key(0, 0)
                value(0, 0, 0)
                value(0, 0, 1)
                for m in range(3):
                    scores_mm(0, m)
                turn(0, 0)

                def step(it, m, j, u, last):
                    following = more_phases(j + 1, last)
                    if more(m + 3, last):
                        scores_mm(it, m + 3)
                    if u == 0 and following:
                        pe.wait_ge(v_sb, count(phase(it, j) * 2 + 2))
                        if (j + 1) % ns == 0:
                            query(it, j + 1)
                    if more(m + 1, last):
                        turn(it, m + 1)
                    if u == 0 and following:
                        key(it, j + 1)
                    values(it, m)
                    if u == 1 and following:
                        value(it, j + 1, 0)
                    if u == 3 and following:
                        value(it, j + 1, 1)
                    if u == TPG - 1 and j % ns == ns - 1 and out_w is not None:
                        pe.wait_ge(c_ready, count(group(it, j) + 1))
                        nc.tensor.matmul(k.bank(1), k.w(out_w), cf[:, 0]).then_inc(o_mm, 1)

                turns(pe, step)

            @block.scalar
            def _(act):
                lower, upper = k.w("c_by_h"), k.w("c_by_p")

                def spread(out, mask, bias, row):
                    for i in range(2):
                        x = nc.scalar.activation(out[:, :, i], k.bank(0).rearrange("p (b s) -> p b s", s=S),
                                                 ACT.Identity, scale=mask[:, i:i + 1],
                                                 bias=spread_bias[:, row, i:i + 1] if bias else 0.0)
                    return x

                def query(it, j):
                    act.wait_ge(q_mm, count(group(it, j) + 1))
                    spread(qe[:, j // ns % 2], lower, q[1], 0).then_inc(q_sb, 1)

                def key(it, j):
                    act.wait_ge(k_mm, count(phase(it, j) + 1))
                    spread(ke[:, j % 2], upper, sources[j % ns][2], 1 + j % ns).then_inc(k_sb, 1)

                def value(it, j, half):
                    act.wait_ge(v_mm, count(phase(it, j) * 2 + (half + 1)))
                    for p in range(2):
                        rows = slice(64 * p, 64 * p + 64)
                        for h in range(2):
                            f = lambda a: a.rearrange("p b (r n e) -> p b r n e", r=NQ, n=NQ)[:, :, :, 2 * p + h]
                            x = nc.scalar.copy(f(ve[rows, 4 * half:4 * half + 4, h]),
                                               f(k.bank(0)[rows].rearrange("p (b d) -> p b d", d=D)))
                    x.then_inc(v_sb, 1)

                def exp(it, m):
                    act.wait_ge(s_read, count(unit(it, m) + 1))
                    nc.scalar.activation(prob[:, m % 4], prob[:, m % 4], ACT.Exp, scale=scale).then_inc(e_ready, 1)

                def evacuate(it, m):
                    act.wait_ge(t_mm, count(unit(it, m) + 1))
                    nc.scalar.copy(pt[:, m % 2].rearrange("p j q -> p (j q)"), k.ps[:, 6 * 512:8 * 512]).then_inc(pt_sb, 1)

                nc.scalar.preload_act_table(ACT.Exp)
                if gated:
                    nc.scalar.activation(gates[:, 0:1], k.w(sources[0][5]), ACT.Exp, scale=-1.0).then_inc(gate_exp, 1)
                if q[1] is not None:
                    nc.scalar.activation(spread_bias[:, 0], lower, ACT.Identity, scale=k.w(q[1]))
                    for i in range(ns):
                        x = nc.scalar.activation(spread_bias[:, 1 + i], upper, ACT.Identity, scale=k.w(sources[i][2]))
                    x.then_inc(offset, 1)
                    act.wait_ge(offset, count(1))
                query(0, 0)
                key(0, 0)
                act.wait_ge(zeroed, count(1))
                value(0, 0, 0)
                value(0, 0, 1)
                for m in range(3):
                    exp(0, m)
                evacuate(0, 0)

                def step(it, m, j, u, last):
                    following = more_phases(j + 1, last)
                    if u == 0 and following and (j + 1) % ns == 0:
                        query(it, j + 1)
                    if more(m + 1, last):
                        evacuate(it, m + 1)
                    if u == 0 and following:
                        key(it, j + 1)
                    if more(m + 3, last):
                        exp(it, m + 3)
                    if u in (1, 3) and following:
                        value(it, j + 1, u // 2)

                turns(act, step)

            @block.vector
            def _(dve):
                if gated:
                    e, a, b = gates[:, 0:1], gates[:, 1:2], gates[:, 2:3]
                    dve.wait_ge(gate_exp, count(1))
                    nc.vector.tensor_scalar(a, e, 1.0, None, ALU.add).then_inc(gate_step, 1)
                    dve.wait_ge(gate_step, count(1))
                    nc.vector.reciprocal(b, a).then_inc(gate_step, 1)
                    dve.wait_ge(gate_step, count(2))
                    nc.vector.tensor_scalar(a, b, -1.0, 1.0, ALU.mult, ALU.add).then_inc(gate_step, 1)
                    dve.wait_ge(gate_step, count(3))

                def centre(it, m):
                    n = unit(it, m)
                    mx = small[:, 0, m % 4].rearrange("p (r h) -> p r h", r=NQ)
                    dve.wait_ge(s_mm, count(n + 1))
                    if rel is not None:
                        dve.wait_ge(rel_loaded[m % 2], count(it * (16 * NU) + 32 * (m // 2 + 1)))
                        extra = relb[:, m % 2].rearrange("p b (r c) -> p r b c", r=NQ)
                    if score_bias is not None:
                        extra = k.w(score_bias).rearrange("p (r c) -> p r c", r=NQ).unsqueeze(2)\
                            .broadcast_to([128, NQ, 2, 2 * S])
                    if biased_scores:
                        nc.vector.tensor_tensor(by_seq(scores), by_seq(scores), extra, ALU.add).then_inc(biased, 1)
                        dve.wait_ge(biased, count(n + 1))
                    nc.vector.tensor_reduce(mx, by_head(scores), AX.X, ALU.max).then_inc(max_ready, 1)
                    dve.wait_ge(max_ready, count(n + 1))
                    nc.vector.tensor_tensor(prob[:, m % 4].rearrange("p (r h) s -> p r h s", r=NQ), by_head(scores),
                                            mx.unsqueeze(3).broadcast_to([128, NQ, NQ, S]), ALU.subtract).then_inc(s_read, 1)

                def total(it, m):
                    n = unit(it, m)
                    dve.wait_ge(e_ready, count(n + 1))
                    nc.vector.tensor_reduce(small[:, 1, m % 4], prob[:, m % 4], AX.X, ALU.add).then_inc(sum_ready, 1)
                    dve.wait_ge(sum_ready, count(n + 1))
                    nc.vector.reciprocal(small[:, 2, m % 4], small[:, 1, m % 4]).then_inc(r_ready, 1)

                def finish(it, j):
                    i, x = j % ns, k.x[:, bass.ts(group(it, j), GW)]
                    if out_w is None:
                        nc.vector.scalar_tensor_tensor(x, k.bank(1), k.w(sources[0][4]), x, ALU.add, ALU.add)\
                            .then_inc(c_read, 1)
                        return
                    if gated:
                        nc.vector.tensor_scalar(cf[:, i], k.bank(1), k.w(sources[i][4]), gates[:, 1 + i:2 + i],
                                                ALU.add, ALU.mult).then_inc(c_read, 1)
                        if i == 0:
                            return
                        dve.wait_ge(c_read, count(phase(it, j) + 1))
                        nc.vector.tensor_tensor(cf[:, 0], cf[:, 0], cf[:, 1], ALU.add).then_inc(c_ready, 1)
                    else:
                        nc.vector.tensor_copy(cf[:, 0], k.bank(1)).then_inc(c_ready, 1)
                    dve.wait_ge(o_mm, count(group(it, j) + 1))
                    nc.vector.scalar_tensor_tensor(x, k.bank(1), k.w(out_b), x, ALU.add, ALU.add).then_inc(x_done, 1)

                centre(0, 0)
                total(0, 0)
                centre(0, 1)
                total(0, 1)
                centre(0, 2)

                def step(it, m, j, u, last):
                    if more(m + 2, last):
                        total(it, m + 2)
                    if more(m + 3, last):
                        centre(it, m + 3)
                    if u == TPG - 1:
                        dve.wait_ge(pv_mm, count(unit(it, m) + 1))
                        finish(it, j)

                turns(dve, step)


def l0_attn(k):
    softmax_attention(k, "l0a", ("l0a_wq", None), [(k.h, "l0a_wk", None, "l0a_wv", None, None)],
                      out_w="l0a_wo", out_b="l0a_bo", score_bias="c_alibi")


def l2_xattn(k):
    softmax_attention(k, "l2x", ("l2x_wq", "l2x_bq"),
                      [(k.h, "l2x_wk", "l2x_bk", "l2x_wv", "l2x_bv", "l2x_gate"),
                       (k.ctx, "l2x_wka", "l2x_bka", "l2x_wva", "l2x_bva", "l2x_gate")],
                      out_w="l2x_wo", out_b="l2x_bo")



def l0_xattn(k):
    nc = k.nc
    layer_norm(k, k.x, k.h, "l0x_ln")
    with Stage(nc) as st:
        (zeroed, staged, q_mm, k_mm, v_mm, q_sb, k_sb, v_sb, s_mm, mask_step, raw, masked, max_ready, s_ready, e_ready,
         sum_ready, inverted, p_ready, c_mm, x_done, mask_loaded) = st.sem(*["l0x_" + s for s in (
             "zeroed staged q_mm k_mm v_mm q_sb k_sb v_sb s_mm mask_step raw masked max_ready s_ready e_ready "
             "sum_ready inverted p_ready c_mm x_done mask_loaded").split()])
        q = st.sb("l0x_q", [D, GW])
        kk = st.sb("l0x_k", [D, GW])
        v = st.sb("l0x_v", [128, 2, TPG, D])
        sc = st.sb("l0x_scores", [128, TPG, S])
        pb = st.sb("l0x_probs", [128, 2, TPG, 2, S])
        mask = st.sb("l0x_mask", [128, T // 128, S], k.dram["cross_mask"].dtype)
        cg = st.sb("l0x_ctx_group", [D, GW])
        mf = st.sb("l0x_maskf", [128, TPG, S])
        keep = st.sb("l0x_keep", [128, TPG, S])
        small = st.sb("l0x_small", [128, 3, TPG])
        scores = k.bank(3, TPG * S).rearrange("p (t q) -> p t q", t=TPG)

        def turns(eng, step):
            with eng.Fori(0, G // 2 - 1) as it:
                for par in range(2):
                    step(it * 2 + par, par, False)
            for par in range(2):
                step(G - 2 + par, par, par == 1)

        with st.block() as block:
            @block.sync
            def _(sp):
                nc.sync.dma_start(mask[:, :, :], k.dram["cross_mask"]).then_inc(mask_loaded, 16)

            @block.gpsimd
            def _(pool):
                nc.gpsimd.memset(pb[:, :, :, :, :], 0.0).then_inc(zeroed, 1)
                with pool.Fori(0, G) as g:
                    pool.wait_ge(v_mm, count(g))
                    nc.gpsimd.tensor_copy(cg[:, :], k.ctx[:, bass.ts(g, GW)]).then_inc(staged, 1)

            @block.tensor
            def _(pe):
                def project(g):
                    c = bass.ds(g * GW, GW)
                    pe.wait_ge(q_sb, count(g))
                    pe.wait_ge(k_sb, count(g))
                    nc.tensor.matmul(k.bank(0), k.w("l0x_wq"), k.h[:, c]).then_inc(q_mm, 1)
                    nc.tensor.matmul(k.bank(1), k.w("l0x_wk"), k.ctx[:, c]).then_inc(k_mm, 1)
                    pe.wait_ge(v_sb, count(g))
                    pe.wait_ge(staged, count(g + 1))
                    for t in range(TPG):
                        m = nc.tensor.matmul(k.bank(2)[:, t * D:(t + 1) * D], cg[:, t * 128:t * 128 + 128], k.w("l0x_wv"))
                    m.then_inc(v_mm, 1)
                    pe.wait_ge(raw, count(g))
                    pe.wait_ge(q_sb, count(g + 1))
                    pe.wait_ge(k_sb, count(g + 1))
                    for t in range(TPG):
                        for b in range(2):
                            c = slice(t * 128 + b * 64, t * 128 + b * 64 + 64)
                            m = nc.tensor.matmul(scores[b * 64:b * 64 + 64, t, :], kk[:, c], q[:, c])
                    m.then_inc(s_mm, 1)

                project(0)

                def step(g, par, last):
                    if not last:
                        project(g + 1)
                    pe.wait_ge(x_done, count(g))
                    pe.wait_ge(v_sb, count(g + 1))
                    pe.wait_ge(p_ready, count(g + 1))
                    for t in range(TPG):
                        m = nc.tensor.matmul(k.bank(4)[:, t * 128:t * 128 + 128], v[:, par, t],
                                             pb[:, par, t].rearrange("p b s -> p (b s)"))
                    m.then_inc(c_mm, 1)

                turns(pe, step)

            @block.scalar
            def _(act):
                def evacuate(g, par):
                    act.wait_ge(s_mm, count(g))
                    act.wait_ge(q_mm, count(g + 1))
                    nc.scalar.copy(q[:, :], k.bank(0)).then_inc(q_sb, 1)
                    act.wait_ge(k_mm, count(g + 1))
                    nc.scalar.copy(kk[:, :], k.bank(1)).then_inc(k_sb, 1)
                    act.wait_ge(v_mm, count(g + 1))
                    nc.scalar.copy(v[:, par].rearrange("p t d -> p (t d)"), k.bank(2)).then_inc(v_sb, 1)
                    act.wait_ge(s_ready, count(g + 1))
                    nc.scalar.activation(sc[:, :, :], sc[:, :, :], ACT.Exp).then_inc(e_ready, 1)

                nc.scalar.preload_act_table(ACT.Exp)
                evacuate(0, 0)

                def step(g, par, last):
                    if not last:
                        evacuate(g + 1, 1 - par)

                turns(act, step)

            @block.vector
            def _(dve):
                mx, sm, rc = small[:, 0, :], small[:, 1, :], small[:, 2, :]
                wide = lambda a: a.unsqueeze(2).broadcast_to([128, TPG, S])
                steps = Chain(dve, mask_step, 2)

                def centre(g):
                    s = sc[:, :, :]
                    steps.turn(g)
                    steps.link(nc.vector.tensor_copy(mf[:, :, :], mask[:, bass.ds(g * TPG, TPG), :]))
                    steps.link(nc.vector.tensor_scalar(keep[:, :, :], mf[:, :, :], -1.0, 1.0, ALU.mult, ALU.add))
                    dve.wait_ge(s_mm, count(g + 1))
                    nc.vector.scalar_tensor_tensor(s, scores, float(D) ** -0.5, keep[:, :, :],
                                                   ALU.mult, ALU.mult).then_inc(raw, 1)
                    dve.wait_ge(raw, count(g + 1))
                    nc.vector.scalar_tensor_tensor(s, mf[:, :, :], 1e-9, s, ALU.mult, ALU.add).then_inc(masked, 1)
                    dve.wait_ge(masked, count(g + 1))
                    nc.vector.tensor_reduce(mx, s, AX.X, ALU.max).then_inc(max_ready, 1)
                    dve.wait_ge(max_ready, count(g + 1))
                    nc.vector.tensor_tensor(s, s, wide(mx), ALU.subtract).then_inc(s_ready, 1)

                def normalise(g, par):
                    s = sc[:, :, :]
                    dve.wait_ge(e_ready, count(g + 1))
                    nc.vector.tensor_reduce(sm, s, AX.X, ALU.add).then_inc(sum_ready, 1)
                    dve.wait_ge(sum_ready, count(g + 1))
                    nc.vector.reciprocal(rc, sm).then_inc(inverted, 1)
                    dve.wait_ge(inverted, count(g + 1))
                    for b in range(2):
                        rows = slice(b * 64, b * 64 + 64)
                        m = nc.vector.tensor_tensor(pb[rows, par, :, b], s[rows], wide(rc)[rows], ALU.mult)
                    m.then_inc(p_ready, 1)

                dve.wait_ge(mask_loaded, count(16))
                dve.wait_ge(zeroed, count(1))
                centre(0)
                normalise(0, 0)

                def step(g, par, last):
                    if not last:
                        centre(g + 1)
                    dve.wait_ge(c_mm, count(g + 1))
                    xc = k.x[:, bass.ds(g * GW, GW)]
                    nc.vector.tensor_tensor(xc, xc, k.bank(4), ALU.add).then_inc(x_done, 1)
                    if not last:
                        normalise(g + 1, 1 - par)

                turns(dve, step)


def feed_forward(k, tag, func, chunks, target, out_bias=None, gates=None, tail=None, src=None, store=None):
    nc, n = k.nc, len(chunks)
    src = k.h if src is None else src
    twice = any(c[2] is not None for c in chunks)
    gated = gates is not None
    with Stage(nc) as st:
        h_mm, rest_mm, acted, multiplied, hidden, out_mm, out_done = st.sem(*[f"{tag}_{s}" for s in (
            "h_mm rest_mm acted multiplied hidden out_mm out_done").split()])
        if store is not None:
            stored = st.sem(tag + "_stored")
        a = st.sb(tag + "_activated", [D, 2, GW])
        m1 = st.sb(tag + "_multiplied", [D, 2, GW])
        m2 = st.sb(tag + "_hidden", [D, 2, GW])
        def final(c):
            return a if c[2] is None and c[4] is None else (m2 if c[4] is not None else m1)

        with st.block() as block:
            @block.tensor
            def _(pe):
                def first(g, i):
                    w1, b1, w3, w2, sel = chunks[i]
                    hg = src[:, bass.ds(g * GW, GW)]
                    m = nc.tensor.matmul(k.bank(i % 2), w1, hg)
                    m.then_inc(h_mm, 1)
                    if w3 is not None:
                        m = nc.tensor.matmul(k.bank(2 + i % 2), w3, hg)
                    if sel is not None and (i == 0 or chunks[i - 1][4] != sel):
                        m = nc.tensor.matmul(k.bank(4 + sel % 2), gates.sel[:, sel * 128:sel * 128 + 128],
                                             gates.pieces[:, bass.ds(g * GW, GW)])
                    if w3 is not None or sel is not None:
                        m.then_inc(rest_mm, 1)

                def second(g, i):
                    pe.wait_ge(hidden, count(g * n + i + 1))
                    if i == 0:
                        pe.wait_ge(out_done, count(g))
                    m = nc.tensor.matmul(k.bank(6), chunks[i][3], final(chunks[i])[:, i % 2], start=(i == 0),
                                         stop=(i == n - 1 and tail is None))
                    if i == n - 1:
                        if tail is not None:
                            m = nc.tensor.matmul(k.bank(6), tail, gates.plain[:, bass.ts(g, GW)], start=False, stop=True)
                        m.then_inc(out_mm, 1)

                def group(g, last):
                    for i in range(n):
                        if i + 1 < n:
                            first(g, i + 1)
                        elif not last:
                            first(g + 1, 0)
                        second(g, i)

                first(0, 0)
                with pe.Fori(0, G - 1) as g:
                    group(g, False)
                group(G - 1, True)

            @block.scalar
            def _(act):
                nc.scalar.preload_act_table(func)
                with act.Fori(0, G) as g:
                    for i, (w1, b1, w3, w2, sel) in enumerate(chunks):
                        act.wait_ge(h_mm, count(g * n + i + 1))
                        if b1 is None:
                            ins = nc.scalar.activation(a[:, i % 2], k.bank(i % 2), func)
                        else:
                            ins = nc.scalar.activation(a[:, i % 2], k.bank(i % 2), func, bias=b1)
                        ins.then_inc(hidden if final(chunks[i]) is a else acted, 1)

            if store is not None:
                @block.sync
                def _(sp):
                    with sp.Fori(0, G) as g:
                        c = bass.ts(g, GW)
                        sp.wait_ge(out_done, count(g + 1))
                        nc.sync.dma_start(store[:, c], target[:, c]).then_inc(stored, 16)
                    sp.wait_ge(stored, count(16 * G))

            with_rest = [c[2] is not None or c[4] is not None for c in chunks]
            both = [c[2] is not None and c[4] is not None for c in chunks]

            @block.vector
            def _(dve):
                with dve.Fori(0, G) as g:
                    for i, (w1, b1, w3, w2, sel) in enumerate(chunks):
                        if not with_rest[i]:
                            continue
                        dve.wait_ge(acted, count(g * sum(with_rest) + sum(with_rest[:i]) + 1))
                        dve.wait_ge(rest_mm, count(g * sum(with_rest) + sum(with_rest[:i]) + 1))
                        if w3 is not None:
                            nc.vector.tensor_tensor(m1[:, i % 2], a[:, i % 2], k.bank(2 + i % 2), ALU.mult)\
                                .then_inc(multiplied if both[i] else hidden, 1)
                        if both[i]:
                            dve.wait_ge(multiplied, count(g * sum(both) + sum(both[:i]) + 1))
                        if sel is not None:
                            nc.vector.tensor_tensor(m2[:, i % 2], (m1 if w3 is not None else a)[:, i % 2],
                                                    k.bank(4 + sel % 2), ALU.mult).then_inc(hidden, 1)
                    c = bass.ts(g, GW)
                    dve.wait_ge(out_mm, count(g + 1))
                    if out_bias is not None:
                        nc.vector.scalar_tensor_tensor(target[:, c], k.bank(6), out_bias, target[:, c],
                                                       ALU.add, ALU.add).then_inc(out_done, 1)
                    else:
                        nc.vector.tensor_tensor(target[:, c], target[:, c], k.bank(6), ALU.add).then_inc(out_done, 1)


class Gates:

    def __init__(self, k, tag, E, selectors, stack, plain=False):
        buf = lambda name, shape, dt: stack.enter_context(k.nc.sbuf_tensor(tag + name, shape, dt))
        self.E, self.source = E, k.dram[selectors]
        self.pieces = buf("_gate_pieces", [3 * E, T], BF16)
        self.sel = buf("_selectors", list(self.source.shape), BF16)
        self.plain = buf("_gates", [E, T], F32) if plain else None


def route(k, tag, E, topk, router_w, mode, gates, bias=None, shared=None):
    nc, NT = k.nc, T // 128
    with Stage(nc) as st:
        logits_mm, exp_in, exp_out, turned, plain_turned, sel_loaded, ident_ready, ready, step = st.sem(
            *[f"{tag}_{s}" for s in ("logits_mm exp_in exp_out turned plain_turned sel_loaded ident_ready ready step").split()])
        lg = k.bank(0, NT * E).rearrange("p (t e) -> p t e", e=E)
        val = st.sb(tag + "_values", [128, NT, E])
        wgt = st.sb(tag + "_weights", [128, NT, E])
        chosen = st.sb(tag + "_chosen", [128, NT, E])
        one = st.sb(tag + "_one", [128, 2, NT])
        marks = st.sb(tag + "_marks", [128, 2, NT, E])
        rest = st.sb(tag + "_rest", [128, 2, NT, E])
        pieces = st.sb(tag + "_pieces", [128, NT, 3, E], BF16)
        ident = st.sb(tag + "_identity", [128, 128], BF16)
        sel = st.sb(tag + "_selectors", list(gates.source.shape))
        if mode == "groups":
            NG, EG = 4, 4
            pair = st.sb(tag + "_pair", [128, NT, NG, 6])
            gs = st.sb(tag + "_group_score", [128, NT, NG])
            gsel = st.sb(tag + "_group_chosen", [128, NT, NG])

        if shared:
            gate_mm, up_mm, gate_sb, up_sb, hidden, down_mm, out_sb, added = st.sem(*[f"{tag}_{s}" for s in (
                "gate_mm up_mm gate_sb up_sb hidden down_mm out_sb added").split()])
            ga = st.sb(tag + "_shared_gate", [D, 2, GW])
            up = st.sb(tag + "_shared_up", [D, 2, GW])
            hid = st.sb(tag + "_shared_hidden", [D, 2, GW])
            so = st.sb(tag + "_shared_out", [D, GW])

        def pairs_of_chunks(eng, chunk, close):
            chunk(0, 0)
            with eng.Fori(0, G - 1) as g:
                chunk(g, 1)
                close(g, 0)
                chunk(g + 1, 0)
                close(g, 1)
            chunk(G - 1, 1)
            close(G - 1, 0)
            close(G - 1, 1)

        with st.block() as block:
            @block.tensor
            def _(pe):
                for t in range(NT):
                    m = nc.tensor.matmul(lg[:, t, :], k.h[:, t * 128:t * 128 + 128], router_w)
                m.then_inc(logits_mm, 1)
                if shared:
                    def up_and_gate(g, i):
                        hg = k.h[:, bass.ds(g * GW, GW)]
                        nc.tensor.matmul(k.bank(1 + i), shared[i][0], hg).then_inc(gate_mm, 1)
                        nc.tensor.matmul(k.bank(3 + i), shared[i][1], hg).then_inc(up_mm, 1)

                    def down(g, i):
                        if i == 0:
                            pe.wait_ge(out_sb, count(g))
                        pe.wait_ge(hidden, count(g * 2 + (i + 1)))
                        nc.tensor.matmul(k.bank(5), shared[i][2], hid[:, i], start=(i == 0), stop=(i == 1)).then_inc(down_mm, 1)

                    pairs_of_chunks(pe, up_and_gate, down)
                    pe.wait_ge(out_sb, count(G))
                pe.wait_ge(ident_ready, count(1))
                pe.wait_ge(ready, count(1))
                for t in range(NT):
                    m = nc.tensor.matmul(k.ps[0:3 * E, t * 128:t * 128 + 128],
                                         pieces[:, t].rearrange("p n e -> p (n e)"), ident[:, :])
                    if t % TPG == TPG - 1:
                        m.then_inc(turned, 1)
                if gates.plain is not None:
                    for t in range(NT):
                        if t % TPG == 0:
                            pe.wait_ge(plain_turned, count(t // TPG + 1))
                        m = nc.tensor.transpose(k.ps[0:E, t * 128:t * 128 + 128], wgt[:, t, :], k.w("c_ident"))
                        if t % TPG == TPG - 1:
                            m.then_inc(turned, 1)

            @block.sync
            def _(sp):
                nc.sync.dma_start(sel[:, :], gates.source).then_inc(sel_loaded, 16)

            @block.gpsimd
            def _(pool):
                nc.gpsimd.tensor_copy(ident[:, :], k.w("c_ident")).then_inc(ident_ready, 1)
                if shared:
                    def multiply(g, i):
                        pool.wait_ge(down_mm, count(g * 2))
                        pool.wait_ge(gate_sb, count(g * 2 + (i + 1)))
                        pool.wait_ge(up_sb, count(g * 2 + (i + 1)))
                        nc.gpsimd.tensor_tensor(hid[:, i], ga[:, i], up[:, i], ALU.mult).then_inc(hidden, 1)

                    def add(g, i):
                        if i == 1:
                            pool.wait_ge(out_sb, count(g + 1))
                            xc = k.x[:, bass.ds(g * GW, GW)]
                            nc.gpsimd.tensor_tensor(xc, xc, so[:, :], ALU.add).then_inc(added, 1)

                    pairs_of_chunks(pool, multiply, add)
                pool.wait_ge(sel_loaded, count(16))
                nc.gpsimd.tensor_copy(gates.sel[:, :], sel[:, :])

            @block.scalar
            def _(act):
                act.wait_ge(exp_in, count(1))
                nc.scalar.activation(wgt[:, :, :], wgt[:, :, :], ACT.Exp,
                                     scale=-1.0 if mode == "groups" else 1.0).then_inc(exp_out, 1)
                if shared:
                    def copy_chunk(g, i):
                        act.wait_ge(hidden, count(g * 2))
                        act.wait_ge(gate_mm, count(g * 2 + (i + 1)))
                        nc.scalar.activation(ga[:, i], k.bank(1 + i), ACT.Silu).then_inc(gate_sb, 1)
                        act.wait_ge(up_mm, count(g * 2 + (i + 1)))
                        nc.scalar.copy(up[:, i], k.bank(3 + i)).then_inc(up_sb, 1)

                    def copy_out(g, i):
                        if i == 1:
                            act.wait_ge(added, count(g))
                            act.wait_ge(down_mm, count(g * 2 + 2))
                            nc.scalar.copy(so[:, :], k.bank(5)).then_inc(out_sb, 1)

                    nc.scalar.preload_act_table(ACT.Silu)
                    pairs_of_chunks(act, copy_chunk, copy_out)
                for g in range(G):
                    act.wait_ge(turned, count(g + 1))
                    nc.scalar.copy(gates.pieces[:, g * GW:g * GW + GW], k.bank(g)[0:3 * E, :]).then_inc(plain_turned, 1)
                if gates.plain is not None:
                    for g in range(G):
                        act.wait_ge(turned, count(G + g + 1))
                        nc.scalar.copy(gates.plain[:, g * GW:g * GW + GW], k.bank(g)[0:E, :])

            @block.vector
            def _(dve):
                ch = Chain(dve, step)
                over = lambda a: a.unsqueeze(2).broadcast_to([128, NT, E])
                mx, rc = one[:, 0], one[:, 1]

                def choose(v, n, topk, out):
                    m0, m1 = marks[:, 0, :, 0:n], marks[:, 1, :, 0:n]
                    wide = lambda a: a.unsqueeze(2).broadcast_to([128, NT, n])
                    for i in range(topk):
                        ch.link(nc.vector.tensor_reduce(mx, v, AX.X, ALU.max))
                        ch.link(nc.vector.tensor_tensor(m0, v, wide(mx), ALU.is_equal))
                        ch.link(nc.vector.tensor_tensor(m0, m0, k.w("c_falling")[:, S - n:S].unsqueeze(1)
                                                        .broadcast_to([128, NT, n]), ALU.mult))
                        ch.link(nc.vector.tensor_reduce(mx, m0, AX.X, ALU.max))
                        pick = out if i == 0 else m1
                        ch.link(nc.vector.tensor_tensor(pick, m0, wide(mx), ALU.is_equal))
                        if i < topk - 1:
                            ch.link(nc.vector.scalar_tensor_tensor(v, pick, LOWEST, v, ALU.mult, ALU.add))
                        if i:
                            ch.link(nc.vector.tensor_tensor(out, out, m1, ALU.add))

                dve.wait_ge(logits_mm, count(1))
                if mode == "groups":
                    nc.vector.tensor_copy(wgt[:, :, :], lg).then_inc(exp_in, 1)
                    dve.wait_ge(exp_out, count(1))
                    ch.link(nc.vector.tensor_scalar(wgt[:, :, :], wgt[:, :, :], 1.0, None, ALU.add))
                    ch.link(nc.vector.reciprocal(wgt[:, :, :], wgt[:, :, :]))
                    ch.link(nc.vector.tensor_tensor(val[:, :, :], wgt[:, :, :], bias.unsqueeze(1)
                                                    .broadcast_to([128, NT, E]), ALU.add))
                    v4 = val[:, :, :].rearrange("p t (g e) -> p t g e", g=NG)
                    pairs = [(a, b) for a in range(EG) for b in range(a + 1, EG)]
                    for i, (a, b) in enumerate(pairs):
                        ins = nc.vector.tensor_tensor(pair[:, :, :, i], v4[:, :, :, a], v4[:, :, :, b], ALU.add)
                    ch.link(ins)
                    ch.link(nc.vector.tensor_reduce(gs[:, :, :], pair[:, :, :, :], AX.X, ALU.max))
                    choose(gs[:, :, :], NG, 2, gsel[:, :, :])
                    ch.link(nc.vector.tensor_scalar(gs[:, :, :], gsel[:, :, :], -1.0, None, ALU.add))
                    gb = gsel[:, :, :].unsqueeze(3).broadcast_to([128, NT, NG, EG])
                    ch.link(nc.vector.tensor_tensor(v4, v4, gb, ALU.mult))
                    ch.link(nc.vector.tensor_tensor(v4, v4, gs[:, :, :].unsqueeze(3).broadcast_to(
                        [128, NT, NG, EG]), ALU.add))
                else:
                    ch.link(nc.vector.tensor_reduce(mx, lg, AX.X, ALU.max))
                    nc.vector.tensor_tensor(wgt[:, :, :], lg, over(mx), ALU.subtract).then_inc(exp_in, 1)
                    if mode == "logits":
                        ch.link(nc.vector.tensor_copy(val[:, :, :], lg))
                    dve.wait_ge(exp_out, count(1))
                    if mode == "probs":
                        ch.link(nc.vector.tensor_reduce(mx, wgt[:, :, :], AX.X, ALU.add))
                        ch.link(nc.vector.reciprocal(rc, mx))
                        ch.link(nc.vector.tensor_tensor(wgt[:, :, :], wgt[:, :, :], over(rc), ALU.mult))
                        ch.link(nc.vector.tensor_copy(val[:, :, :], wgt[:, :, :]))
                choose(val[:, :, :], E, topk, chosen[:, :, :])
                ch.link(nc.vector.tensor_tensor(wgt[:, :, :], wgt[:, :, :], chosen[:, :, :], ALU.mult))
                ch.link(nc.vector.tensor_reduce(mx, wgt[:, :, :], AX.X, ALU.add))
                if mode == "groups":
                    ch.link(nc.vector.tensor_scalar(mx, mx, 1e-20, None, ALU.add))
                ch.link(nc.vector.reciprocal(rc, mx))
                if mode != "probs":
                    ch.link(nc.vector.tensor_scalar(rc, rc, 2.5 if mode == "groups" else 0.5, None, ALU.mult))
                ch.link(nc.vector.tensor_tensor(wgt[:, :, :], wgt[:, :, :], over(rc), ALU.mult))
                ch.link(nc.vector.tensor_copy(pieces[:, :, 0], wgt[:, :, :]))
                ch.link(nc.vector.tensor_tensor(rest[:, 0], wgt[:, :, :], pieces[:, :, 0], ALU.subtract))
                ch.link(nc.vector.tensor_copy(pieces[:, :, 1], rest[:, 0]))
                ch.link(nc.vector.tensor_tensor(rest[:, 1], rest[:, 0], pieces[:, :, 1], ALU.subtract))
                nc.vector.tensor_copy(pieces[:, :, 2], rest[:, 1]).then_inc(ready, 1)


def l0_ffn(k):
    layer_norm(k, k.x, k.h, "l0f_ln")
    feed_forward(k, "l0f", ACT.Relu, [(k.w(f"l0f_w1_{i}"), k.w(f"l0f_b1_{i}"), None, k.w(f"l0f_w2_{i}"), None)
                                      for i in range(4)], k.h, out_bias=k.w("l0f_b2"))
    layer_norm(k, k.h, k.h, "l0f_ln2", gain=k.w("l0f_gamma"), bias=k.w("l0f_beta"), add_to=k.x)


def l1_ffn(k):
    layer_norm(k, k.x, k.h, "l1f_ln")
    with ExitStack() as stack:
        gates = Gates(k, "l1f", 8, "sel_l1", stack, plain=True)
        route(k, "l1f_route", 8, 2, k.w("l1f_gate"), "logits", gates)
        feed_forward(k, "l1f", ACT.Relu, [(k.w(f"l1f_wd_{i}"), k.w(f"l1f_bd_{i}"), None, k.w(f"l1f_wu_{i}"), i)
                                          for i in range(4)], k.x, gates=gates, tail=k.w("l1f_bu"))


def l2_ffn(k):
    layer_norm(k, k.x, k.h, "l2f_ln")
    with ExitStack() as stack:
        gates = Gates(k, "l2f", 8, "sel_l2", stack)
        route(k, "l2f_route", 8, 2, k.w("l2f_gate"), "probs", gates)
        feed_forward(k, "l2f", ACT.Silu, [(k.w(f"l2f_w1_{i}"), None, k.w(f"l2f_w3_{i}"), k.w(f"l2f_w2_{i}"), i // 2)
                                          for i in range(16)], k.x, gates=gates)


def l3_ffn(k, out):
    layer_norm(k, k.x, k.h, "l3f_ln")
    with ExitStack() as stack:
        gates = Gates(k, "l3f", 16, "sel_l3", stack)
        route(k, "l3f_route", 16, 4, k.w("l3f_router"), "groups", gates, bias=k.w("l3f_bias"),
              shared=[(k.w(f"l3f_sg_{i}"), k.w(f"l3f_su_{i}"), k.w(f"l3f_sd_{i}")) for i in range(2)])
        chunks = [(k.w(f"l3f_g_{i}"), None, k.w(f"l3f_u_{i}"), k.w(f"l3f_d_{i}"), i) for i in range(16)]
        feed_forward(k, "l3f", ACT.Silu, chunks, k.x, gates=gates, store=out)


def l1_attn(k):
    nc, tag = k.nc, "l1a"
    TURNS = G // 2
    layer_norm(k, k.x, k.h, "l1a_ln")
    with Stage(nc) as st:
        (zeroed, q_mm, k_mm, q_relu, k_relu, q_plus, k_plus, k_spread, scanned, dk_ready, den_mm, maxed,
         rd_ready, bias_ready, s_mm, a_ready, staged, v_mm, v_sb, n_mm, c_raw, c_ready, o_mm, x_done) = st.sem(*["l1a_" + n for n in (
             "zeroed q_mm k_mm q_relu k_relu q_plus k_plus k_spread scanned dk_ready den_mm maxed "
             "rd_ready bias_ready s_mm a_ready staged v_mm v_sb n_mm c_raw c_ready o_mm x_done").split()])
        qr = st.sb("l1a_q_relu", [D, GW])
        kr = st.sb("l1a_k_relu", [D, GW])
        qf = st.sb("l1a_q", [D, GW])
        kf = st.sb("l1a_k", [D, GW])
        kc = st.sb("l1a_k_running_sum", [D, GW])
        dk = st.sb("l1a_q_times_sum", [D, GW])
        rd = st.sb("l1a_one_over_sum", [D, GW])
        cf = st.sb("l1a_context", [D, GW])
        bias = st.sb("l1a_value_bias", [D, GW])
        qe = st.sb("l1a_q_spread", [D, 2, GW // S, 2, S])
        ke = st.sb("l1a_k_spread", [D, 2, GW // S, 2, S])
        twice = st.sb("l1a_source_twice", [D, GW // S, 2, S])
        ve = st.sb("l1a_values_spread", [128, GW // S, 2, D])
        am = st.sb("l1a_weights", [128, 2, H, S])
        scores = k.ps[:, 2 * 512:6 * 512].rearrange("p (r c) -> p r c", r=NQ)[:, :, 0:NQ * S]

        def turns(eng, step):
            with eng.Fori(0, TURNS - 1) as it:
                for m in range(2 * TPG):
                    step(it * 2 + m // TPG, m // TPG, m % TPG, False)
            for m in range(2 * TPG):
                step((TURNS - 1) * 2 + m // TPG, m // TPG, m % TPG, m >= TPG)

        with st.block() as block:
            @block.gpsimd
            def _(pool):
                def stage(g, half):
                    c = bass.ds(g * GW + half * (GW // 2), GW // 2)
                    nc.gpsimd.tensor_copy(twice[:, 4 * half:4 * half + 4], k.h[:, c].rearrange("p (b s) -> p b s", s=S)
                                          .unsqueeze(2).broadcast_to([D, 4, 2, S])).then_inc(staged, 1)

                nc.gpsimd.memset(ve[:, :, :, :], 0.0).then_inc(zeroed, 1)
                stage(0, 0)
                stage(0, 1)

                def step(g, j, u, last):
                    if last:
                        return
                    if u == 1:
                        pool.wait_ge(v_mm, count(g * 2 + 1))
                        stage(g + 1, 0)
                    if u == 2:
                        pool.wait_ge(v_mm, count(g * 2 + 2))
                        stage(g + 1, 1)

                turns(pool, step)

            @block.tensor
            def _(pe):
                def weights(n, g, j, t):
                    if t == 0:
                        pe.wait_ge(k_spread, count(g + 1))
                    pe.wait_ge(a_ready, count(n))
                    for b in range(2):
                        for r in range(NQ):
                            f = slice(32 * r, 32 * r + 32)
                            x = nc.tensor.matmul(scores[:, r, b * 2 * S:(b + 1) * 2 * S],
                                                 ke[f, j, t * 2 + b].rearrange("p h s -> p (h s)"),
                                                 qe[f, j, t * 2 + b].rearrange("p h s -> p (h s)"),
                                                 tile_position=(32 * r, 0))
                    x.then_inc(s_mm, 1)

                def values(n, g, t):
                    if t == 0:
                        pe.wait_ge(v_sb, count(g * 2 + 1))
                        pe.wait_ge(c_ready, count(g))
                    if t == 2:
                        pe.wait_ge(v_sb, count(g * 2 + 2))
                    pe.wait_ge(a_ready, count(n + 1))
                    for b in range(2):
                        for r in range(NQ):
                            f = slice(32 * r, 32 * r + 32)
                            for h in range(2):
                                x = nc.tensor.matmul(
                                    k.bank(1)[f, t * 128 + b * 64:t * 128 + b * 64 + 64],
                                    ve[:, t * 2 + b, h, f], am[:, t % 2, 4 * r + 2 * b + h],
                                    start=(h == 0), stop=(h == 1), tile_position=(0, 32 * r))
                    x.then_inc(n_mm, 1)

                def query(g):
                    nc.tensor.matmul(k.bank(0), k.w("l1a_wq"), k.h[:, bass.ds(g * GW, GW)]).then_inc(q_mm, 1)

                def key(g):
                    nc.tensor.matmul(k.bank(7), k.w("l1a_wk"), k.h[:, bass.ds(g * GW, GW)]).then_inc(k_mm, 1)

                def value(g, half):
                    pe.wait_ge(k_relu if half else q_relu, count(g + 1))
                    pe.wait_ge(staged, count(g * 2 + (half + 1)))
                    for b in range(4):
                        x = nc.tensor.matmul(k.bank(7 if half else 0)[:, b * D:b * D + D],
                                             twice[:, 4 * half + b].rearrange("p c s -> p (c s)"), k.w("l1a_wv"))
                    x.then_inc(v_mm, 1)

                query(0)
                key(0)
                value(0, 0)
                value(0, 1)
                weights(0, 0, 0, 0)

                def step(g, j, u, last):
                    n = g * TPG + u
                    if not (last and u == TPG - 1):
                        weights(n + 1, g + (u + 1) // TPG, (j + (u + 1) // TPG) % 2, (u + 1) % TPG)
                    if u == 0:
                        pe.wait_ge(x_done, count(g))
                        pe.wait_ge(dk_ready, count(g + 1))
                        nc.tensor.matmul(k.bank(6), k.w("c_heads"), dk[:, :]).then_inc(den_mm, 1)
                    values(n, g, u)
                    if not last:
                        if u == 0:
                            query(g + 1)
                        if u == 1:
                            pe.wait_ge(v_sb, count(g * 2 + 2))
                            key(g + 1)
                        if u >= 2:
                            value(g + 1, u - 2)
                    if u == TPG - 1:
                        pe.wait_ge(c_ready, count(g + 1))
                        nc.tensor.matmul(k.bank(6), k.w("l1a_wo"), cf[:, :]).then_inc(o_mm, 1)

                turns(pe, step)

            @block.scalar
            def _(act):
                def query(g, j):
                    act.wait_ge(q_mm, count(g + 1))
                    nc.scalar.activation(qr[:, :], k.bank(0), ACT.Relu, bias=k.w("l1a_bq")).then_inc(q_relu, 1)
                    act.wait_ge(q_plus, count(g + 1))
                    spread(qe[:, j], qf, k.w("c_by_h"))

                def key(g, j):
                    act.wait_ge(k_mm, count(g + 1))
                    nc.scalar.activation(kr[:, :], k.bank(7), ACT.Relu, bias=k.w("l1a_bk")).then_inc(k_relu, 1)
                    act.wait_ge(k_plus, count(g + 1))
                    spread(ke[:, j], kf, k.w("c_by_p")).then_inc(k_spread, 1)

                def spread(out, f, mask):
                    for i in range(2):
                        x = nc.scalar.mul(out[:, :, i], f[:, :].rearrange("p (b s) -> p b s", s=S), mask[:, i:i + 1])
                    return x

                def value(g, half):
                    act.wait_ge(v_mm, count(g * 2 + (half + 1)))
                    for p in range(2):
                        rows = slice(64 * p, 64 * p + 64)
                        for h in range(2):
                            f = lambda a: a.rearrange("p b (r n e) -> p b r n e", r=NQ, n=NQ)[:, :, :, 2 * p + h]
                            x = nc.scalar.copy(f(ve[rows, 4 * half:4 * half + 4, h]),
                                               f(k.bank(7 if half else 0)[rows].rearrange("p (b d) -> p b d", d=D)))
                    x.then_inc(v_sb, 1)

                query(0, 0)
                key(0, 0)
                act.wait_ge(zeroed, count(1))
                value(0, 0)
                value(0, 1)

                def step(g, j, u, last):
                    if not last:
                        if u == 0:
                            query(g + 1, (j + 1) % 2)
                        if u == 1:
                            key(g + 1, (j + 1) % 2)
                        if u >= 2:
                            value(g + 1, u - 2)

                turns(act, step)

            @block.vector
            def _(dve):
                causal = k.w("c_causal").unsqueeze(1).unsqueeze(1).broadcast_to([128, NQ, NQ, S])

                def mask(n, t):
                    dve.wait_ge(s_mm, count(n + 1))
                    nc.vector.tensor_tensor(am[:, t % 2].rearrange("p (r h) s -> p r h s", r=NQ),
                                            scores.rearrange("p r (h s) -> p r h s", s=S), causal,
                                            ALU.mult).then_inc(a_ready, 1)

                def query_plus(g):
                    dve.wait_ge(q_relu, count(g + 1))
                    nc.vector.tensor_scalar(qf[:, :], qr[:, :], 1e-6, None, ALU.add).then_inc(q_plus, 1)

                def key_plus(g):
                    dve.wait_ge(k_relu, count(g + 1))
                    nc.vector.tensor_scalar(kf[:, :], kr[:, :], 1e-6, None, ALU.add).then_inc(k_plus, 1)

                def running_sum(g):
                    dve.wait_ge(k_plus, count(g + 1))
                    nc.vector.tensor_tensor_scan(kc[:, :], k.w("c_restart"), kf[:, :], 0.0, ALU.mult, ALU.add)\
                        .then_inc(scanned, 1)
                    dve.wait_ge(scanned, count(g + 1))
                    nc.vector.tensor_tensor(dk[:, :], qf[:, :], kc[:, :], ALU.mult).then_inc(dk_ready, 1)

                query_plus(0)
                key_plus(0)
                running_sum(0)
                mask(0, 0)

                def step(g, j, u, last):
                    n = g * TPG + u
                    if u == 1 and not last:
                        dve.wait_ge(k_spread, count(g + 1))
                        query_plus(g + 1)
                    if u == 2 and not last:
                        key_plus(g + 1)
                    if not (last and u == TPG - 1):
                        mask(n + 1, (u + 1) % TPG)
                    if u == 0:
                        dve.wait_ge(den_mm, count(g + 1))
                        nc.vector.tensor_scalar(rd[:, :], k.bank(6), 1e-6, None, ALU.max).then_inc(maxed, 1)
                        dve.wait_ge(maxed, count(g + 1))
                        nc.vector.reciprocal(rd[:, 0:GW // 2], rd[:, 0:GW // 2])
                    if u == 1:
                        nc.vector.reciprocal(rd[:, GW // 2:GW], rd[:, GW // 2:GW]).then_inc(rd_ready, 1)
                    if u == 2:
                        dve.wait_ge(rd_ready, count(g + 1))
                        nc.vector.scalar_tensor_tensor(bias[:, :], k.bank(6), k.w("l1a_bv"), rd[:, :],
                                                       ALU.mult, ALU.mult).then_inc(bias_ready, 1)
                    if u == 2 and not last:
                        running_sum(g + 1)
                    if u == TPG - 1:
                        dve.wait_ge(bias_ready, count(g + 1))
                        dve.wait_ge(n_mm, count(n + 1))
                        nc.vector.tensor_tensor(cf[:, :], k.bank(1), rd[:, :], ALU.mult).then_inc(c_raw, 1)
                        dve.wait_ge(c_raw, count(g + 1))
                        nc.vector.tensor_tensor(cf[:, :], cf[:, :], bias[:, :], ALU.add).then_inc(c_ready, 1)
                        dve.wait_ge(o_mm, count(g + 1))
                        xc = k.x[:, bass.ds(g * GW, GW)]
                        nc.vector.scalar_tensor_tensor(xc, k.bank(6), k.w("l1a_bo"), xc, ALU.add, ALU.add)\
                            .then_inc(x_done, 1)

                turns(dve, step)


def l1_xattn(k):
    nc = k.nc
    rel = nc.dram_tensor("relative_scores", (T, H * S), F32, kind="Internal").ap()
    rel_rows = rel.rearrange("(b s) n -> s b n", s=S)
    layer_norm(k, k.x, k.h, "l1x_ln")
    R = 2 * S - 1
    PAIRS = S // 2
    with Stage(nc) as st:
        q_mm, q_ready, table_loaded, mask_loaded, mask_scaled = st.sem(
            "l1r_q_mm", "l1r_q_ready", "l1r_table_loaded", "l1r_mask_loaded", "l1r_mask_scaled")
        staged = st.sem("l1r_staged0", "l1r_staged1")
        r_mm = st.sem("l1r_mm0", "l1r_mm1")
        rows_ready = st.sem("l1r_rows0", "l1r_rows1")
        stored = st.sem("l1r_stored0", "l1r_stored1")
        qf = st.sb("l1r_q", [D, T])
        table = st.sb("l1r_table", [D, H, R])
        qs = st.sb("l1r_q_positions", [D, 2, 2, B])
        rs = st.sb("l1r_rows", [2 * B, 2, H * S])
        mask = st.sb("l1r_mask", [2 * B, S])
        with st.block() as block:
            @block.sync
            def _(sp):
                nc.sync.dma_start(table[:, :, :].rearrange("p h r -> p (h r)"), k.dram["rel_in"]).then_inc(table_loaded, 16)
                for i in range(2):
                    nc.sync.dma_start(mask[i * B:(i + 1) * B, :], k.dram["mask_in"]).then_inc(mask_loaded, 16)
                with sp.Fori(0, PAIRS // 2) as i:
                    for p in range(2):
                        for pos in range(2):
                            sp.wait_ge(rows_ready[p], count(i + 1))
                            nc.sync.dma_start(rel_rows[bass.ds(i * 4 + (2 * p + pos), 1)].rearrange("s b n -> (s b) n"),
                                              rs[pos * B:(pos + 1) * B, p]).then_inc(stored[p], 16)
                for p in range(2):
                    sp.wait_ge(stored[p], count(16 * PAIRS))

            @block.gpsimd
            def _(pool):
                pool.wait_ge(q_ready, count(G))
                q3 = qf[:, :].rearrange("p (b s) -> p s b", s=S)
                with pool.Fori(0, PAIRS // 2) as i:
                    for p in range(2):
                        pool.wait_ge(r_mm[p], count(i))
                        nc.gpsimd.tensor_copy(qs[:, p], q3[:, bass.ds(i * 4 + 2 * p, 2), :]).then_inc(staged[p], 1)

            @block.tensor
            def _(pe):
                for g in range(G):
                    nc.tensor.matmul(k.bank(g), k.w("l1x_wq"), k.h[:, g * GW:g * GW + GW]).then_inc(q_mm, 1)
                pe.wait_ge(q_ready, count(G))
                pe.wait_ge(table_loaded, count(16))
                for i in range(PAIRS // 2):
                    for p in range(2):
                        pe.wait_ge(staged[p], count(i + 1))
                        pe.wait_ge(rows_ready[p], count(i))
                        for half in range(2):
                            for pos in range(2):
                                first = S - 1 - (4 * i + 2 * p + pos)
                                m = nc.tensor.matmul(k.bank(2 * p + half)[pos * B:(pos + 1) * B, :], qs[:, p, pos],
                                                     table[:, 8 * half:8 * half + 8, first:first + S],
                                                     tile_position=(0, 64 * pos))
                        m.then_inc(r_mm[p], 1)

            @block.vector
            def _(dve):
                for g in range(G):
                    dve.wait_ge(q_mm, count(g + 1))
                    nc.vector.tensor_scalar(qf[:, g * GW:g * GW + GW], k.bank(g), k.w("l1x_bq"), None, ALU.add)\
                        .then_inc(q_ready, 1)
                dve.wait_ge(mask_loaded, count(32))
                nc.vector.tensor_scalar(mask[:, :], mask[:, :], float(DH) ** 0.5, None, ALU.mult).then_inc(mask_scaled, 1)
                dve.wait_ge(mask_scaled, count(1))
                with dve.Fori(0, PAIRS // 2) as i:
                    for p in range(2):
                        dve.wait_ge(stored[p], count(i * 32))
                        dve.wait_ge(r_mm[p], count(i + 1))
                        nc.vector.tensor_tensor(rs[:, p].rearrange("b (h s) -> b h s", s=S),
                                                k.ps[:, 2 * p * 512:(2 * p + 2) * 512].rearrange("b (h s) -> b h s", s=S),
                                                mask[:, :].unsqueeze(1).broadcast_to([2 * B, H, S]), ALU.add)\
                            .then_inc(rows_ready[p], 1)
    softmax_attention(k, "l1x", ("l1x_wq", "l1x_bq"), [(k.ctx, "l1x_wk", "l1x_bk", "l1x_wv", "l1x_bv", None)],
                      rel=rel, normed=True)


def l2_attn(k):
    nc = k.nc
    SIGMA, MU = 0.282095, 0.707107
    layer_norm(k, k.x, k.h, "l2a_ln")
    with ExitStack() as outer:
        xn = outer.enter_context(nc.sbuf_tensor("l2a_xn", [D, T], F32))
        mx = outer.enter_context(nc.sbuf_tensor("l2a_averaged", [D, T], F32))
        bias = outer.enter_context(nc.sbuf_tensor("l2a_bias", [128, S], F32))
        hb = outer.enter_context(nc.sbuf_tensor("l2a_hx_bias", [D, 2], F32))
        layer_norm(k, k.h, xn, "l2a_ln2", gain=k.w("l2a_ln_w"), bias=k.w("l2a_ln_b"))
        with Stage(nc) as st:
            step, act_step, bias_in, bias_mm, kern_in, kern_ready, dve_averaged, pe_averaged, diag_ready, diag_used \
                = st.sem(*["l2e_" + n for n in ("step act_step bias_in bias_mm kern_in kern_ready dve_averaged "
                                                "pe_averaged diag_ready diag_used").split()])
            N = 16
            sm = st.sb("l2e_small", [D, 4, N])
            pw = st.sb("l2e_powers", [D, N, S])
            kern = st.sb("l2e_kernel", [D, S])
            rot = st.sb("l2e_rotary", [D, 3, 128])
            p_, a_, lq, cf = (sm[:, i] for i in range(4))
            DIAGS = 4
            diag = st.sb("l2e_diagonals", [D, DIAGS, D])
            PE_BANKS = (7, 6)
            DVE_PARTS = ((0, 6 * GW),)
            with st.block() as block:
                @block.scalar
                def _(act):
                    act.wait_ge(kern_in, count(1))
                    nc.scalar.preload_act_table_set("natural_log_exp_and_others")
                    nc.scalar.activation(sm[:, 0:2], k.w("l2a_delta_alpha").rearrange("p (a n) -> p a n", a=2),
                                         ACT.Exp, scale=-1.0).then_inc(act_step, 1)
                    act.wait_ge(kern_in, count(2))
                    nc.scalar.activation(lq, lq, ACT.Ln).then_inc(act_step, 1)
                    act.wait_ge(kern_in, count(3))
                    nc.scalar.activation(pw[:, :, :], pw[:, :, :], ACT.Exp).then_inc(act_step, 1)
                    act.wait_ge(kern_ready, count(1))
                    for j in range(S):
                        if j >= DIAGS:
                            act.wait_ge(diag_used, count(j - DIAGS + 1))
                        nc.scalar.mul(diag[:, j % DIAGS], k.w("c_ident"), kern[:, j:j + 1]).then_inc(diag_ready, 1)
                    act.wait_ge(dve_averaged, count(len(DVE_PARTS)))
                    act.wait_ge(pe_averaged, count(1))
                    for g in range(G):
                        nc.scalar.activation(mx[:, g * GW:g * GW + GW], k.bank(g), ACT.Silu)

                @block.tensor
                def _(pe):
                    pe.wait_ge(bias_in, count(1))
                    nc.tensor.matmul(k.bank(7, S), rot[:, 2], rot[:, 0, 0:S]).then_inc(bias_mm, 1)
                    for j in range(S):
                        pe.wait_ge(diag_ready, count(j + 1))
                        for g in PE_BANKS:
                            first = max(g * GW, j * S)
                            if first < (g + 1) * GW:
                                m = nc.tensor.matmul(k.ps[:, first:(g + 1) * GW], diag[:, j % DIAGS],
                                                     xn[:, first - j * S:(g + 1) * GW - j * S],
                                                     start=(j == 0), stop=(j * S >= g * GW + GW - S))
                        m.then_inc(diag_used if j < S - 1 else pe_averaged, 1)

                @block.vector
                def _(dve):
                    ch = Chain(dve, step)
                    nc.vector.tensor_scalar(hb[:, 1:2], k.w("l2a_bmx0"), 0.5, None, ALU.mult)
                    nc.vector.tensor_tensor(hb[:, 0:1], k.w("l2a_bmx4"), k.w("l2a_bh"), ALU.add).then_inc(kern_in, 1)
                    for i, (a, s) in enumerate((("l2a_ra", "l2a_ras"), ("l2a_rb", "l2a_rbs"))):
                        ch.link(nc.vector.tensor_scalar(rot[:, 1, :], k.w("c_sin"), k.w(s), None, ALU.mult))
                        m = nc.vector.scalar_tensor_tensor(rot[:, 2 * i, :], k.w("c_cos"), k.w(a), rot[:, 1, :],
                                                           ALU.mult, ALU.add)
                        if i == 0:
                            ch.link(m)
                    m.then_inc(bias_in, 1)
                    dve.wait_ge(act_step, count(1))
                    ch.link(nc.vector.tensor_scalar(sm[:, 0:2], sm[:, 0:2], 1.0, None, ALU.add))
                    ch.link(nc.vector.reciprocal(sm[:, 0:2], sm[:, 0:2]))
                    ch.link(nc.vector.tensor_tensor(lq, p_, a_, ALU.mult))
                    nc.vector.tensor_scalar(lq, lq, -1.0, 1.0, ALU.mult, ALU.add).then_inc(kern_in, 1)
                    dve.wait_ge(bias_mm, count(1))
                    ch.link(nc.vector.tensor_scalar(bias[:, :], k.bank(7, S), -MU, 1.0 / SIGMA, ALU.add, ALU.mult))
                    ch.link(nc.vector.tensor_tensor(cf, p_, k.w("l2a_beta"), ALU.mult))
                    ch.link(nc.vector.scalar_tensor_tensor(cf, k.w("l2a_gamma"), float(N) ** -0.5, cf, ALU.mult, ALU.mult))
                    dve.wait_ge(act_step, count(2))
                    nc.vector.tensor_tensor(pw[:, :, :], lq.unsqueeze(2).broadcast_to([D, N, S]),
                                            k.w("c_pos").unsqueeze(1).broadcast_to([D, N, S]), ALU.mult)\
                        .then_inc(kern_in, 1)
                    dve.wait_ge(act_step, count(3))
                    ch.link(nc.vector.tensor_tensor(pw[:, :, :], pw[:, :, :], cf.unsqueeze(2).broadcast_to([D, N, S]),
                                                    ALU.mult))
                    ch.link(nc.vector.tensor_reduce(kern[:, :], pw[:, :, :].rearrange("p n s -> p s n"), AX.X, ALU.add))
                    nc.vector.tensor_tensor(kern[:, 0:1], kern[:, 0:1], k.w("l2a_omega"), ALU.add).then_inc(kern_ready, 1)
                    dve.wait_ge(kern_ready, count(1))
                    for i, (start, end) in enumerate(DVE_PARTS):
                        for j in range(end // S):
                            c = max(start, j * S)
                            o, src = k.ps[:, c:end], xn[:, c - j * S:end - j * S]
                            if j == 0:
                                ch.link(nc.vector.tensor_scalar(o, src, kern[:, 0:1], None, ALU.mult))
                            else:
                                m = nc.vector.scalar_tensor_tensor(o, src, kern[:, j:j + 1], o, ALU.mult, ALU.add)
                                if j < end // S - 1:
                                    ch.link(m)
                        m.then_inc(dve_averaged, 1)
        with Stage(nc) as st:
            (zeroed, staged, v_mm, v_sb, uz_mm, r_mm, uz_sb, r_sb, qk_ready, s_mm, shifted, at_zero, t_ready, inverted, g_ready,
             a_ready, gate_ready, h_mm, r_ready, o_mm, o_sb, less, gated, summed) = st.sem(*["l2a_" + n for n in (
                 "zeroed staged v_mm v_sb uz_mm r_mm uz_sb r_sb qk_ready s_mm shifted at_zero t_ready inverted g_ready "
                 "a_ready gate_ready h_mm r_ready o_mm o_sb less gated summed").split()])
            xg = st.sb("l2a_xn_group", [D, GW // S, S])
            vs = st.sb("l2a_values", [128, TPG, 2 * D])
            uz = st.sb("l2a_u_z", [D, 2, GW])
            rg = st.sb("l2a_r", [D, 2, GW])
            ug = st.sb("l2a_update_gate", [D, GW])
            qk = st.sb("l2a_qk", [D, 2, GW])
            tt = st.sb("l2a_t", [128, 3, TPG, S])
            wt = st.sb("l2a_weights", [128, TPG, 2, S])
            hr = st.sb("l2a_hr", [D, 2, GW])
            hh = st.sb("l2a_h_new", [D, GW])
            mg = lambda g: mx[:, :].rearrange("p (l s) -> p s l", s=S)[:, bass.ds(g * (GW // S), GW // S), :]
            of_group = lambda a, g: a[:, :].rearrange("p (l s) -> p s l", s=S)[:, bass.ds(g * (GW // S), GW // S), :]

            def turns(eng, step):
                with eng.Fori(0, G - 1) as g:
                    step(g, False)
                step(G - 1, True)

            with st.block() as block:
                @block.gpsimd
                def _(pool):
                    nc.gpsimd.memset(wt[:, :, :, :], 0.0).then_inc(zeroed, 1)
                    nc.gpsimd.tensor_copy(xg[:, :, :], of_group(xn, 0)).then_inc(staged, 1)
                    with pool.Fori(1, G) as g:
                        pool.wait_ge(v_mm, count(g))
                        nc.gpsimd.tensor_copy(xg[:, :, :], of_group(xn, g)).then_inc(staged, 1)

                @block.tensor
                def _(pe):
                    def values(g):
                        pe.wait_ge(staged, count(g + 1))
                        pe.wait_ge(v_sb, count(g))
                        for t in range(TPG):
                            o = k.bank(t // 2)[:, t % 2 * 256:t % 2 * 256 + 256]
                            nc.tensor.matmul(o, xg[:, 2 * t:2 * t + 2].rearrange("p a b -> p (a b)"), k.w("l2a_wv"),
                                             start=True, stop=False)
                            m = nc.tensor.matmul(o, k.w("c_ones_row"), k.w("l2a_bv"), start=False, stop=True)
                        m.then_inc(v_mm, 1)

                    def update_and_z(g):
                        pe.wait_ge(uz_sb, count(2 * g))
                        for i in range(2):
                            nc.tensor.matmul(k.bank(4 + i), k.w(f"l2a_wmx{i}"), mg(g)).then_inc(uz_mm, 1)

                    def reset(g):
                        for i in range(2):
                            nc.tensor.matmul(k.bank(2 + i), k.w(f"l2a_wmx{2 + i}"), mg(g)).then_inc(r_mm, 1)

                    values(0)
                    update_and_z(0)
                    reset(0)

                    def step(g, last):
                        pe.wait_ge(qk_ready, count(g + 1))
                        for t in range(TPG):
                            for b in range(2):
                                c = slice(t * 128 + b * 64, t * 128 + b * 64 + 64)
                                m = nc.tensor.matmul(k.bank(6)[b * 64:b * 64 + 64, t * S:t * S + S], qk[:, 1, c], qk[:, 0, c])
                        m.then_inc(s_mm, 1)
                        if not last:
                            values(g + 1)
                        pe.wait_ge(o_sb, count(g))
                        nc.tensor.matmul(k.bank(7), k.w("l2a_wmx4"), mg(g), start=True, stop=False)
                        pe.wait_ge(v_sb, count(g + 1))
                        pe.wait_ge(r_sb, count(2 * g + 2))
                        pe.wait_ge(a_ready, count(g + 1))
                        for t in range(TPG):
                            for c in range(2):
                                m = nc.tensor.matmul(k.bank(2 + c)[:, t * 2 * S:(t + 1) * 2 * S], vs[:, t, c * D:c * D + D],
                                                     wt[:, t].rearrange("p b s -> p (b s)"))
                        m.then_inc(h_mm, 1)
                        if not last:
                            update_and_z(g + 1)
                        pe.wait_ge(r_ready, count(g + 1))
                        nc.tensor.matmul(k.bank(7), k.w("l2a_wh0"), hr[:, 0], start=False, stop=False)
                        nc.tensor.matmul(k.bank(7), k.w("l2a_wh1"), hr[:, 1], start=False, stop=True).then_inc(o_mm, 1)
                        if not last:
                            reset(g + 1)

                    turns(pe, step)

                @block.scalar
                def _(act):
                    def values(g):
                        act.wait_ge(v_mm, count(g + 1))
                        nc.scalar.activation(vs[:, :, :].rearrange("p t d -> p (t d)"), k.ps[:, 0:1024], ACT.Silu)\
                            .then_inc(v_sb, 1)

                    def update_and_z(g):
                        act.wait_ge(uz_mm, count(2 * g + 1))
                        nc.scalar.activation(uz[:, 0], k.bank(4), ACT.Tanh, bias=hb[:, 1:2], scale=0.5).then_inc(uz_sb, 1)
                        act.wait_ge(uz_mm, count(2 * g + 2))
                        nc.scalar.activation(uz[:, 1], k.bank(5), ACT.Silu, bias=k.w("l2a_bmx1")).then_inc(uz_sb, 1)

                    def reset(g):
                        for i in range(2):
                            act.wait_ge(r_mm, count(2 * g + (i + 1)))
                            nc.scalar.activation(rg[:, i], k.bank(2 + i), ACT.Silu, bias=k.w(f"l2a_bmx{2 + i}"))\
                                .then_inc(r_sb, 1)

                    nc.scalar.preload_act_table(ACT.Silu)
                    values(0)
                    update_and_z(0)
                    reset(0)

                    def step(g, last):
                        act.wait_ge(t_ready, count(g + 1))
                        nc.scalar.activation(tt[:, 2], tt[:, 0], ACT.Gelu).then_inc(g_ready, 1)
                        act.wait_ge(h_mm, count(g + 1))
                        if not last:
                            values(g + 1)
                            act.wait_ge(gate_ready, count(g + 1))
                            update_and_z(g + 1)
                        act.wait_ge(summed, count(g))
                        act.wait_ge(o_mm, count(g + 1))
                        nc.scalar.activation(hh[:, :], k.bank(7), ACT.Silu, bias=hb[:, 0:1]).then_inc(o_sb, 1)
                        if not last:
                            reset(g + 1)

                    turns(act, step)

                @block.vector
                def _(dve):
                    def queries_keys(g):
                        dve.wait_ge(uz_sb, count(2 * g + 2))
                        for i in range(2):
                            m = nc.vector.tensor_scalar(qk[:, i], uz[:, 1], k.w("l2a_qg")[:, i:i + 1],
                                                        k.w("l2a_qb")[:, i:i + 1], ALU.mult, ALU.add)
                        m.then_inc(qk_ready, 1)

                    queries_keys(0)
                    t0, eq, ge = (tt[:, i] for i in range(3))
                    dve.wait_ge(zeroed, count(1))

                    def step(g, last):
                        dve.wait_ge(s_mm, count(g + 1))
                        nc.vector.scalar_tensor_tensor(
                            t0, k.bank(6, TPG * S).rearrange("p (t s) -> p t s", s=S), 1.0 / (S * SIGMA),
                            bias[:, :].unsqueeze(1).broadcast_to([128, TPG, S]), ALU.mult, ALU.add).then_inc(shifted, 1)
                        dve.wait_ge(shifted, count(g + 1))
                        nc.vector.tensor_scalar(eq, t0, 0.0, 1e-20, ALU.is_equal, ALU.mult).then_inc(at_zero, 1)
                        dve.wait_ge(at_zero, count(g + 1))
                        nc.vector.tensor_tensor(t0, t0, eq, ALU.add).then_inc(t_ready, 1)
                        dve.wait_ge(t_ready, count(g + 1))
                        nc.vector.reciprocal(eq, t0).then_inc(inverted, 1)
                        dve.wait_ge(inverted, count(g + 1))
                        dve.wait_ge(g_ready, count(g + 1))
                        for b in range(2):
                            rows = slice(b * 64, b * 64 + 64)
                            m = nc.vector.tensor_tensor(wt[rows, :, b], ge[rows], eq[rows], ALU.mult)
                        m.then_inc(a_ready, 1)
                        nc.vector.tensor_scalar(ug[:, :], uz[:, 0], 0.5, 0.5, ALU.mult, ALU.add).then_inc(gate_ready, 1)
                        dve.wait_ge(h_mm, count(g + 1))
                        nc.vector.tensor_tensor(hr[:, :, :], k.ps[:, 2 * 512:4 * 512].rearrange("p (c n) -> p c n", c=2),
                                                rg[:, :, :], ALU.mult).then_inc(r_ready, 1)
                        if not last:
                            queries_keys(g + 1)
                        w = lambda a: a.rearrange("p (s l) -> p s l", l=S)
                        dve.wait_ge(gate_ready, count(g + 1))
                        dve.wait_ge(o_sb, count(g + 1))
                        nc.vector.tensor_tensor(w(hh[:, :]), w(hh[:, :]), of_group(k.h, g), ALU.subtract).then_inc(less, 1)
                        dve.wait_ge(less, count(g + 1))
                        nc.vector.tensor_tensor(hh[:, :], hh[:, :], ug[:, :], ALU.mult).then_inc(gated, 1)
                        dve.wait_ge(gated, count(g + 1))
                        nc.vector.tensor_tensor(w(hh[:, :]), w(hh[:, :]), of_group(k.h, g), ALU.add).then_inc(summed, 1)
                        dve.wait_ge(summed, count(g + 1))
                        nc.vector.tensor_tensor(of_group(k.x, g), of_group(k.x, g), w(hh[:, :]), ALU.add)

                    turns(dve, step)


def l3_attn(k):
    nc = k.nc
    layer_norm(k, k.x, k.h, "l3a_ln")
    with nc.sbuf_tensor("l3a_normed", [D, T], F32) as n:
        layer_norm(k, k.h, n, "l3a_ln1", gain=k.w("l3a_g1"), bias=k.w("l3a_b1"))
        with Stage(nc) as st:
            (staged, q_mm, kv_mm, q_low, k_low, q_exp, k_exp, qf_ready, kf_ready, v_sb, ksum_mm, masked, den_mm, num_mm,
             den_read, rd_ready, c_ready, o_mm, h_done, ones_set) = st.sem(*["l3a_" + s for s in (
                 "staged q_mm kv_mm q_low k_low q_exp k_exp qf_ready kf_ready v_sb ksum_mm masked den_mm num_mm "
                 "den_read rd_ready c_ready o_mm h_done ones_set").split()])
            ng = st.sb("l3a_n_group", [D, GW])
            lo = st.sb("l3a_low", [128, 2, GW])
            qf = st.sb("l3a_q", [D, 2, GW])
            kf = st.sb("l3a_k", [128, TPG, D])
            vv = st.sb("l3a_v_one", [128, TPG, D + 1])
            kvm = st.sb("l3a_kv_masked", [D, 2, TPG, D])
            qk = st.sb("l3a_q_times_k_sum", [D, GW])
            sums = k.ps[:, 3 * 512:7 * 512].rearrange("p (b t c) -> p b t c", b=2, t=TPG)
            rd = st.sb("l3a_den", [D, GW])
            cf = st.sb("l3a_context", [D, GW])
            kvb = k.ps[:, 512:1536].rearrange("p (t a d) -> p t a d", t=TPG, a=2)

            def turns(eng, step):
                with eng.Fori(0, G // 2 - 1) as it:
                    for par in range(2):
                        step(it * 2 + par, par, False)
                for par in range(2):
                    step(G - 2 + par, par, par == 1)

            with st.block() as block:
                @block.gpsimd
                def _(pool):
                    nc.gpsimd.memset(vv[:, :, D:D + 1], 1.0).then_inc(ones_set, 1)
                    with pool.Fori(0, G) as g:
                        pool.wait_ge(kv_mm, count(g))
                        nc.gpsimd.tensor_copy(ng[:, :], n[:, bass.ts(g, GW)]).then_inc(staged, 1)

                @block.tensor
                def _(pe):
                    def project(g):
                        pe.wait_ge(qf_ready, count(g))
                        nc.tensor.matmul(k.bank(0), k.w("l3a_wq"), n[:, bass.ds(g * GW, GW)]).then_inc(q_mm, 1)
                        pe.wait_ge(staged, count(g + 1))
                        pe.wait_ge(kf_ready, count(g))
                        pe.wait_ge(v_sb, count(g))
                        for t in range(TPG):
                            m = nc.tensor.matmul(k.bank(1 + t // 2)[:, t % 2 * 256:t % 2 * 256 + 256],
                                                 ng[:, t * 128:t * 128 + 128], k.w("l3a_wkv"))
                        m.then_inc(kv_mm, 1)

                    def key_sums(g):
                        pe.wait_ge(den_read, count(g))
                        pe.wait_ge(kf_ready, count(g + 1))
                        pe.wait_ge(v_sb, count(g + 1))
                        for t in range(TPG):
                            for b in range(2):
                                rows = slice(b * 64, b * 64 + 64)
                                m = nc.tensor.matmul(sums[:, b, t, 0:D + 1], kf[rows, t], vv[rows, t])
                        m.then_inc(ksum_mm, 1)

                    pe.wait_ge(ones_set, count(1))
                    project(0)
                    key_sums(0)

                    def step(g, par, last):
                        if not last:
                            project(g + 1)
                        pe.wait_ge(h_done, count(g))
                        pe.wait_ge(masked, count(g + 1))
                        nc.tensor.matmul(k.bank(3), k.w("c_heads"), qk[:, :]).then_inc(den_mm, 1)
                        for t in range(TPG):
                            for b in range(2):
                                c = slice(t * 128 + b * 64, t * 128 + b * 64 + 64)
                                m = nc.tensor.matmul(k.bank(7)[:, c], kvm[:, b, t], qf[:, par, c])
                        m.then_inc(num_mm, 1)
                        if not last:
                            key_sums(g + 1)
                        pe.wait_ge(c_ready, count(g + 1))
                        nc.tensor.matmul(k.bank(7), k.w("l3a_wo"), cf[:, :]).then_inc(o_mm, 1)

                    turns(pe, step)

                @block.scalar
                def _(act):
                    def features(g):
                        act.wait_ge(q_mm, count(g + 1))
                        act.wait_ge(qf_ready, count(g))
                        nc.scalar.activation(lo[:, 0], k.bank(0), ACT.Relu, scale=-1.0).then_inc(q_low, 1)
                        act.wait_ge(q_low, count(g + 1))
                        nc.scalar.activation(lo[:, 0], lo[:, 0], ACT.Exp, scale=-1.0).then_inc(q_exp, 1)
                        act.wait_ge(kv_mm, count(g + 1))
                        act.wait_ge(kf_ready, count(g))
                        nc.scalar.activation(lo[:, 1].rearrange("p (t d) -> p t d", d=D), kvb[:, :, 0], ACT.Relu,
                                             scale=-1.0).then_inc(k_low, 1)
                        act.wait_ge(k_low, count(g + 1))
                        nc.scalar.activation(lo[:, 1], lo[:, 1], ACT.Exp, scale=-1.0).then_inc(k_exp, 1)
                        act.wait_ge(kf_ready, count(g + 1))
                        act.wait_ge(ksum_mm, count(g))
                        nc.scalar.copy(vv[:, :, 0:D], kvb[:, :, 1]).then_inc(v_sb, 1)

                    nc.scalar.preload_act_table(ACT.Exp)
                    features(0)
                    with act.Fori(1, G) as g:
                        features(g)

                @block.vector
                def _(dve):
                    heads = k.w("c_heads").unsqueeze(1).unsqueeze(1).broadcast_to([D, 2, TPG, D])

                    def features(g, par):
                        dve.wait_ge(q_exp, count(g + 1))
                        nc.vector.scalar_tensor_tensor(qf[:, par], k.bank(0), 0.0, lo[:, 0], ALU.max, ALU.add)\
                            .then_inc(qf_ready, 1)
                        dve.wait_ge(k_exp, count(g + 1))
                        dve.wait_ge(ksum_mm, count(g))
                        nc.vector.scalar_tensor_tensor(kf[:, :, :], kvb[:, :, 0], 0.0,
                                                       lo[:, 1].rearrange("p (t d) -> p t d", d=D), ALU.max, ALU.add)\
                            .then_inc(kf_ready, 1)

                    def mask(g, par):
                        dve.wait_ge(ksum_mm, count(g + 1))
                        dve.wait_ge(qf_ready, count(g + 1))
                        nc.vector.tensor_tensor(kvm[:, :, :, :], sums[:, :, :, 0:D], heads, ALU.mult)
                        nc.vector.tensor_tensor(
                            qk[:, :].rearrange("p (t b s) -> p t b s", b=2, s=S),
                            qf[:, par].rearrange("p (t b s) -> p t b s", b=2, s=S),
                            sums[:, :, :, D].rearrange("p b t -> p t b").unsqueeze(3).broadcast_to([D, TPG, 2, S]),
                            ALU.mult).then_inc(masked, 1)

                    features(0, 0)
                    mask(0, 0)

                    def step(g, par, last):
                        dve.wait_ge(den_mm, count(g + 1))
                        nc.vector.tensor_scalar(rd[:, :], k.bank(3), 1e-6, None, ALU.add).then_inc(den_read, 1)
                        if not last:
                            features(g + 1, 1 - par)
                        dve.wait_ge(den_read, count(g + 1))
                        nc.vector.reciprocal(rd[:, :], rd[:, :]).then_inc(rd_ready, 1)
                        dve.wait_ge(rd_ready, count(g + 1))
                        dve.wait_ge(num_mm, count(g + 1))
                        nc.vector.tensor_tensor(cf[:, :], k.bank(7), rd[:, :], ALU.mult).then_inc(c_ready, 1)
                        if not last:
                            mask(g + 1, 1 - par)
                        dve.wait_ge(o_mm, count(g + 1))
                        hc = k.h[:, bass.ds(g * GW, GW)]
                        nc.vector.scalar_tensor_tensor(hc, k.bank(7), k.w("l3a_bo"), hc, ALU.add, ALU.add)\
                            .then_inc(h_done, 1)

                    turns(dve, step)
        layer_norm(k, k.h, n, "l3a_ln2", gain=k.w("l3a_g2"), bias=k.w("l3a_b2"), add_to=k.x, add=k.h)
        feed_forward(k, "l3a_ff", ACT.Gelu, [(k.w(f"l3a_w1_{i}"), k.w(f"l3a_fb_{i}"), None, k.w(f"l3a_w2_{i}"), None)
                                             for i in range(4)], k.x, out_bias=k.w("l3a_fb2"), src=n)


def l3_xattn(k):
    nc = k.nc
    layer_norm(k, k.x, k.h, "l3x_ln", add_to=k.x)
    with Stage(nc) as st:
        (staged, turn_mm, turned, s_mm, e_ready, plus_one, sim_ready, choice_step, chosen, agg_mm, counted, inverted,
         ok_ready, out_mm, x_done, ones_set, ab) = st.sem(*["l3x_" + s for s in (
             "staged turn_mm turned s_mm e_ready plus_one sim_ready choice_step chosen agg_mm counted inverted "
             "ok_ready out_mm x_done ones_set ab").split()])
        hg = st.sb("l3x_h_group", [D, 2, GW])
        tm = st.sb("l3x_token_major", [128, 2, 2, TPG, D])
        sim = st.sb("l3x_sim", [128, 2, 2, TPG, S])
        pick = st.sb("l3x_pick", [128, 3, TPG, S])
        small = st.sb("l3x_small", [128, 3, TPG])
        okk = st.sb("l3x_rows", [128, TPG, D])
        ones = st.sb("l3x_ones", [128, 1])
        neg = st.sb("l3x_negated", [128, 2])
        both = lambda par: sim[:, par].rearrange("p a t s -> p (a t s)")

        def turns(eng, step):
            with eng.Fori(0, G // 2 - 1) as it:
                for par in range(2):
                    step(it * 2 + par, par, False)
            for par in range(2):
                step(G - 2 + par, par, par == 1)

        with st.block() as block:
            @block.gpsimd
            def _(pool):
                nc.gpsimd.memset(ones[:, :], 1.0).then_inc(ones_set, 1)
                with pool.Fori(0, G) as g:
                    pool.wait_ge(turn_mm, count(g))
                    nc.gpsimd.tensor_copy(hg[:, 0], k.h[:, bass.ts(g, GW)])
                    nc.gpsimd.tensor_copy(hg[:, 1], k.ctx[:, bass.ts(g, GW)]).then_inc(staged, 1)

            @block.tensor
            def _(pe):
                def likeness(g):
                    pe.wait_ge(staged, count(g + 1))
                    pe.wait_ge(e_ready, count(g))
                    for a in range(2):
                        for t in range(TPG):
                            for b in range(2):
                                c = slice(t * 128 + b * 64, t * 128 + b * 64 + 64)
                                m = nc.tensor.matmul(k.bank(2)[b * 64:b * 64 + 64, a * 256 + t * S:a * 256 + t * S + S],
                                                     hg[:, a, c], hg[:, 1 - a, c])
                    m.then_inc(s_mm, 1)
                    pe.wait_ge(turned, count(g))
                    for a in range(2):
                        for t in range(TPG - a):
                            turn(a, t)

                def turn(a, t):
                    return nc.tensor.transpose(k.bank(a)[:, t * D:t * D + D], hg[:, a, t * 128:t * 128 + 128],
                                               k.w("c_ident"))

                def last_turn():
                    turn(1, TPG - 1).then_inc(turn_mm, 1)

                pe.wait_ge(ones_set, count(1))
                likeness(0)
                last_turn()

                def step(g, par, last):
                    if not last:
                        likeness(g + 1)
                    pe.wait_ge(turned, count(g + 1))
                    pe.wait_ge(x_done, count(g))
                    pe.wait_ge(chosen, count(g + 1))
                    if not last:
                        last_turn()
                    for t in range(TPG):
                        for b in range(2):
                            rows = slice(b * 64, b * 64 + 64)
                            nc.tensor.matmul(k.bank(4 + b)[rows, t * D:t * D + D], pick[rows, 2, t], tm[rows, par, 0, t])
                            m = nc.tensor.matmul(k.bank(6 + b)[rows, t:t + 1], pick[rows, 1, t], ones[rows, :])
                    m.then_inc(agg_mm, 1)
                    pe.wait_ge(ok_ready, count(g + 1))
                    for t in range(TPG):
                        for b in range(2):
                            rows = slice(b * 64, b * 64 + 64)
                            m = nc.tensor.matmul(k.bank(6 + b)[:, t * S:t * S + S], okk[rows, t], sim[rows, par, 1, t])
                    m.then_inc(out_mm, 1)

                turns(pe, step)

            @block.scalar
            def _(act):
                def exp_and_copy(g, par):
                    act.wait_ge(s_mm, count(g + 1))
                    nc.scalar.activation(both(par), k.bank(2), ACT.Exp, scale=neg[:, 0:1], bias=neg[:, 1:2]).then_inc(e_ready, 1)
                    act.wait_ge(turn_mm, count(g + 1))
                    nc.scalar.copy(tm[:, par].rearrange("p a t d -> p (a t d)"), k.ps[:, 0:1024]).then_inc(turned, 1)

                nc.scalar.preload_act_table(ACT.Exp)
                act.wait_ge(ab, count(1))
                exp_and_copy(0, 0)

                def step(g, par, last):
                    if not last:
                        act.wait_ge(chosen, count(g + 1))
                        exp_and_copy(g + 1, 1 - par)

                turns(act, step)

            @block.vector
            def _(dve):
                nc.vector.tensor_scalar(neg[:, :], k.w("l3x_ab"), -1.0, None, ALU.mult).then_inc(ab, 1)
                mx, den, rc = (small[:, i] for i in range(3))
                wide = lambda a: a.unsqueeze(2).broadcast_to([128, TPG, S])
                choice = Chain(dve, choice_step, 5)

                def sigmoid(g, par):
                    dve.wait_ge(e_ready, count(g + 1))
                    nc.vector.tensor_scalar(both(par), both(par), 1.0, None, ALU.add).then_inc(plus_one, 1)
                    dve.wait_ge(plus_one, count(g + 1))
                    nc.vector.reciprocal(both(par), both(par)).then_inc(sim_ready, 1)

                def choose(g, par):
                    choice.turn(g)
                    dve.wait_ge(sim_ready, count(g + 1))
                    choice.link(nc.vector.tensor_reduce(mx, sim[:, par, 0], AX.X, ALU.max))
                    choice.link(nc.vector.tensor_tensor(pick[:, 0], sim[:, par, 0], wide(mx), ALU.is_equal))
                    choice.link(nc.vector.tensor_tensor(pick[:, 0], pick[:, 0], k.w("c_falling").unsqueeze(1)
                                                        .broadcast_to([128, TPG, S]), ALU.mult))
                    choice.link(nc.vector.tensor_reduce(mx, pick[:, 0], AX.X, ALU.max))
                    choice.link(nc.vector.tensor_tensor(pick[:, 1], pick[:, 0], wide(mx), ALU.is_equal))
                    nc.vector.tensor_tensor(pick[:, 2], pick[:, 1], sim[:, par, 0], ALU.mult).then_inc(chosen, 1)

                sigmoid(0, 0)
                choose(0, 0)

                def step(g, par, last):
                    if not last:
                        sigmoid(g + 1, 1 - par)
                    dve.wait_ge(agg_mm, count(g + 1))
                    dve.wait_ge(turned, count(g + 1))
                    for b in range(2):
                        rows = slice(b * 64, b * 64 + 64)
                        nc.vector.tensor_tensor(okk[rows].rearrange("p t d -> p (t d)"), k.bank(4 + b)[rows],
                                                tm[rows, par, 1].rearrange("p t d -> p (t d)"), ALU.add)
                        m = nc.vector.tensor_scalar(den[rows], k.bank(6 + b, TPG)[rows], 1.0, None, ALU.add)
                    m.then_inc(counted, 1)
                    dve.wait_ge(counted, count(g + 1))
                    nc.vector.reciprocal(rc, den).then_inc(inverted, 1)
                    dve.wait_ge(inverted, count(g + 1))
                    nc.vector.tensor_tensor(okk[:, :, :], okk[:, :, :], rc.unsqueeze(2).broadcast_to([128, TPG, D]),
                                            ALU.mult).then_inc(ok_ready, 1)
                    if not last:
                        choose(g + 1, 1 - par)
                    dve.wait_ge(out_mm, count(g + 1))
                    xg = k.x[:, bass.ds(g * GW, GW)].rearrange("p (t b s) -> p b t s", b=2, s=64)
                    for b in range(2):
                        m = nc.vector.tensor_tensor(xg[:, b], xg[:, b],
                                                    k.bank(6 + b, 256).rearrange("p (t s) -> p t s", s=64), ALU.add)
                    m.then_inc(x_done, 1)

                turns(dve, step)


def build(nc, cols, dram, out):
    with ExitStack() as stack:
        k = Core(nc, cols, stack, dram)
        experts = lambda area: (area + "_experts", k.packed[area][:, 0:cols[area][""]], dram["packed_" + area])
        needed_first = Load(k, [("x", k.x[:, :], dram["x_in"]), ("first", k.packed["first"][:, :], dram["packed_first"])])
        rest = Load(k, [("ctx", k.ctx[:, :], dram["ctx_in"]),
                        ("shared", k.packed["shared"][:, :], dram["packed_shared"]), experts("l2f")])
        needed_first.finish()
        l0_attn(k)
        rest.finish()
        l0_xattn(k)
        l0_ffn(k)
        l1_attn(k)
        l1_xattn(k)
        l1_ffn(k)
        l2_attn(k)
        l2_xattn(k)
        l2_ffn(k)
        last_experts = Load(k, [experts("l3f")])
        l3_attn(k)
        l3_xattn(k)
        last_experts.finish()
        l3_ffn(k, out)


def layout(inp):
    n = lambda name: np.asarray(inp[name])
    col = lambda a: a.reshape(-1, 1)
    one = np.float32
    c = {}
    c["c_mean"] = np.full((D, D), 1.0 / D, one)
    c["c_eps"] = np.full((D, 1), LN_EPS, one)
    c["c_ident"] = np.eye(128, dtype=one)
    c["c_by_h"] = (np.arange(D)[:, None] // DH % 2 == np.arange(2)).astype(one)
    c["c_by_p"] = (np.arange(D)[:, None] // DH % NQ // 2 == np.arange(2)).astype(one)
    slope = (2.0 ** (-8.0 * np.arange(1, H + 1, dtype=one) / H)).astype(one)
    pos = np.arange(S, dtype=one)
    h, qpos = np.arange(128)[:, None, None, None] // S, np.tile(pos, 2)[:, None, None, None]
    r, p = np.arange(NQ)[None, :, None, None], np.arange(2)[None, None, :, None]
    c["c_alibi"] = np.where(pos > qpos, one(NEG), slope[4 * r + 2 * p + h] * (pos - qpos)).astype(one).reshape(128, -1)
    c["l0a_wq"], c["l0a_wk"], c["l0a_wv"] = n("L0_attn_W_query"), n("L0_attn_W_key"), n("L0_attn_W_value")
    c["l0a_wo"], c["l0a_bo"] = n("L0_attn_W_proj"), col(n("L0_attn_b_proj"))
    w, b = n("L2_xattn_Wqkv"), n("L2_xattn_bqkv")
    c["l2x_wq"], c["l2x_wk"], c["l2x_wv"] = w[:, 0:D], w[:, D:2 * D], w[:, 2 * D:]
    c["l2x_bq"], c["l2x_bk"], c["l2x_bv"] = col(b[0:D]), col(b[D:2 * D]), col(b[2 * D:])
    w, b = n("L2_xattn_Wqkv_aux"), n("L2_xattn_bqkv_aux")
    c["l2x_wka"], c["l2x_wva"], c["l2x_bka"], c["l2x_bva"] = w[:, D:2 * D], w[:, 2 * D:], col(b[D:2 * D]), col(b[2 * D:])
    c["l2x_wo"], c["l2x_bo"] = n("L2_xattn_Wo"), col(n("L2_xattn_bo"))
    c["l2x_gate"] = col(np.repeat(n("L2_xattn_g"), DH))
    w1, w2, b1 = n("L0_ffn_w1")[0], n("L0_ffn_w2")[0], n("L0_ffn_b1")[0]
    for i in range(4):
        r = slice(i * 128, i * 128 + 128)
        c[f"l0f_w1_{i}"], c[f"l0f_b1_{i}"], c[f"l0f_w2_{i}"] = w1[:, r], col(b1[r]), w2[r]
    c["l0f_b2"], c["l0f_gamma"], c["l0f_beta"] = col(n("L0_ffn_b2")[0]), col(n("L0_ffn_gamma")), col(n("L0_ffn_beta"))
    wd, bd, wu = n("L1_ffn_Wd"), n("L1_ffn_bd"), n("L1_ffn_Wu")
    c["l1f_gate"], c["l1f_bu"] = n("L1_ffn_w_gate"), n("L1_ffn_bu")
    for i in range(4):
        e = slice(2 * i, 2 * i + 2)
        c[f"l1f_wd_{i}"] = wd[e].transpose(1, 0, 2).reshape(128, 128)
        c[f"l1f_bd_{i}"], c[f"l1f_wu_{i}"] = col(bd[e]), wu[e].reshape(128, 128)
    w1, w2, w3 = n("L2_ffn_w1"), n("L2_ffn_w2"), n("L2_ffn_w3")
    c["l2f_gate"] = n("L2_ffn_gate_w").T
    for i in range(16):
        e, r = i // 2, slice(i % 2 * 128, i % 2 * 128 + 128)
        c[f"l2f_w1_{i}"], c[f"l2f_w3_{i}"], c[f"l2f_w2_{i}"] = w1[e, r].T, w3[e, r].T, w2[e][:, r].T
    c["l3f_router"] = n("L3_ffn_router_w").T
    c["l3f_bias"] = np.broadcast_to(n("L3_ffn_bias")[None], (128, 16))
    for i in range(16):
        c[f"l3f_g_{i}"], c[f"l3f_u_{i}"], c[f"l3f_d_{i}"] = n("L3_ffn_gate_w")[i], n("L3_ffn_up_w")[i], n("L3_ffn_down_w")[i]
    for i in range(2):
        r = slice(i * 128, i * 128 + 128)
        c[f"l3f_sg_{i}"], c[f"l3f_su_{i}"] = n("L3_ffn_sh_gate_w")[:, r], n("L3_ffn_sh_up_w")[:, r]
        c[f"l3f_sd_{i}"] = n("L3_ffn_sh_down_w")[r]
    c["c_ones_row"] = np.ones((1, 128), one)
    c["c_heads"] = (np.arange(D)[:, None] // DH == np.arange(D) // DH).astype(one)
    c["c_restart"] = np.broadcast_to((np.arange(GW) % S != 0).astype(one)[None], (128, GW))
    c["c_causal"] = (np.arange(128)[:, None] % S <= np.arange(S)).astype(one)
    c["c_pos"] = np.broadcast_to(pos[None], (128, S))
    c["c_falling"] = np.broadcast_to((S - pos)[None], (128, S))
    freqs = np.exp(np.arange(D // 2, dtype=one) * one(-np.log(10000.0) / (D // 2)))
    ang = np.tile(freqs[:, None] * pos[None, :], (2, 2))
    c["c_cos"] = np.cos(ang).astype(one)
    c["c_sin"] = (np.sin(ang) * np.where(np.arange(D) < D // 2, -1.0, 1.0)[:, None]).astype(one)
    w, b = n("L1_attn_qkv_w"), n("L1_attn_qkv_b")
    c["l1a_wq"], c["l1a_wk"], c["l1a_wv"] = w[0:D].T, w[D:2 * D].T, w[2 * D:].T
    c["l1a_bq"], c["l1a_bk"], c["l1a_bv"] = col(b[0:D]), col(b[D:2 * D]), col(b[2 * D:])
    c["l1a_wo"], c["l1a_bo"] = n("L1_attn_out_w").T, col(n("L1_attn_out_b"))
    for x in "qkv":
        c[f"l1x_w{x}"], c[f"l1x_b{x}"] = n(f"L1_xattn_W{x}"), col(n(f"L1_xattn_b{x}"))
    for x in ("ln_w", "ln_b", "bh"):
        c[f"l2a_{x}"] = col(n(f"L2_attn_{x}"))
    c["l2a_delta_alpha"] = np.concatenate([n("L2_attn_ema_delta")[:, :, 0], n("L2_attn_ema_alpha")[:, :, 0]], axis=1)
    c["l2a_beta"], c["l2a_gamma"], c["l2a_omega"] = (n("L2_attn_ema_beta")[:, :, 0], n("L2_attn_ema_gamma"),
                                                     col(n("L2_attn_ema_omega")))
    c["l2a_wv"], c["l2a_bv"] = n("L2_attn_Wv").T, n("L2_attn_bv")[None]
    for i in range(5):
        r = slice(i * D, i * D + D)
        c[f"l2a_wmx{i}"], c[f"l2a_bmx{i}"] = n("L2_attn_Wmx")[r].T, col(n("L2_attn_bmx")[r])
    for i in range(2):
        c[f"l2a_wh{i}"] = n("L2_attn_Wh")[:, i * D:i * D + D].T
    c["l2a_qg"], c["l2a_qb"] = n("L2_attn_qk_gamma").T, n("L2_attn_qk_beta").T
    for x, name in (("ra", "alpha"), ("rb", "beta")):
        v = n(f"L2_attn_rot_{name}")[0]
        c[f"l2a_{x}"], c[f"l2a_{x}s"] = col(v), col(np.roll(v, D // 2))
    w = n("L3_attn_qkv_w")
    c["l3a_wq"], c["l3a_wkv"], c["l3a_wo"] = w[0:D].T, w[D:].T, n("L3_attn_proj_w").T
    c["l3a_bo"] = col(n("L3_attn_proj_b"))
    for i in (1, 2):
        c[f"l3a_g{i}"], c[f"l3a_b{i}"] = col(n(f"L3_attn_norm{i}_g")), col(n(f"L3_attn_norm{i}_b"))
    for i in range(4):
        r = slice(i * 128, i * 128 + 128)
        c[f"l3a_w1_{i}"], c[f"l3a_w2_{i}"] = n("L3_attn_fc1_w")[r].T, n("L3_attn_fc2_w")[:, r].T
        c[f"l3a_fb_{i}"] = col(n("L3_attn_fc1_b")[r])
    c["l3a_fb2"] = col(n("L3_attn_fc2_b"))
    c["l3x_ab"] = np.broadcast_to(np.stack([n("L3_xattn_sim_alpha")[0], n("L3_xattn_sim_beta")[0]])[None], (128, 2))
    c["l0x_wq"] = n("L0_xattn_Wq").T
    c["l0x_wk"] = n("L0_xattn_Wk").T
    c["l0x_wv"] = n("L0_xattn_Wv").T
    return c


def kernel(**inputs):
    import concourse.bacc as bacc
    from concourse.bass_utils import run_bass_kernel_spmd

    nc = bacc.Bacc("TRN2", target_bir_lowering=False, num_devices=1)
    pieces = layout(inputs)
    cols, packed = {}, {}
    early = {"c_mean", "c_eps", "c_ident", "c_by_h", "c_by_p", "c_alibi"}
    area_of = lambda name: ("first" if name in early or name[:3] == "l0a" else
                            name[:3] if name[:3] in ("l2f", "l3f") else "shared")
    for area in ("first", "shared", "l2f", "l3f"):
        own = {name: a for name, a in pieces.items() if area_of(name) == area}
        at, where = 0, {}
        for name, a in own.items():
            where[name] = (at, a.shape[1], a.shape[0])
            at += a.shape[1]
        where[""] = at
        cols[area], packed[area] = where, np.zeros((128, at), np.float32)
        for name, a in own.items():
            o, w, r = where[name]
            packed[area][0:r, o:o + w] = a
    n = lambda name: np.asarray(inputs[name])
    tiles = lambda a: np.ascontiguousarray(a.reshape(B // 2, 128, S).transpose(1, 0, 2))
    table = np.zeros((D, 2, NQ, 2, 2 * S - 1), np.float32)
    for head in range(H):
        table[head * DH:head * DH + DH, head % 2, head // NQ, head % NQ // 2] = n("L1_xattn_rel_table")[1:2 * S].T
    arrays = {
        "rel_in": table.reshape(D, -1),
        "mask_in": n("mask_Bx1x1xS2_ff0").reshape(B, S),
        **{name: np.tile(np.repeat(np.eye(e, dtype=np.float32), width, axis=1), (3, 1))
           for name, e, width in (("sel_l1", 8, 64), ("sel_l2", 8, 128), ("sel_l3", 16, 128))},
        "x_in": np.ascontiguousarray(n("x").reshape(T, D).T),
        "ctx_in": np.ascontiguousarray(n("ctx_1024").reshape(T, D).T),
        **{"packed_" + area: a for area, a in packed.items()},
        "cross_mask": tiles(n("mask_BxSxS2_bk0").transpose(0, 2, 1)),
    }
    aps = {name: nc.dram_tensor(name, a.shape, mybir.dt.from_np(a.dtype), kind="ExternalInput").ap()
           for name, a in arrays.items()}
    out = nc.dram_tensor("y_out", (D, T), F32, kind="ExternalOutput").ap()
    build(nc, cols, aps, out)
    r = run_bass_kernel_spmd(nc, [arrays], core_ids=[0])
    return np.ascontiguousarray(r.results[0]["y_out"].T).reshape(B, S, D)
```
